# Optimizing a Trainium2 kernel written in Bass

```python
import numpy as np
import jax
import jax.numpy as jnp

def _softmax(x, axis=-1):
    return jax.nn.softmax(x, axis=axis)

def _gelu(x):
    return jax.nn.gelu(x, approximate=True)

def _silu(x):
    return jax.nn.silu(x)

def _sigmoid(x):
    return jax.nn.sigmoid(x)

def _layernorm(x, axis=-1, eps=1e-05):
    m = jnp.mean(x, axis=axis, keepdims=True)
    v = jnp.var(x, axis=axis, keepdims=True)
    return (x - m) / jnp.sqrt(v + eps)

def _scatter_add(tgt, idx, src, axis=0):
    return tgt.at[idx].add(src)

def _segment_sum(src, seg, n):
    return jax.ops.segment_sum(src, seg, n)
kernel_name = 'mk_early_fusion_d2_tok_img256_r4_3bea68'

def setup_inputs(seed: int=0):
    np.random.seed(seed)
    _w = jnp.asarray

    def _rec_inputs():
        import jax
        import jax.numpy as jnp
        _rk = jax.random.key(seed)
        x = -4.65018e-05 + 0.999886 * jax.random.normal(jax.random.fold_in(_rk, 1), (8, 3, 128, 128), jnp.float32)
        txt = 0.00586266 + 1.07098 * jax.random.normal(jax.random.fold_in(_rk, 2), (8, 128, 64), jnp.float32)
        return (x, txt)
    x, txt = _rec_inputs()

    def _L0_tok_setup():
        import jax, jax.numpy as jnp
        import numpy as np
        B, C, H, P, D = (64, 3, 128, 16, 64)
        NP = H // P
        key = jax.random.key(seed)
        ks = jax.random.split(key, 7)
        s = lambda fan_in: 1.0 / np.sqrt(fan_in)
        return {'x': jax.random.normal(ks[0], (B, C, H, H), dtype=jnp.float32), 'Wp': jax.random.normal(ks[1], (P * P * C, D), dtype=jnp.float32) * s(P * P * C), 'bp': jax.random.normal(ks[2], (D,), dtype=jnp.float32) * 0.01, 'W1': jax.random.normal(ks[3], (2, D), dtype=jnp.float32) * s(2), 'b1': jax.random.normal(ks[4], (D,), dtype=jnp.float32) * 0.01, 'W2': jax.random.normal(ks[5], (D, D), dtype=jnp.float32) * s(D), 'b2': jax.random.normal(ks[6], (D,), dtype=jnp.float32) * 0.01}
    _L0_tok_all = _L0_tok_setup()
    _L0_tok_in = {k: v for k, v in _L0_tok_all.items() if k in ('Wp', 'bp', 'W1', 'b1', 'W2', 'b2')}
    del _L0_tok_all

    def _L0_attn_setup():
        import jax, jax.numpy as jnp
        import numpy as np
        F = 64
        key = jax.random.key(seed)
        ks = jax.random.split(key, 6)
        s = 1.0 / np.sqrt(F)
        x = jax.random.normal(ks[0], (16, 256, F), dtype=jnp.float32)
        W_alpha = jax.random.uniform(ks[1], (F, F), minval=-s, maxval=s, dtype=jnp.float32)
        W_beta = jax.random.uniform(ks[2], (F, F), minval=-s, maxval=s, dtype=jnp.float32)
        W_unary = jax.random.uniform(ks[3], (F, F), minval=-s, maxval=s, dtype=jnp.float32)
        b_unary = jax.random.uniform(ks[4], (F,), minval=-s, maxval=s, dtype=jnp.float32)
        W_r = jax.random.uniform(ks[5], (F, F), minval=-s, maxval=s, dtype=jnp.float32)
        return {'x': x, 'W_alpha': W_alpha, 'W_beta': W_beta, 'W_unary': W_unary, 'b_unary': b_unary, 'W_r': W_r}
    _L0_attn_all = _L0_attn_setup()
    _L0_attn_in = {k: v for k, v in _L0_attn_all.items() if k in ('W_alpha', 'W_beta', 'W_unary', 'b_unary', 'W_r')}
    del _L0_attn_all

    def _L0_ffn_setup():
        import jax, jax.numpy as jnp
        import numpy as np
        B, T, C = (64, 96, 64)
        NH, NKV = (4, 2)
        HD = C // NH
        NREP = NH // NKV
        NE, TOPK = (8, 2)
        HID = int(8 / 3 * C)
        EPS_RMS = 1e-06

        def _rope_tables(t_len):
            inv_freq = 1.0 / 10000.0 ** (np.arange(0, HD, 2, dtype=np.float32) / HD)
            t = np.arange(t_len, dtype=np.float32)
            freqs = np.outer(t, inv_freq)
            emb = np.concatenate([freqs, freqs], axis=-1)
            return (jnp.asarray(np.cos(emb)), jnp.asarray(np.sin(emb)))

        def _rotate_half(x):
            h = x.shape[-1] // 2
            return jnp.concatenate([-x[..., h:], x[..., :h]], axis=-1)

        def _rmsnorm(v, w):
            return v * jax.lax.rsqrt(jnp.mean(v * v, axis=-1, keepdims=True) + EPS_RMS) * w
        key = jax.random.key(seed)
        ks = jax.random.split(key, 10)
        s = lambda k, shape: jax.random.normal(k, shape, jnp.float32) * 0.02
        return {'x': jax.random.normal(ks[0], (B, T, C), jnp.float32), 'ln1_w': jnp.ones((C,), jnp.float32), 'ln2_w': jnp.ones((C,), jnp.float32), 'wq': s(ks[1], (NH * HD, C)), 'wk': s(ks[2], (NKV * HD, C)), 'wv': s(ks[3], (NKV * HD, C)), 'wo': s(ks[4], (C, C)), 'router_w': s(ks[5], (NE, C)), 'w1': s(ks[6], (NE, HID, C)), 'w2': s(ks[7], (NE, C, HID)), 'w3': s(ks[8], (NE, HID, C))}
    _L0_ffn_all = _L0_ffn_setup()
    _L0_ffn_in = {k: v for k, v in _L0_ffn_all.items() if k in ('ln1_w', 'ln2_w', 'wq', 'wk', 'wv', 'wo', 'router_w', 'w1', 'w2', 'w3')}
    del _L0_ffn_all

    def _L1_attn_setup():
        import jax, jax.numpy as jnp
        import numpy as np
        B, L, D, UNITS = (2, 256, 64, 32)
        key = jax.random.key(seed)
        k1, k2, k3, k4 = jax.random.split(key, 4)
        inputs = jax.random.normal(k1, (B, L, D), dtype=jnp.float32)
        Wt = jax.random.normal(k2, (D, UNITS), dtype=jnp.float32) * (1.0 / np.sqrt(D))
        Wx = jax.random.normal(k3, (UNITS, D), dtype=jnp.float32) * (1.0 / np.sqrt(D))
        bh = jnp.zeros((UNITS,), dtype=jnp.float32)
        Wa = jax.random.normal(k4, (UNITS, 1), dtype=jnp.float32) * (1.0 / np.sqrt(UNITS))
        ba = jnp.zeros((1,), dtype=jnp.float32)
        return {'inputs': inputs, 'Wt': Wt, 'Wx': Wx, 'bh': bh, 'Wa': Wa, 'ba': ba}
    _L1_attn_all = _L1_attn_setup()
    _L1_attn_in = {k: v for k, v in _L1_attn_all.items() if k in ('Wt', 'Wx', 'bh', 'Wa', 'ba')}
    del _L1_attn_all

    def _L1_ffn_setup():
        import math
        import jax, jax.numpy as jnp
        import numpy as np
        CAPACITY_FACTOR = 1.25
        TOP_K = 2
        LN_EPS = 1e-05

        def _layer_norm(x, gamma, beta):
            mu = jnp.mean(x, axis=-1, keepdims=True)
            var = jnp.var(x, axis=-1, keepdims=True)
            return (x - mu) * jax.lax.rsqrt(var + LN_EPS) * gamma + beta
        key = jax.random.key(seed)
        ks = jax.random.split(key, 4)
        B, S, D, F, E = (8, 1024, 64, 128, 8)
        x = jax.random.normal(ks[0], (B, S, D), dtype=jnp.float32)
        Wr = jax.random.normal(ks[1], (D, E), dtype=jnp.float32) / np.sqrt(D)
        br = jnp.zeros((E,), jnp.float32)
        W1 = jax.random.normal(ks[2], (E, D, F), dtype=jnp.float32) / np.sqrt(D)
        b1 = jnp.zeros((E, F), jnp.float32)
        W2 = jax.random.normal(ks[3], (E, F, D), dtype=jnp.float32) / np.sqrt(F)
        b2 = jnp.zeros((E, D), jnp.float32)
        gamma = jnp.ones((D,), jnp.float32)
        beta = jnp.zeros((D,), jnp.float32)
        return {'x': x, 'Wr': Wr, 'br': br, 'W1': W1, 'b1': b1, 'W2': W2, 'b2': b2, 'gamma': gamma, 'beta': beta}
    _L1_ffn_all = _L1_ffn_setup()
    _L1_ffn_in = {k: v for k, v in _L1_ffn_all.items() if k in ('Wr', 'br', 'W1', 'b1', 'W2', 'b2', 'gamma', 'beta')}
    del _L1_ffn_all
    return {'x': x, 'txt': txt, 'L0_tok_Wp': _L0_tok_in['Wp'], 'L0_tok_bp': _L0_tok_in['bp'], 'L0_tok_W1': _L0_tok_in['W1'], 'L0_tok_b1': _L0_tok_in['b1'], 'L0_tok_W2': _L0_tok_in['W2'], 'L0_tok_b2': _L0_tok_in['b2'], 'L0_attn_W_alpha': _L0_attn_in['W_alpha'], 'L0_attn_W_beta': _L0_attn_in['W_beta'], 'L0_attn_W_unary': _L0_attn_in['W_unary'], 'L0_attn_b_unary': _L0_attn_in['b_unary'], 'L0_attn_W_r': _L0_attn_in['W_r'], 'L0_ffn_ln1_w': _L0_ffn_in['ln1_w'], 'L0_ffn_ln2_w': _L0_ffn_in['ln2_w'], 'L0_ffn_wq': _L0_ffn_in['wq'], 'L0_ffn_wk': _L0_ffn_in['wk'], 'L0_ffn_wv': _L0_ffn_in['wv'], 'L0_ffn_wo': _L0_ffn_in['wo'], 'L0_ffn_router_w': _L0_ffn_in['router_w'], 'L0_ffn_w1': _L0_ffn_in['w1'], 'L0_ffn_w2': _L0_ffn_in['w2'], 'L0_ffn_w3': _L0_ffn_in['w3'], 'L1_attn_Wt': _L1_attn_in['Wt'], 'L1_attn_Wx': _L1_attn_in['Wx'], 'L1_attn_bh': _L1_attn_in['bh'], 'L1_attn_Wa': _L1_attn_in['Wa'], 'L1_attn_ba': _L1_attn_in['ba'], 'L1_ffn_Wr': _L1_ffn_in['Wr'], 'L1_ffn_br': _L1_ffn_in['br'], 'L1_ffn_W1': _L1_ffn_in['W1'], 'L1_ffn_b1': _L1_ffn_in['b1'], 'L1_ffn_W2': _L1_ffn_in['W2'], 'L1_ffn_b2': _L1_ffn_in['b2'], 'L1_ffn_gamma': _L1_ffn_in['gamma'], 'L1_ffn_beta': _L1_ffn_in['beta']}

def reference(x, txt, L0_tok_Wp, L0_tok_bp, L0_tok_W1, L0_tok_b1, L0_tok_W2, L0_tok_b2, L0_attn_W_alpha, L0_attn_W_beta, L0_attn_W_unary, L0_attn_b_unary, L0_attn_W_r, L0_ffn_ln1_w, L0_ffn_ln2_w, L0_ffn_wq, L0_ffn_wk, L0_ffn_wv, L0_ffn_wo, L0_ffn_router_w, L0_ffn_w1, L0_ffn_w2, L0_ffn_w3, L1_attn_Wt, L1_attn_Wx, L1_attn_bh, L1_attn_Wa, L1_attn_ba, L1_ffn_Wr, L1_ffn_br, L1_ffn_W1, L1_ffn_b1, L1_ffn_W2, L1_ffn_b2, L1_ffn_gamma, L1_ffn_beta):
    import jax
    import jax.numpy as jnp

    def _L0_tok_ref(x, Wp, bp, W1, b1, W2, b2):
        import jax, jax.numpy as jnp
        import numpy as np
        B, C, H, P, D = (64, 3, 128, 16, 64)
        NP = H // P
        b = x.shape[0]
        patches = x.reshape(b, C, NP, P, NP, P)
        patches = patches.transpose(0, 2, 4, 1, 3, 5).reshape(b, NP * NP, C * P * P)
        embedded = jnp.einsum('bnk,kd->bnd', patches, Wp) + bp
        gx, gy = jnp.meshgrid(jnp.arange(NP, dtype=jnp.float32), jnp.arange(NP, dtype=jnp.float32), indexing='ij')
        xy = jnp.stack([gx, gy], axis=-1).reshape(1, -1, 2) / (NP - 1)
        pos = jax.nn.relu(xy @ W1 + b1) @ W2 + b2
        return embedded + pos

    def _L0_attn_ref(x, W_alpha, W_beta, W_unary, b_unary, W_r):
        import jax, jax.numpy as jnp
        import numpy as np
        F = 64
        B, N, _ = x.shape
        alpha = jnp.einsum('bnf,gf->bng', x, W_alpha)
        beta = jnp.einsum('bnf,gf->bng', x, W_beta)
        unary = jnp.einsum('bnf,gf->bng', x, W_unary) + b_unary
        scores = jnp.einsum('bif,bjf->bij', alpha, beta)
        scores = scores * (1.0 - jnp.eye(N, dtype=x.dtype))
        att = jnp.einsum('bij,bjf->bif', scores, unary) / N
        out = jnp.einsum('bif,gf->big', att, W_r) + x
        return out

    def _L0_ffn_ref(x, ln1_w, ln2_w, wq, wk, wv, wo, router_w, w1, w2, w3):
        import jax, jax.numpy as jnp
        import numpy as np
        B, T, C = (64, 96, 64)
        NH, NKV = (4, 2)
        HD = C // NH
        NREP = NH // NKV
        NE, TOPK = (8, 2)
        HID = int(8 / 3 * C)
        EPS_RMS = 1e-06

        def _rope_tables(t_len):
            inv_freq = 1.0 / 10000.0 ** (np.arange(0, HD, 2, dtype=np.float32) / HD)
            t = np.arange(t_len, dtype=np.float32)
            freqs = np.outer(t, inv_freq)
            emb = np.concatenate([freqs, freqs], axis=-1)
            return (jnp.asarray(np.cos(emb)), jnp.asarray(np.sin(emb)))

        def _rotate_half(x):
            h = x.shape[-1] // 2
            return jnp.concatenate([-x[..., h:], x[..., :h]], axis=-1)

        def _rmsnorm(v, w):
            return v * jax.lax.rsqrt(jnp.mean(v * v, axis=-1, keepdims=True) + EPS_RMS) * w
        Bx, Tx, Cx = x.shape
        h = _rmsnorm(x, ln1_w)
        q = (h @ wq.T).reshape(Bx, Tx, NH, HD).transpose(0, 2, 1, 3)
        k = (h @ wk.T).reshape(Bx, Tx, NKV, HD).transpose(0, 2, 1, 3)
        v = (h @ wv.T).reshape(Bx, Tx, NKV, HD).transpose(0, 2, 1, 3)
        cos, sin = _rope_tables(Tx)
        cos, sin = (cos[None, None], sin[None, None])
        q = q * cos + _rotate_half(q) * sin
        k = k * cos + _rotate_half(k) * sin
        k = jnp.repeat(k, NREP, axis=1)
        v = jnp.repeat(v, NREP, axis=1)
        scores = jnp.einsum('bhtd,bhsd->bhts', q, k) / jnp.sqrt(jnp.float32(HD))
        causal = jnp.tril(jnp.ones((Tx, Tx), dtype=bool))
        scores = jnp.where(causal[None, None], scores, jnp.float32(-1e+30))
        att = jax.nn.softmax(scores, axis=-1)
        y = jnp.einsum('bhts,bhsd->bhtd', att, v).transpose(0, 2, 1, 3).reshape(Bx, Tx, Cx)
        x = x + y @ wo.T
        flat = _rmsnorm(x, ln2_w).reshape(-1, Cx)
        probs = jax.nn.softmax(flat @ router_w.T, axis=-1)
        tp, ti = jax.lax.top_k(probs, TOPK)
        tp = tp / (jnp.sum(tp, axis=-1, keepdims=True) + 1e-09)
        weights = jnp.sum(tp[..., None] * jax.nn.one_hot(ti, NE, dtype=flat.dtype), axis=1)
        out = jnp.zeros_like(flat)
        for e in range(NE):
            hh = jax.nn.silu(flat @ w1[e].T) * (flat @ w3[e].T)
            out = out + weights[:, e:e + 1] * (hh @ w2[e].T)
        return x + out.reshape(Bx, Tx, Cx)

    def _L1_attn_ref(inputs, Wt, Wx, bh, Wa, ba):
        import jax, jax.numpy as jnp
        import numpy as np
        B, L, D, UNITS = (2, 256, 64, 32)
        q = jnp.einsum('bld,du->blu', inputs, Wt)
        k = jnp.einsum('bld,ud->blu', inputs, Wx)
        beta = jnp.tanh(q[:, :, None, :] + k[:, None, :, :] + bh)
        alpha = jnp.einsum('bqku,u->bqk', beta, Wa[:, 0]) + ba[0]
        a = jax.nn.softmax(alpha, axis=-1)
        c_r = jnp.einsum('bqk,bkd->bqd', a, inputs)
        return c_r

    def _L1_ffn_ref(x, Wr, br, W1, b1, W2, b2, gamma, beta):
        import math
        import jax, jax.numpy as jnp
        import numpy as np
        CAPACITY_FACTOR = 1.25
        TOP_K = 2
        LN_EPS = 1e-05

        def _layer_norm(x, gamma, beta):
            mu = jnp.mean(x, axis=-1, keepdims=True)
            var = jnp.var(x, axis=-1, keepdims=True)
            return (x - mu) * jax.lax.rsqrt(var + LN_EPS) * gamma + beta
        B, S, D = x.shape
        E = Wr.shape[1]
        N = B * S
        K = TOP_K
        logits = jnp.mean(x, axis=1) @ Wr + br
        routing_weights = jax.nn.softmax(logits, axis=-1)
        capacity = float(math.ceil(N * CAPACITY_FACTOR / E))
        expected_loads = routing_weights.sum(axis=0) * (N / B)
        scale = jnp.where(expected_loads > capacity, capacity / expected_loads, 1.0)
        routing_weights = jax.nn.softmax(routing_weights * scale, axis=-1)
        rw_tok = jnp.broadcast_to(routing_weights[:, None, :], (B, S, E)).reshape(N, E)
        top_w, top_i = jax.lax.top_k(rw_tok, K)
        top_w = jax.nn.softmax(top_w, axis=-1)
        xf = x.reshape(N, D)
        h = jax.nn.gelu(jnp.einsum('nd,edf->enf', xf, W1) + b1[:, None, :], approximate=False)
        y = jnp.einsum('enf,efd->end', h, W2) + b2[:, None, :]
        w_dense = jnp.zeros((N, E), x.dtype).at[jnp.arange(N)[:, None], top_i].add(top_w)
        out = jnp.einsum('ne,end->nd', w_dense, y).reshape(B, S, D)
        out = _layer_norm(out + x, gamma, beta)
        return out
    h = _L0_tok_ref(x, L0_tok_Wp, L0_tok_bp, L0_tok_W1, L0_tok_b1, L0_tok_W2, L0_tok_b2)
    h = jnp.concatenate([h, txt], axis=1)
    h = h + _L0_attn_ref(_layernorm(h, axis=-1), L0_attn_W_alpha, L0_attn_W_beta, L0_attn_W_unary, L0_attn_b_unary, L0_attn_W_r)
    h = h + _L0_ffn_ref(_layernorm(h, axis=-1), L0_ffn_ln1_w, L0_ffn_ln2_w, L0_ffn_wq, L0_ffn_wk, L0_ffn_wv, L0_ffn_wo, L0_ffn_router_w, L0_ffn_w1, L0_ffn_w2, L0_ffn_w3)
    h = h + _L1_attn_ref(_layernorm(h, axis=-1), L1_attn_Wt, L1_attn_Wx, L1_attn_bh, L1_attn_Wa, L1_attn_ba)
    h = h + _L1_ffn_ref(_layernorm(h, axis=-1), L1_ffn_Wr, L1_ffn_br, L1_ffn_W1, L1_ffn_b1, L1_ffn_W2, L1_ffn_b2, L1_ffn_gamma, L1_ffn_beta)
    return h

_drawn_inputs = setup_inputs


def setup_inputs(seed=0):
    import zlib

    import numpy as np

    out = dict(_drawn_inputs(seed))
    spreads = {'L0_ffn_ln1_w': (1.0, 0.6),
     'L0_ffn_ln2_w': (1.0, 0.6),
     'L1_attn_bh': (0.0, 2.0),
     'L1_ffn_br': (0.0, 0.1),
     'L1_ffn_b1': (0.0, 0.8),
     'L1_ffn_b2': (0.0, 0.574),
     'L1_ffn_gamma': (1.0, 0.577),
     'L1_ffn_beta': (0.0, 0.337)}
    factors = {'L0_tok_bp': 8.0,
     'L0_tok_b1': 8.0,
     'L0_tok_b2': 8.0,
     'L0_attn_b_unary': 7.156,
     'L0_ffn_wq': 8.0,
     'L0_ffn_wk': 8.0,
     'L0_ffn_wv': 8.0,
     'L0_ffn_router_w': 8.0,
     'L0_ffn_w1': 8.0,
     'L0_ffn_w2': 8.0,
     'L0_ffn_w3': 8.0,
     'L1_attn_Wt': 43.512,
     'L1_attn_Wx': 7.631,
     'L1_attn_Wa': 7.922}
    for name, (base, spread) in spreads.items():
        noise = np.random.default_rng([zlib.crc32(name.encode()), seed]).standard_normal(out[name].shape)
        drawn = base * np.exp(spread * noise) if base else spread * noise
        out[name] = jnp.asarray(drawn.astype(out[name].dtype))
    for name, factor in factors.items():
        out[name] = (out[name] * factor).astype(out[name].dtype)
    return out
```

```python
from contextlib import ExitStack

import numpy as np

import concourse.bass as bass
from concourse import mybir

ALU = mybir.AluOpType
ACT = mybir.ActivationFunctionType
F32 = mybir.dt.float32
BF16 = mybir.dt.bfloat16
X = mybir.AxisListType.X

B = 8
CH, HW, PS = 3, 128, 16
NPS = HW // PS
NPATCH = NPS * NPS
TXT = 128
N = NPATCH + TXT
D = 64
P = N // 2
NT = 2 * B
TOK = B * N
KC = CH * PS * PS // 128
PAIRS = B // 2
CW = 2 * N
NH, NKV, HD = 4, 2, 16
NE, HID = 8, 170
HALL = NE * HID
MT = -(-HALL // 128)
MPAD = MT * 128
U = 32
IB = 128 // U
NCH = P // IB
RND = 8
FE = 128
CAP = float(-(-TOK * 5 // (4 * 8)))
NEG = -1e30
FILLS = 13

W64 = {}
_at = 0
for _name, _n in (("Wa", D), ("Wb", D), ("Wu", D + 1), ("WrT", D), ("ln1", 1), ("ln2", 1),
                  ("q", 128), ("qs", 128), ("k", 128), ("ks", 128), ("v", NKV * HD),
                  ("rw", NE), ("w1", HALL), ("w3", HALL),
                  ("wt", U), ("wx", 3 * U), ("e1", NE * FE), ("wr", NE)):
    W64[_name] = (_at, _n)
    _at += _n
NW64 = _at
C128 = {}
_at = 0
for _name, _n in (("ident", 128), ("cos", N), ("sin", N), ("mask", 3 * P), ("rank", NE), ("wo", D),
                  ("w2", MT * D), ("was", RND * U), ("ba", 1), ("bh", 1), ("gamma", D), ("beta", D),
                  ("e2", NE * D)):
    C128[_name] = (_at, _n)
    _at += _n
NC128 = _at


def early_fusion(nc, patches, wpatch, txt, w64_d, e1row, tok66, tok3, c128_d, b2_d, idb_d, sel_d, rep_d, hot_d, out):
    qrows = nc.dram_tensor("qrows", (2, B, 3, P, U), BF16, kind="Internal").ap()
    with ExitStack() as ctx:
        def sb(name, shape, dt=F32):
            return ctx.enter_context(nc.sbuf_tensor(name, shape, dt))

        S = {n: ctx.enter_context(nc.semaphore(n)) for n in (
            "ld_x", "ld_txt", "ld_w64", "ld_row", "ld_c", "ld_tok", "ld_b", "ld_b2", "ld_hot", "st_q", "ld_q", "st_out",
            "filled", "gc_ready", "gt_ready", "lnw_ready", "rep_ready",
            "dve", "var", "veps", "rstd", "fo",
            "hid_mm", "hid", "emb_mm", "emb", "embT", "h0",
            "gmm",
            "z1", "zT_mm", "zT", "gv_mm", "v_sb", "zv_mm", "zv", "p_mm", "p_sb", "lo_mm", "hz1", "h1",
            "xn", "z2", "xT_mm", "xT", "v_mm", "vall", "qk_mm", "rope_cs", "rope", "vb", "s_mm", "s_sb", "nmax", "p_exp",
            "pt_mm", "pt_sb", "y_mm", "y_sb", "pr_mm", "x2", "h12",
            "xr", "rT_mm", "rT", "lg_mm", "lg_max", "lg_exp", "wp3", "wT_mm", "wT", "up_mm", "silu", "bw", "hh",
            "dn_mm", "ym", "ymT_mm", "h2",
            "z3", "aT_mm", "aT", "q_mm", "k_mm", "qp", "kp", "bld_mm", "tanh", "al_mm", "al_sb", "amax", "aexp", "pn",
            "pt2_mm", "pt2", "c_mm", "h3",
            "z4", "fT_mm", "fT", "msum", "rl_mm", "rl_max", "rl_exp", "ld_mm", "r2max", "r2exp", "e2exp",
            "wd", "wdT_mm", "wdT", "b2w_mm", "dg", "wB_mm", "bB_mm", "wbc", "w2s", "e1_mm", "gelu", "e2_mm", "oT",
            "o_mm", "y_out")}

        w64 = sb("w64", [128, NW64])
        c128 = sb("c128", [128, NC128])
        xP = sb("xP", [128, KC, B * NPATCH])
        wpT = sb("wpT", [128, KC, D])
        t66 = sb("t66", [D + 2, D])
        t3 = sb("t3", [3, D + NPATCH])
        hid = sb("hid", [D + 2, NPATCH])
        b2s = sb("b2s", [NE, D])
        idb = sb("idb", [128, 128], BF16)
        sel = sb("sel", [3 * NE, MPAD], BF16)
        rep = sb("rep", [3 * U, 128], BF16)
        GT = sb("GT", [D, D])
        GC = sb("GC", [128, 2 * D])

        def w(name, lo=0, hi=None):
            at, n = W64[name]
            return w64[:, at + lo:at + (n if hi is None else hi)]

        def c(name):
            at, n = C128[name]
            return c128[:, at:at + n]

        ident = c("ident")
        H = sb("H", [P, NT, D])
        Z = sb("Z", [P, NT, D])
        Y = sb("Y", [P, NT, D])
        XN = sb("XN", [P, NT, D])
        HZ = sb("HZ", [P, NT, D])
        V = XN
        stat = sb("stat", [P, NT, 6])
        mv = sb("mv", [P, NT, 2])
        rstd = sb("rstd", [P, NT])
        mhalf = sb("mhalf", [P, NT])
        r2 = sb("r2", [P, NT])
        dg = sb("dg", [P, NT])
        TA = sb("TA", [128, TOK])
        TB = sb("TB", [128, TOK])
        embS = sb("embS", [D, B * NPATCH])
        ZV = sb("ZV", [D, B * D])
        PB = sb("PB", [128, B, D])
        Vall = sb("Vall", [P, NT, NKV, 2 * HD])
        Vb = sb("Vb", [P, 4, NKV, 2 * HD])
        rope = sb("rope", [128, 4, CW])
        QT = sb("QT", [128, CW])
        KT = sb("KT", [128, CW])
        SP_ = sb("SP_", [128, 3, 2, NH, 3 * P])
        Ssb = SP_[0:P, 0]
        nmx = sb("nmx", [P, 2, 2, NH])
        Pex = SP_[0:P, 1]
        PT = SP_[0:P, 2]
        yT = sb("yT", [128, CW])
        ones = sb("ones", [128, 128])
        lg = sb("lg", [P, NT, NE])
        pr = sb("pr", [P, NT, NE])
        oh = sb("oh", [P, 3, NT, NE])
        sm = sb("sm", [P, 4, NT])
        wp3 = sb("wp3", [P, NT, 3, NE], BF16)
        wT = sb("wT", [3 * NE, TOK], BF16)
        up_sb = sb("up_sb", [128, 3, 2, CW])
        silu, bw, hh = up_sb[:, 0], up_sb[:, 1], up_sb[:, 2]
        ym = sb("ym", [128, N])
        qp = sb("qp", [P, 2, B, 3, U], BF16)
        qr = sb("qr", [P, NT, U])
        kb = xP[0:3 * U, 0:3, :].rearrange("p k n -> p (k n)")
        khi = xP[0:3 * U, 3:5, :].rearrange("p k n -> p (k n)").bitcast(BF16)[:, 0:TOK]
        RH = sb("RH", [3 * U + 6, B, 2, N], BF16)
        LQ = sb("LQ", [3 * U + 6, B, NCH, 128], BF16)
        TH = SP_[:, :, :, :, :].rearrange("p a b c d -> p (a b c d)")[:, 0:6 * CW].rearrange("p (s j n) -> p s j n", s=2, j=3)
        AL = rope[:, 0, :].rearrange("p (a n) -> p a n", a=2)
        ast = sb("ast", [128, 2, 4])
        PT2 = rope[0:P, 1, :].rearrange("p (a n) -> p a n", a=2)
        ms = sb("ms", [128, B])
        rt = sb("rt", [B, 16, NE])
        rs = sb("rs", [B, 24])
        wdT = sb("wdT", [NE, B])
        b2w = sb("b2w", [B, D])
        dgw = Vall[0:B].rearrange("p t k e -> p (t k e)")[:, 0:B * (NE + D)]
        wBC = sb("wBC", [128, B, NE])
        bBC = HZ[:, 8:16, :]
        W2S = up_sb[:, :, :, :].rearrange("p a b n -> p (a b n)")[:, 0:2 * NE * D].rearrange(
            "p (i e d) -> p i e d", i=2, e=NE)
        G1 = SP_[:, :, :, :, :].rearrange("p a b c d -> p (a b c d)")[:, 0:NE * CW].rearrange("p (e n) -> p e n", e=NE)
        oT = rope[:, 2, 0:N]

        ps = ctx.enter_context(nc.psum_tensor("ps", [128, 8, 512], F32))

        def bank(i, rows, *dims):
            n = 1
            for x in dims:
                n *= x
            v = ps[0:rows, i, 0:n]
            if len(dims) == 2:
                v = v.rearrange("p (a b) -> p a b", a=dims[0])
            if len(dims) == 3:
                v = v.rearrange("p (a b c) -> p a b c", a=dims[0], b=dims[1])
            return v

        def mm(out_, lhsT, rhs, start=True, stop=True, **k):
            return nc.tensor.matmul(out_, lhsT, rhs, start=start, stop=stop, **k)

        def bc(ap, n):
            return ap.unsqueeze(2).to_broadcast([ap.shape[0], ap.shape[1], n])

        block = ctx.enter_context(nc.Block())

        @block.sync
        def _(sp):
            for k in range(KC):
                sp.dma_start(xP[:, k, :], patches[:, k, :]).then_inc(S["ld_x"], 16)
            sp.dma_start(c128[:, :], c128_d).then_inc(S["ld_c"], 16)
            sp.wait_ge(S["qp"], 1)
            for half in range(2):
                sp.dma_start(qrows[half].rearrange("b a p u -> p (b a) u"),
                             qp[:, half, :, :, :].rearrange("p b a u -> p (b a) u")).then_inc(S["st_q"], 16)
            sp.wait_ge(S["st_q"], 32)
            for b in range(B):
                for half in range(2):
                    row = 3 * U + 3 * half
                    sp.dma_start(LQ[row:row + 3, b, :, :].rearrange("o c q -> o (c q)"),
                                 qrows[half, b].rearrange("a p u -> a (p u)")).then_inc(S["ld_q"], 16)
            sp.wait_ge(S["y_out"], 1)
            for i in range(2):
                sp.dma_start(out[:, i * P:(i + 1) * P, :].rearrange("b p d -> p b d"),
                             Y[:, i:NT:2, :]).then_inc(S["st_out"], 16)
            sp.wait_ge(S["st_out"], 32)

        @block.gpsimd
        def _(pool):
            for name in ("rope",):
                pool.sem_inc(S[name], 1)
            fills = [(w64[D:128, :], 0.0), (GC[D:128, :], 0.0), (PB[D:128, :, :], 0.0), (TB[D:128, :], 0.0),
                     (ms[D:128, :], 0.0), (TA[D:128, :], 0.0),
                     (TA[D:D + 1, :], 1.0), (TB[D:D + 1, :], 1.0), (ms[D:D + 1, :], 1.0), (hid[D:D + 2, :], 1.0),
                     (ones[:, :], 1.0), (mhalf[:, :], -0.5), (Vall[:, :, :, :], 0.0)]
            for n, (ap, value) in enumerate(fills):
                if n:
                    pool.wait_ge(S["filled"], n)
                nc.gpsimd.memset(ap, value).then_inc(S["filled"], 1)
            pool.wait_ge(S["filled"], FILLS)
            pool.dma_start(w64[D:D + 1, W64["e1"][0]:NW64], e1row).then_inc(S["ld_row"], 16)
            pool.dma_start(idb[:, :], idb_d).then_inc(S["ld_b"], 16)
            pool.dma_start(rep[:, :], rep_d).then_inc(S["ld_b"], 16)
            pool.dma_start(sel[:, :], sel_d).then_inc(S["ld_b"], 16)
            pool.dma_start(RH[3 * U:3 * U + 6, :, :, :], hot_d).then_inc(S["ld_hot"], 16)
            pool.wait_ge(S["ld_b"], 48)
            nc.gpsimd.tensor_copy(
                LQ[0:3 * U, :, :, :].rearrange("p b c q -> p (b c) q"),
                rep[:, :].unsqueeze(1).to_broadcast([3 * U, B * NCH, 128])).then_inc(S["rep_ready"], 1)
            def rsqrt(n, out_, in_, eps):
                pool.wait_ge(S["var"], n)
                nc.gpsimd.tensor_scalar(out_, in_, eps, None, ALU.add).then_inc(S["veps"], 1)
                pool.wait_ge(S["veps"], n)
                half = mhalf[:, 0:out_.shape[1]]
                nc.gpsimd.tensor_tensor(out_, out_, half, ALU.pow).then_inc(S["rstd"], 1)

            rsqrt(1, rstd[:, :], mv[:, :, 1], 1e-5)
            pool.wait_ge(S["z1"], 1)
            nc.gpsimd.tensor_tensor(HZ[:, :, :], H[:, :, :], Z[:, :, :], ALU.add).then_inc(S["hz1"], 1)
            rsqrt(2, rstd[:, :], mv[:, :, 1], 1e-5)
            rsqrt(3, r2[:, :], r2[:, :], 1e-6)
            with pool.Fori(0, PAIRS) as g:
                pool.wait_ge(S["rope_cs"], g + 1)
                nc.gpsimd.tensor_tensor(QT[:, :], rope[:, 0, :], rope[:, 1, :], ALU.add)
                nc.gpsimd.tensor_tensor(KT[:, :], rope[:, 2, :], rope[:, 3, :], ALU.add).then_inc(S["rope"], 1)
            rsqrt(4, r2[:, :], r2[:, :], 1e-6)
            rsqrt(5, rstd[:, :], mv[:, :, 1], 1e-5)
            rsqrt(6, rstd[:, :], mv[:, :, 1], 1e-5)
            rsqrt(7, rstd[:, :], mv[:, :, 1], 1e-5)

        @block.scalar
        def _(act):
            for name in ("oT",):
                act.sem_inc(S[name], 1)
            act.dma_start(wpT[:, :, :], wpatch).then_inc(S["ld_tok"], 16)
            act.dma_start(t66[:, :], tok66).then_inc(S["ld_tok"], 16)
            act.dma_start(t3[:, :], tok3).then_inc(S["ld_tok"], 16)
            act.dma_start(w64[0:D, :], w64_d).then_inc(S["ld_w64"], 16)
            act.dma_start(H[NPATCH:P, 0:NT:2, :], txt[:, 0:P - NPATCH, :].rearrange("b p d -> p b d")
                          ).then_inc(S["ld_txt"], 16)
            act.dma_start(H[:, 1:NT:2, :], txt[:, P - NPATCH:TXT, :].rearrange("b p d -> p b d")
                          ).then_inc(S["ld_txt"], 16)
            act.dma_start(b2s[:, :], b2_d).then_inc(S["ld_b2"], 16)
            act.wait_ge(S["hid_mm"], 1)
            nc.scalar.activation(hid[0:D, :], bank(0, D, NPATCH), ACT.Relu).then_inc(S["hid"], 1)
            act.wait_ge(S["gmm"], 1)
            act.wait_ge(S["filled"], FILLS)
            nc.scalar.copy(GC[0:D, 0:D], bank(1, D, D))
            nc.scalar.copy(GC[0:D + 1, D:2 * D], bank(2, D + 1, D))
            nc.scalar.copy(GT[:, :], bank(3, D, D)).then_inc(S["gc_ready"], 1)
            act.wait_ge(S["emb_mm"], 1)
            nc.scalar.copy(embS[:, :], bank(4, D, B * NPATCH)).then_inc(S["emb"], 1)

            def feature_major(dst, done, ready):
                for g in range(PAIRS):
                    act.wait_ge(done, g + 1)
                    nc.scalar.copy(dst[0:D, g * CW:(g + 1) * CW], bank(g, D, CW)).then_inc(ready, 1)

            feature_major(TA, S["zT_mm"], S["zT"])
            for q in range(PAIRS):
                act.wait_ge(S["gv_mm"], q + 1)
                nc.scalar.copy(V[:, 4 * q:4 * q + 4, :], bank(4 + q, P, 4, 2 * D)[:, :, D:2 * D]).then_inc(S["v_sb"], 1)
            act.wait_ge(S["zv_mm"], 1)
            nc.scalar.copy(ZV[:, :], bank(0, D, B * D)).then_inc(S["zv"], 1)
            act.wait_ge(S["p_mm"], 1)
            nc.scalar.copy(PB[0:D, :, :], bank(1, D, B, D)).then_inc(S["p_sb"], 1)
            feature_major(TB, S["xT_mm"], S["xT"])
            act.wait_ge(S["v_mm"], 1)
            nc.scalar.copy(Vall[:, :, :, 0:HD].rearrange("p t k e -> p (t k) e"), bank(4, P, NT * NKV, HD)).then_inc(S["vall"], 1)
            act.wait_ge(S["vall"], 1)
            with act.Fori(0, PAIRS) as g:
                act.wait_ge(S["y_mm"], 1 + g * 2)
                nc.scalar.copy(Vb[:, :, :, :].rearrange("p t k e -> p (t k e)"),
                               Vall[:, bass.ds(g * 4, 4), :, :].rearrange("p t k e -> p (t k e)")).then_inc(S["vb"], 1)
                for i in range(2):
                    act.wait_ge(S["nmax"], g * 2 + (i + 1))
                    for h in range(NH):
                        nc.scalar.activation(Pex[:, i, h, 0:P], Ssb[:, i, h, 0:P], ACT.Exp,
                                             bias=nmx[:, i, 0, h:h + 1], scale=HD ** -0.5)
                        last = nc.scalar.activation(Pex[:, i, h, P:3 * P], Ssb[:, i, h, P:3 * P], ACT.Exp,
                                                    bias=nmx[:, i, 1, h:h + 1], scale=HD ** -0.5)
                    last.then_inc(S["p_exp"], 1)
                for i in range(2):
                    act.wait_ge(S["pt_mm"], g * 2 + (i + 1))
                    nc.scalar.copy(PT[:, i, :, :], ps[0:P, 4 * i:4 * i + 4, 0:3 * P]).then_inc(S["pt_sb"], 1)
            feature_major(TA, S["rT_mm"], S["rT"])
            act.wait_ge(S["lg_max"], 1)
            nc.scalar.activation(pr[:, :, :], lg[:, :, :], ACT.Exp).then_inc(S["lg_exp"], 1)
            act.wait_ge(S["wT_mm"], 1)
            nc.scalar.copy(wT[:, :].rearrange("p (a b) -> p a b", a=2),
                           ps[0:3 * NE, 5:7, :].bitcast(BF16)[:, :, 0:TOK // 2]).then_inc(S["wT"], 1)
            with act.Fori(0, PAIRS) as g:
                for m in range(MT):
                    rows = min(128, HALL - 128 * m)
                    act.wait_ge(S["up_mm"], g * MT + (m + 1))
                    act.wait_ge(S["bw"], 1 + g * MT + max(m - 1, 0))
                    nc.scalar.activation(silu[0:rows, m % 2, :], ps[0:rows, 3 * (m % 2), 0:CW],
                                         ACT.Silu).then_inc(S["silu"], 1)
                act.wait_ge(S["dn_mm"], 1 + g * MT + MT)
                nc.scalar.copy(ym[:, :], bank(6, 128, N)).then_inc(S["ym"], 1)
            feature_major(TB, S["aT_mm"], S["aT"])
            with act.Fori(0, B) as b:
                for r in range(RND):
                    act.wait_ge(S["bld_mm"], b * RND + (r + 1))
                    if r >= 2:
                        act.wait_ge(S["al_mm"], 1 + b * RND + (r - 1))
                    else:
                        act.wait_ge(S["al_mm"], 1 + b * RND)
                    nc.scalar.activation(TH[:, r % 2, :, :], ps[:, 3 * (r % 2):3 * (r % 2) + 3, 0:CW],
                                         ACT.Tanh).then_inc(S["tanh"], 1)
                act.wait_ge(S["amax"], b + 1)
                nc.scalar.activation(AL[:, 0, :], AL[:, 0, :], ACT.Exp, bias=ast[:, 0, 1:2], accum_out=ast[:, 0, 2:3])
                nc.scalar.activation(AL[0:64, 1, :], AL[0:64, 1, :], ACT.Exp, bias=ast[0:64, 1, 1:2],
                                     accum_out=ast[0:64, 1, 2:3]).then_inc(S["aexp"], 1)
                act.wait_ge(S["pt2_mm"], 1 + b + 1)
                nc.scalar.copy(PT2[:, :, :], bank(0, P, 2, N)).then_inc(S["pt2"], 1)
            feature_major(TA, S["fT_mm"], S["fT"])
            act.wait_ge(S["rl_max"], 1)
            nc.scalar.activation(rt[:, 1, :], rt[:, 0, :], ACT.Exp, accum_out=rs[:, 1:2]).then_inc(S["rl_exp"], 1)
            act.wait_ge(S["r2max"], 1)
            nc.scalar.activation(rt[:, 4, :], rt[:, 3, :], ACT.Exp, accum_out=rs[:, 3:4]).then_inc(S["r2exp"], 1)
            act.wait_ge(S["e2exp"], 1)
            nc.scalar.activation(rs[:, 11:12], rs[:, 10:11], ACT.Exp).then_inc(S["e2exp"], 1)
            act.wait_ge(S["wdT_mm"], 1)
            nc.scalar.copy(wdT[:, :], bank(5, NE, B)).then_inc(S["wdT"], 1)
            act.wait_ge(S["b2w_mm"], 1)
            nc.scalar.copy(b2w[:, :], bank(6, B, D)).then_inc(S["wdT"], 1)
            act.wait_ge(S["bB_mm"], 1)
            nc.scalar.copy(bBC[:, :, :], bank(7, P, B, D)).then_inc(S["wbc"], 1)
            with act.Fori(0, PAIRS) as g:
                act.wait_ge(S["e2_mm"], 1 + g)
                for e in range(NE):
                    act.wait_ge(S["e1_mm"], g * NE + (e + 1))
                    nc.scalar.activation(G1[:, e, :], ps[:, e % 4, 0:CW], ACT.Gelu).then_inc(S["gelu"], 1)
                act.wait_ge(S["e2_mm"], 1 + g + 1)
                nc.scalar.copy(oT[:, :], bank(4, 128, N)).then_inc(S["oT"], 1)

        @block.vector
        def _(dve):
            for name in ("bw", "x2", "hh", "h2", "h3", "fo",):
                dve.sem_inc(S[name], 1)
            count = [0]

            def link(ins, base=0):
                count[0] += 1
                ins.then_inc(S["dve"], 1)
                dve.wait_ge(S["dve"], base + count[0])

            V_ = nc.vector

            def norm(src, dst, tiles, n, base=0):
                for t in range(tiles):
                    last = V_.bn_stats(stat[:, t, :], src[:, t, :])
                link(last, base)
                for t in range(tiles):
                    last = V_.bn_aggr(mv[:, t, :], stat[:, t, :])
                last.then_inc(S["var"], 1)
                dve.wait_ge(S["var"], n)
                link(V_.tensor_tensor(dst, src, bc(mv[:, 0:tiles, 0], D), ALU.subtract), base)
                dve.wait_ge(S["rstd"], n)

            dve.wait_ge(S["ld_w64"], 16)
            q0, v1 = W64["q"][0], W64["v"][0] + W64["v"][1]
            r0, w31 = W64["rw"][0], W64["w3"][0] + W64["w3"][1]
            V_.tensor_scalar(w64[0:D, q0:v1], w64[0:D, q0:v1], w("ln1")[0:D], None, ALU.mult)
            V_.tensor_scalar(w64[0:D, r0:w31], w64[0:D, r0:w31], w("ln2")[0:D], None, ALU.mult).then_inc(S["lnw_ready"], 1)
            dve.wait_ge(S["embT"], 1)
            V_.tensor_copy(H[0:NPATCH, 0:NT:2, :], bank(5, NPATCH, B, D)).then_inc(S["h0"], 1)
            dve.wait_ge(S["h0"], 1)
            dve.wait_ge(S["ld_txt"], 32)
            norm(H[:, :, :], Z[:, :, :], NT, 1)
            V_.tensor_tensor(Z[:, :, :], Z[:, :, :], bc(rstd[:, :], D), ALU.mult).then_inc(S["z1"], 1)
            dve.wait_ge(S["z1"], 1)
            for q in range(PAIRS):
                dve.wait_ge(S["v_sb"], q + 1)
                last = V_.tensor_tensor(Y[:, 4 * q:4 * q + 4, :], bank(4 + q, P, 4, 2 * D)[:, :, 0:D],
                                        Z[:, 4 * q:4 * q + 4, :], ALU.mult)
            link(last)
            link(V_.tensor_reduce(dg[:, :], Y[:, :, :], axis=X, op=ALU.add))
            link(V_.tensor_tensor(Y[:, :, :], V[:, :, :], bc(dg[:, :], D), ALU.mult))
            for q in range(2):
                dve.wait_ge(S["lo_mm"], q + 1)
                last = V_.tensor_tensor(Y[:, 8 * q:8 * q + 8, :], bank(2 + q, P, 8, D), Y[:, 8 * q:8 * q + 8, :],
                                        ALU.subtract)
            link(last)
            dve.wait_ge(S["hz1"], 1)
            V_.scalar_tensor_tensor(H[:, :, :], Y[:, :, :], 1.0 / N, HZ[:, :, :], ALU.mult, ALU.add).then_inc(S["h1"], 1)
            dve.wait_ge(S["h1"], 1)
            norm(H[:, :, :], Z[:, :, :], NT, 2)
            link(V_.tensor_tensor(Z[:, :, :], Z[:, :, :], bc(rstd[:, :], D), ALU.mult))
            link(V_.tensor_tensor(r2[:, :], rstd[:, :], rstd[:, :], ALU.mult))
            V_.tensor_tensor(r2[:, :], r2[:, :], mv[:, :, 1], ALU.mult).then_inc(S["var"], 1)
            dve.wait_ge(S["rstd"], 3)
            V_.tensor_tensor(XN[:, :, :], Z[:, :, :], bc(r2[:, :], D), ALU.mult).then_inc(S["xn"], 1)
            b0 = count[0]
            CHB = 6
            with dve.Fori(0, PAIRS) as g:
                count[0] = b0
                base = g * CHB
                dve.wait_ge(S["qk_mm"], g * 4 + 4)
                dve.wait_ge(S["rope"], 1 + g)
                for j in range(4):
                    tab = c("cos") if j % 2 == 0 else c("sin")
                    last = V_.tensor_tensor(rope[:, j, :].rearrange("p (i n) -> p i n", i=2),
                                            ps[:, j, 0:CW].rearrange("p (i n) -> p i n", i=2),
                                            tab.unsqueeze(1).to_broadcast([128, 2, N]), ALU.mult)
                last.then_inc(S["rope_cs"], 1)
                for i in range(2):
                    dve.wait_ge(S["s_mm"], g * 2 + (i + 1))
                    link(V_.tensor_tensor(Ssb[:, i, :, :], ps[0:P, 4 * i:4 * i + 4, 0:3 * P],
                                          c("mask")[0:P].unsqueeze(1).to_broadcast([P, NH, 3 * P]), ALU.add), base)
                    V_.tensor_reduce(nmx[:, i, 0, :], Ssb[:, i, :, 0:P], axis=X, op=ALU.max)
                    link(V_.tensor_reduce(nmx[:, i, 1, :], Ssb[:, i, :, P:3 * P], axis=X, op=ALU.max), base)
                    V_.tensor_scalar(nmx[:, i, :, :], nmx[:, i, :, :], -(HD ** -0.5), None, ALU.mult).then_inc(S["nmax"], 1)
                for i in range(2):
                    dve.wait_ge(S["y_mm"], 1 + g * 2 + (i + 1))
                    link(V_.reciprocal(rope[:, 3, i * N:(i + 1) * N], ps[:, 4 * i + 1, 0:N]), base)
                    V_.tensor_tensor(yT[:, i * N:(i + 1) * N], ps[:, 4 * i, 0:N], rope[:, 3, i * N:(i + 1) * N],
                                     ALU.mult).then_inc(S["y_sb"], 1)
                dve.wait_ge(S["pr_mm"], g + 1)
                V_.tensor_tensor(Y[:, bass.ds(g * 4, 4), :], bank(2, P, 4, D), Z[:, bass.ds(g * 4, 4), :],
                                 ALU.add).then_inc(S["x2"], 1)
                assert count[0] - b0 == CHB
            count[0] = b0 + PAIRS * CHB
            dve.wait_ge(S["x2"], 1 + PAIRS)
            link(V_.tensor_tensor(XN[:, :, :], Y[:, :, :], Y[:, :, :], ALU.mult))
            link(V_.tensor_reduce(r2[:, :], XN[:, :, :], axis=X, op=ALU.add))
            V_.tensor_scalar(r2[:, :], r2[:, :], 1.0 / D, None, ALU.mult).then_inc(S["var"], 1)
            dve.wait_ge(S["rstd"], 4)
            V_.tensor_tensor(XN[:, :, :], Y[:, :, :], bc(r2[:, :], D), ALU.mult).then_inc(S["xr"], 1)
            link(V_.tensor_tensor(H[:, :, :], H[:, :, :], Y[:, :, :], ALU.add))
            dve.wait_ge(S["lg_mm"], 1)
            link(V_.tensor_reduce(sm[:, 0, :], bank(4, P, NT, NE), axis=X, op=ALU.max))
            V_.tensor_tensor(lg[:, :, :], bank(4, P, NT, NE), bc(sm[:, 0, :], NE), ALU.subtract).then_inc(S["lg_max"], 1)
            dve.wait_ge(S["lg_exp"], 1)
            link(V_.tensor_reduce(sm[:, 1, :], pr[:, :, :], axis=X, op=ALU.add))
            link(V_.reciprocal(sm[:, 1, :], sm[:, 1, :]))
            link(V_.tensor_tensor(pr[:, :, :], pr[:, :, :], bc(sm[:, 1, :], NE), ALU.mult))
            rank = c("rank")[0:P].unsqueeze(1).to_broadcast([P, NT, NE])

            def first_max(src, dst, s):
                link(V_.tensor_reduce(s, src, axis=X, op=ALU.max))
                link(V_.tensor_tensor(dst, src, bc(s, NE), ALU.is_equal))
                link(V_.tensor_tensor(dst, dst, rank, ALU.mult))
                link(V_.tensor_reduce(s, dst, axis=X, op=ALU.max))
                link(V_.tensor_tensor(dst, dst, bc(s, NE), ALU.is_equal))

            first_max(pr[:, :, :], oh[:, 0, :, :], sm[:, 2, :])
            link(V_.scalar_tensor_tensor(oh[:, 1, :, :], oh[:, 0, :, :], -2.0, pr[:, :, :], ALU.mult, ALU.add))
            first_max(oh[:, 1, :, :], oh[:, 2, :, :], sm[:, 3, :])
            link(V_.tensor_tensor(oh[:, 0, :, :], oh[:, 0, :, :], oh[:, 2, :, :], ALU.add))
            link(V_.tensor_tensor(pr[:, :, :], pr[:, :, :], oh[:, 0, :, :], ALU.mult))
            link(V_.tensor_reduce(sm[:, 0, :], pr[:, :, :], axis=X, op=ALU.add))
            link(V_.tensor_scalar(sm[:, 0, :], sm[:, 0, :], 1e-9, None, ALU.add))
            link(V_.reciprocal(sm[:, 0, :], sm[:, 0, :]))
            link(V_.tensor_tensor(pr[:, :, :], pr[:, :, :], bc(sm[:, 0, :], NE), ALU.mult))

            def split3(src, hi, mid, lo, rest):
                link(V_.tensor_copy(hi, src))
                link(V_.tensor_tensor(rest, src, hi, ALU.subtract))
                link(V_.tensor_copy(mid, rest))
                return V_.tensor_tensor(lo, rest, mid, ALU.subtract)

            split3(pr[:, :, :], wp3[:, :, 0, :], wp3[:, :, 1, :], wp3[:, :, 2, :], lg[:, :, :]).then_inc(S["wp3"], 1)
            with dve.Fori(0, PAIRS) as g:
                for m in range(MT):
                    rows = min(128, HALL - 128 * m)
                    bk = 3 * (m % 2)
                    dve.wait_ge(S["silu"], g * MT + (m + 1))
                    V_.tensor_tensor(bw[0:rows, m % 2, :], silu[0:rows, m % 2, :], ps[0:rows, bk + 1, 0:CW],
                                     ALU.mult).then_inc(S["bw"], 1)
                    dve.wait_ge(S["bw"], 1 + g * MT + (m + 1))
                    dve.wait_ge(S["dn_mm"], 1 + g * MT + max(m - 1, 0))
                    V_.tensor_tensor(hh[0:rows, m % 2, :], bw[0:rows, m % 2, :], ps[0:rows, bk + 2, 0:CW],
                                     ALU.mult).then_inc(S["hh"], 1)
                dve.wait_ge(S["ymT_mm"], g + 1)
                V_.tensor_tensor(H[:, bass.ds(g * 4, 4), :].rearrange("p (i h) d -> p i h d", i=2),
                                 H[:, bass.ds(g * 4, 4), :].rearrange("p (i h) d -> p i h d", i=2),
                                 bank(7, P, 2, 2, D).rearrange("p h i d -> p i h d"), ALU.add).then_inc(S["h2"], 1)
            dve.wait_ge(S["h2"], 1 + PAIRS)
            norm(H[:, :, :], Z[:, :, :], NT, 5)
            V_.tensor_tensor(Z[:, :, :], Z[:, :, :], bc(rstd[:, :], D), ALU.mult).then_inc(S["z3"], 1)
            dve.wait_ge(S["q_mm"], 1)
            qv = qp[:, :, :, :, :].rearrange("p h b a u -> p b h a u")
            split3(bank(4, P, B, 2, U), qv[:, :, :, 0, :], qv[:, :, :, 1, :], qv[:, :, :, 2, :],
                   qr[:, :, :].rearrange("p (b h) u -> p b h u", h=2)).then_inc(S["qp"], 1)
            for g in range(PAIRS):
                dve.wait_ge(S["k_mm"], g + 1)
                last = V_.tensor_scalar(kb[:, g * CW:(g + 1) * CW], bank(g, 3 * U, CW), c("bh")[0:3 * U], None, ALU.add)
            link(last)
            link(V_.tensor_copy(khi[:, :], kb[:, :]))
            RHv = RH[:, :, :, :]

            def twice(ap, p):
                return ap.rearrange("p (b n) -> p b n", b=B).unsqueeze(2).to_broadcast([p, B, 2, N])

            def rows2(dst, src, sub=None):
                for s in range(2):
                    o = dst[:, :, s, :]
                    if sub is None:
                        last = V_.tensor_copy(o, src.rearrange("p (b n) -> p b n", b=B))
                    else:
                        last = V_.tensor_tensor(o, src.rearrange("p (b n) -> p b n", b=B),
                                                sub.rearrange("p (b n) -> p b n", b=B), ALU.subtract)
                return last

            rows2(RHv[0:U], khi[0:U, :])
            for p0, p1 in ((U, 2 * U), (2 * U, 3 * U)):
                last = V_.tensor_tensor(kb[p0:p1, :], kb[p0:p1, :], khi[p0:p1, :], ALU.subtract)
            link(last)
            for p0, p1 in ((U, 2 * U), (2 * U, 3 * U)):
                last = V_.tensor_copy(khi[p0:p1, :], kb[p0:p1, :])
            link(last)
            rows2(RHv[U:2 * U], khi[U:2 * U, :])
            rows2(RHv[2 * U:3 * U], kb[2 * U:3 * U, :], khi[2 * U:3 * U, :]).then_inc(S["kp"], 1)
            b1 = count[0]
            CHD = 3
            with dve.Fori(0, B) as b:
                count[0] = b1
                base = b * CHD
                dve.wait_ge(S["al_mm"], 1 + b * RND + RND)
                dve.wait_ge(S["pt2_mm"], 1 + b)
                V_.tensor_scalar(AL[:, 0, :], ps[:, 6, 0:N], c("ba"), None, ALU.add)
                link(V_.tensor_scalar(AL[0:64, 1, :], ps[0:64, 7, 0:N], c("ba")[0:64], None, ALU.add), base)
                V_.tensor_reduce(ast[:, 0, 0:1], AL[:, 0, :], axis=X, op=ALU.max)
                link(V_.tensor_reduce(ast[0:64, 1, 0:1], AL[0:64, 1, :], axis=X, op=ALU.max), base)
                V_.tensor_scalar(ast[:, 0, 1:2], ast[:, 0, 0:1], -1.0, None, ALU.mult)
                V_.tensor_scalar(ast[0:64, 1, 1:2], ast[0:64, 1, 0:1], -1.0, None, ALU.mult).then_inc(S["amax"], 1)
                dve.wait_ge(S["aexp"], b + 1)
                V_.reciprocal(ast[:, 0, 3:4], ast[:, 0, 2:3])
                link(V_.reciprocal(ast[0:64, 1, 3:4], ast[0:64, 1, 2:3]), base)
                V_.tensor_scalar(AL[:, 0, :], AL[:, 0, :], ast[:, 0, 3:4], None, ALU.mult)
                V_.tensor_scalar(AL[0:64, 1, :], AL[0:64, 1, :], ast[0:64, 1, 3:4], None, ALU.mult).then_inc(S["pn"], 1)
                dve.wait_ge(S["c_mm"], b + 1)
                V_.tensor_tensor(H[:, bass.ds(b * 2, 2), :], bank(1, P, 2, D), H[:, bass.ds(b * 2, 2), :],
                                 ALU.add).then_inc(S["h3"], 1)
                assert count[0] - b1 == CHD
            count[0] = b1 + B * CHD
            dve.wait_ge(S["h3"], 1 + B)
            norm(H[:, :, :], Z[:, :, :], NT, 6)
            V_.tensor_tensor(Z[:, :, :], Z[:, :, :], bc(rstd[:, :], D), ALU.mult).then_inc(S["z4"], 1)
            dve.wait_ge(S["fT"], PAIRS)
            link(V_.tensor_reduce(ms[0:D, :], TA[0:D, :].rearrange("p (b n) -> p b n", b=B), axis=X, op=ALU.add))
            V_.tensor_scalar(ms[0:D, :], ms[0:D, :], 1.0 / N, None, ALU.mult).then_inc(S["msum"], 1)
            dve.wait_ge(S["rl_mm"], 1)
            link(V_.tensor_reduce(rs[:, 0:1], bank(4, B, NE), axis=X, op=ALU.max))
            V_.tensor_scalar(rt[:, 0, :], bank(4, B, NE), rs[:, 0:1], None, ALU.subtract).then_inc(S["rl_max"], 1)
            dve.wait_ge(S["rl_exp"], 1)
            link(V_.reciprocal(rs[:, 1:2], rs[:, 1:2]))
            V_.tensor_scalar(rt[:, 2, :], rt[:, 1, :], rs[:, 1:2], None, ALU.mult).then_inc(S["wd"], 1)
            dve.wait_ge(S["ld_mm"], 1)
            link(V_.tensor_scalar(rt[:, 5, :], bank(5, B, NE), float(N), None, ALU.mult))
            link(V_.reciprocal(rt[:, 5, :], rt[:, 5, :]))
            link(V_.tensor_scalar(rt[:, 5, :], rt[:, 5, :], CAP, 1.0, ALU.mult, ALU.min))
            link(V_.tensor_tensor(rt[:, 2, :], rt[:, 2, :], rt[:, 5, :], ALU.mult))
            link(V_.tensor_reduce(rs[:, 2:3], rt[:, 2, :], axis=X, op=ALU.max))
            V_.tensor_scalar(rt[:, 3, :], rt[:, 2, :], rs[:, 2:3], None, ALU.subtract).then_inc(S["r2max"], 1)
            dve.wait_ge(S["r2exp"], 1)
            link(V_.reciprocal(rs[:, 3:4], rs[:, 3:4]))
            link(V_.tensor_scalar(rt[:, 7, :], rt[:, 4, :], rs[:, 3:4], None, ALU.mult))

            def first_max8(src, dst, s):
                link(V_.tensor_reduce(s, src, axis=X, op=ALU.max))
                link(V_.tensor_scalar(dst, src, s, None, ALU.is_equal))
                link(V_.tensor_tensor(dst, dst, c("rank")[0:B], ALU.mult))
                link(V_.tensor_reduce(rs[:, 4:5], dst, axis=X, op=ALU.max))
                link(V_.tensor_scalar(dst, dst, rs[:, 4:5], None, ALU.is_equal))

            first_max8(rt[:, 7, :], rt[:, 8, :], rs[:, 5:6])
            link(V_.scalar_tensor_tensor(rt[:, 9, :], rt[:, 8, :], -2.0, rt[:, 7, :], ALU.mult, ALU.add))
            first_max8(rt[:, 9, :], rt[:, 10, :], rs[:, 6:7])
            V_.tensor_tensor(rs[:, 10:11], rs[:, 6:7], rs[:, 5:6], ALU.subtract).then_inc(S["e2exp"], 1)
            dve.wait_ge(S["e2exp"], 2)
            link(V_.tensor_scalar(rs[:, 12:13], rs[:, 11:12], 1.0, None, ALU.add))
            link(V_.scalar_tensor_tensor(rt[:, 11, :], rt[:, 10, :], rs[:, 11:12], rt[:, 8, :], ALU.mult, ALU.add))
            link(V_.reciprocal(rs[:, 12:13], rs[:, 12:13]))
            V_.tensor_scalar(rt[:, 12, :], rt[:, 11, :], rs[:, 12:13], None, ALU.mult).then_inc(S["wd"], 1)
            dve.wait_ge(S["wd"], 2)
            eye = ident[0:B, 0:B]
            V_.tensor_tensor(dgw[:, 0:B * NE].rearrange("p (b e) -> p b e", b=B),
                             rt[:, 12, :].unsqueeze(1).to_broadcast([B, B, NE]), bc(eye, NE), ALU.mult)
            dve.wait_ge(S["wdT"], 2)
            V_.tensor_tensor(dgw[:, B * NE:].rearrange("p (b e) -> p b e", b=B),
                             b2w[:, :].unsqueeze(1).to_broadcast([B, B, D]), bc(eye, D), ALU.mult).then_inc(S["dg"], 1)
            dve.wait_ge(S["wB_mm"], 1)
            V_.tensor_copy(wBC[:, :, :], bank(6, 128, B, NE)).then_inc(S["wbc"], 1)
            dve.wait_ge(S["wbc"], 2)
            with dve.Fori(0, PAIRS) as g:
                dve.wait_ge(S["e2_mm"], 1 + g)
                for i in range(2):
                    V_.tensor_tensor(W2S[:, i, :, :], c("e2").rearrange("p (e d) -> p e d", e=NE),
                                     wBC[:, bass.ds(g * 2 + i, 1), :].rearrange("p o e -> p (o e)").unsqueeze(2
                                     ).to_broadcast([128, NE, D]), ALU.mult).then_inc(S["w2s"], 1)
                dve.wait_ge(S["o_mm"], g + 1)
                V_.tensor_tensor(Y[:, bass.ds(g * 4, 4), :].rearrange("p (i h) d -> p i h d", i=2),
                                 Z[:, bass.ds(g * 4, 4), :].rearrange("p (i h) d -> p i h d", i=2),
                                 bank(6, P, 2, 2, D).rearrange("p h i d -> p i h d"), ALU.add).then_inc(S["fo"], 1)
            dve.wait_ge(S["fo"], 1 + PAIRS)
            link(V_.tensor_tensor(Y[:, :, :].rearrange("p (b h) d -> p b h d", h=2),
                                  Y[:, :, :].rearrange("p (b h) d -> p b h d", h=2),
                                  bBC.unsqueeze(2).to_broadcast([P, B, 2, D]), ALU.add))
            norm(Y[:, :, :], Y[:, :, :], NT, 7)
            link(V_.tensor_tensor(Y[:, :, :], Y[:, :, :], bc(rstd[:, :], D), ALU.mult))
            link(V_.tensor_tensor(Y[:, :, :], Y[:, :, :], c("gamma")[0:P].unsqueeze(1).to_broadcast([P, NT, D]),
                                  ALU.mult))
            link(V_.tensor_tensor(Y[:, :, :], Y[:, :, :], c("beta")[0:P].unsqueeze(1).to_broadcast([P, NT, D]),
                                  ALU.add))
            V_.tensor_tensor(Y[:, :, :], Y[:, :, :], H[:, :, :], ALU.add).then_inc(S["y_out"], 1)

        @block.tensor
        def _(pe):
            for name in ("y_mm", "al_mm", "e2_mm", "dn_mm", "pt2_mm",):
                pe.sem_inc(S[name], 1)
            pe.wait_ge(S["ld_tok"], 48)
            mm(bank(0, D, NPATCH), t3[:, 0:D], t3[:, D:]).then_inc(S["hid_mm"], 1)
            pe.wait_ge(S["ld_w64"], 16)
            mm(bank(1, D, D), w("Wa")[0:D], w("Wb")[0:D])
            mm(bank(2, D + 1, D), w("Wu")[0:D], w("WrT")[0:D])
            mm(bank(3, D, D), w("Wb")[0:D], w("Wa")[0:D]).then_inc(S["gmm"], 1)
            for k in range(KC):
                pe.wait_ge(S["ld_x"], 16 * KC) if k == 0 else None
                mm(bank(4, D, B * NPATCH), wpT[:, k, :], xP[:, k, :], start=(k == 0), stop=False)
            pe.wait_ge(S["hid"], 1)
            pe.wait_ge(S["filled"], FILLS)
            mm(bank(4, D, B, NPATCH), t66[:, :], hid[:, :].unsqueeze(1).to_broadcast([D + 2, B, NPATCH]),
               start=False, stop=True).then_inc(S["emb_mm"], 1)
            pe.wait_ge(S["emb"], 1)
            pe.wait_ge(S["ld_c"], 16)
            for b in range(B):
                last = nc.tensor.transpose(bank(5, NPATCH, B, D)[:, b, :], embS[:, b * NPATCH:(b + 1) * NPATCH],
                                           ident[0:D, 0:D])
            last.then_inc(S["embT"], 1)

            def transposes(src, done):
                for g in range(PAIRS):
                    for t in range(4):
                        last = nc.tensor.transpose(bank(g, D, 4, P)[:, t, :], src[:, 4 * g + t, :], ident[0:P, 0:P])
                    last.then_inc(done, 1)

            pe.wait_ge(S["z1"], 1)
            pe.wait_ge(S["gc_ready"], 1)
            transposes(Z, S["zT_mm"])
            for q in range(PAIRS):
                pe.wait_ge(S["zT"], q + 1)
                if q == 1:
                    pe.wait_ge(S["h0"], 1)
                for t in range(4):
                    a = (4 * q + t) * P
                    last = mm(bank(4 + q, P, 4, 2 * D)[:, t, :], TA[:, a:a + P], GC[:, :])
                last.then_inc(S["gv_mm"], 1)
            pe.wait_ge(S["v_sb"], PAIRS)
            for b in range(B):
                for t in (2 * b, 2 * b + 1):
                    last = mm(bank(0, D, B, D)[:, b, :], Z[:, t, :], V[:, t, :], start=(t % 2 == 0), stop=(t % 2 == 1))
            last.then_inc(S["zv_mm"], 1)
            pe.wait_ge(S["zv"], 1)
            mm(bank(1, D, B * D), GT[:, :], ZV[:, :]).then_inc(S["p_mm"], 1)
            pe.wait_ge(S["p_sb"], 1)
            for q in range(2):
                for t in range(8):
                    a = (8 * q + t) * P
                    last = mm(bank(2 + q, P, 8, D)[:, t, :], TA[:, a:a + P], PB[:, (8 * q + t) // 2, :])
                last.then_inc(S["lo_mm"], 1)
            pe.wait_ge(S["xn"], 1)
            pe.wait_ge(S["lnw_ready"], 1)
            transposes(XN, S["xT_mm"])
            pe.wait_ge(S["xT"], PAIRS)
            for t in range(NT):
                last = mm(bank(4, P, NT, NKV * HD)[:, t, :], TB[:, t * P:(t + 1) * P], w("v"))
            last.then_inc(S["v_mm"], 1)
            pe.wait_ge(S["vall"], 1)
            with pe.Fori(0, PAIRS) as g:
                pe.wait_ge(S["x2"], 1 + g)
                for j, name in enumerate(("q", "qs", "k", "ks")):
                    mm(ps[:, j, 0:CW], w(name), TB[:, bass.ds(g * CW, CW)]).then_inc(S["qk_mm"], 1)
                pe.wait_ge(S["rope"], 1 + g + 1)
                for i in range(2):
                    for h in range(NH):
                        r = slice(32 * h, 32 * h + 32)
                        for t in range(2):
                            a = i * N + t * P
                            last = mm(ps[0:P, 4 * i + h, t * P:t * P + (t + 1) * P], QT[r, a:a + P],
                                      KT[r, i * N:i * N + (t + 1) * P])
                    last.then_inc(S["s_mm"], 1)
                for i in range(2):
                    pe.wait_ge(S["p_exp"], g * 2 + (i + 1))
                    for h in range(NH):
                        for src, dst in ((0, 0), (P, P), (2 * P, 2 * P)):
                            last = nc.tensor.transpose(ps[0:P, 4 * i + h, dst:dst + P],
                                                       Pex[:, i, h, src:src + P], ident[0:P, 0:P])
                    last.then_inc(S["pt_mm"], 1)
                pe.wait_ge(S["vb"], g + 1)
                for i in range(2):
                    pe.wait_ge(S["pt_sb"], g * 2 + (i + 1))
                    for dst, stat_ in ((4 * i, None), (4 * i + 1, ones)):
                        for t in range(2):
                            for h in range(NH):
                                lhs = ones[0:P, 0:32] if stat_ is not None else Vb[:, 2 * i + t, h // 2, :]
                                last = mm(ps[32 * h:32 * h + 32, dst, t * P:N], lhs,
                                          PT[:, i, h, 2 * P * t:2 * P + P * t], start=(t == 0), stop=(t == 1),
                                          skip_group_check=True)
                    last.then_inc(S["y_mm"], 1)
                for i in range(2):
                    pe.wait_ge(S["y_sb"], g * 2 + (i + 1))
                    for t in range(2):
                        a = i * N + t * P
                        last = mm(bank(2, P, 4, D)[:, 2 * i + t, :], yT[:, a:a + P], c("wo"))
                last.then_inc(S["pr_mm"], 1)
            pe.wait_ge(S["xr"], 1)
            transposes(XN, S["rT_mm"])
            pe.wait_ge(S["rT"], PAIRS)
            for t in range(NT):
                last = mm(bank(4, P, NT, NE)[:, t, :], TA[:, t * P:(t + 1) * P], w("rw"))
            last.then_inc(S["lg_mm"], 1)
            pe.wait_ge(S["wp3"], 1)
            pe.wait_ge(S["ld_b"], 48)
            for t in range(NT):
                dst = ps[0:3 * NE, 5 + t // 8, :].bitcast(BF16)[:, (t % 8) * P:(t % 8 + 1) * P]
                last = nc.tensor.transpose(dst, wp3[:, t, :, :].rearrange("p a e -> p (a e)"), idb[0:P, 0:P])
            last.then_inc(S["wT_mm"], 1)
            pe.wait_ge(S["wT"], 1)
            with pe.Fori(0, PAIRS) as g:
                def up(m):
                    rows = min(128, HALL - 128 * m)
                    s = 3 * (m % 2)
                    pe.wait_ge(S["hh"], 1 + g * MT + max(m - 1, 0))
                    rhs = TA[:, bass.ds(g * CW, CW)]
                    mm(ps[0:rows, s, 0:CW], w("w1", 128 * m, 128 * m + rows), rhs)
                    mm(ps[0:rows, s + 1, 0:CW], w("w3", 128 * m, 128 * m + rows), rhs)
                    mm(ps[0:rows, s + 2, 0:CW], sel[:, 128 * m:128 * m + rows],
                       wT[:, bass.ds(g * CW, CW)]).then_inc(S["up_mm"], 1)

                def down(m):
                    rows = min(128, HALL - 128 * m)
                    pe.wait_ge(S["hh"], 1 + g * MT + (m + 1))
                    w2 = c("w2").rearrange("p (m d) -> p m d", m=MT)[0:rows, m, :]
                    for i in range(2):
                        last = mm(ps[64 * i:64 * i + 64, 6, 0:N], w2, hh[0:rows, m % 2, i * N:(i + 1) * N],
                                  start=(m == 0), stop=(m == MT - 1), skip_group_check=True)
                    last.then_inc(S["dn_mm"], 1)

                up(0)
                for m in range(1, MT):
                    up(m)
                    if m >= 2:
                        down(m - 2)
                down(MT - 2)
                down(MT - 1)
                pe.wait_ge(S["ym"], g + 1)
                pe.wait_ge(S["h2"], 1 + g)
                for t in range(2):
                    last = nc.tensor.transpose(bank(7, P, 2, 2 * D)[:, t, :], ym[:, t * P:(t + 1) * P], ident)
                last.then_inc(S["ymT_mm"], 1)
            pe.wait_ge(S["z3"], 1)
            transposes(Z, S["aT_mm"])
            pe.wait_ge(S["aT"], PAIRS)
            for t in range(NT):
                last = mm(bank(4, P, NT, U)[:, t, :], TB[:, t * P:(t + 1) * P], w("wt"))
            last.then_inc(S["q_mm"], 1)
            for g in range(PAIRS):
                mm(bank(g, 3 * U, CW), w("wx"), TB[:, g * CW:(g + 1) * CW]).then_inc(S["k_mm"], 1)
            pe.wait_ge(S["kp"], 1)
            pe.wait_ge(S["ld_hot"], 16)
            pe.wait_ge(S["rep_ready"], 1)
            pe.wait_ge(S["ld_q"], 16 * 2 * B)
            was = c("was").rearrange("p (r u) -> p r u", r=RND)
            with pe.Fori(0, B) as b:
                pe.wait_ge(S["h3"], 1 + b)
                def build(r):
                    if r >= 2:
                        pe.wait_ge(S["tanh"], b * RND + (r - 1))
                    for j in range(3):
                        last = mm(ps[:, 3 * (r % 2) + j, 0:CW],
                                  LQ[:, bass.ds(b, 1), RND * j + r, :].rearrange("p o q -> p (o q)"),
                                  RH[:, bass.ds(b, 1), :, :].rearrange("p o s n -> p (o s n)"))
                    last.then_inc(S["bld_mm"], 1)

                def contract(r):
                    pe.wait_ge(S["tanh"], b * RND + (r + 1))
                    for j in range(3):
                        for s in range(2):
                            n = j + 3 * s
                            last = mm(ps[32 * (n % 4):32 * (n % 4) + 32, 6 + n // 4, 0:N], was[:, r, :],
                                      TH[:, r % 2, j, s * N:(s + 1) * N], start=(r == 0), stop=(r == RND - 1),
                                      skip_group_check=True)
                    last.then_inc(S["al_mm"], 1)

                build(0)
                for r in range(1, RND):
                    build(r)
                    contract(r - 1)
                contract(RND - 1)
                pe.wait_ge(S["pn"], b + 1)
                for t in range(2):
                    nc.tensor.transpose(bank(0, P, 2, N)[:, t, 0:128], AL[:, 0, t * P:(t + 1) * P], ident)
                    last = nc.tensor.transpose(bank(0, P, 2, N)[:, t, 128:N], AL[0:64, 1, t * P:(t + 1) * P],
                                               ident[0:64, 0:64])
                last.then_inc(S["pt2_mm"], 1)
                pe.wait_ge(S["pt2"], b + 1)
                for q in range(2):
                    for t in range(2):
                        last = mm(bank(1, P, 2, D)[:, q, :], PT2[:, t, q * P:(q + 1) * P],
                                  Z[:, bass.ds(b * 2 + t, 1), :].rearrange("p o d -> p (o d)"),
                                  start=(t == 0), stop=(t == 1))
                last.then_inc(S["c_mm"], 1)
            pe.wait_ge(S["z4"], 1)
            transposes(Z, S["fT_mm"])
            pe.wait_ge(S["msum"], 1)
            pe.wait_ge(S["ld_row"], 16)
            mm(bank(4, B, NE), ms[:, :], w("wr")).then_inc(S["rl_mm"], 1)
            pe.wait_ge(S["wd"], 1)
            mm(bank(5, B, NE), ones[0:B, 0:B], rt[:, 2, :]).then_inc(S["ld_mm"], 1)
            pe.wait_ge(S["wd"], 2)
            nc.tensor.transpose(bank(5, NE, B), rt[:, 12, :], ident[0:B, 0:B]).then_inc(S["wdT_mm"], 1)
            pe.wait_ge(S["wdT"], 1)
            pe.wait_ge(S["ld_b2"], 16)
            mm(bank(6, B, D), wdT[:, :], b2s[:, :]).then_inc(S["b2w_mm"], 1)
            pe.wait_ge(S["dg"], 1)
            mm(bank(6, 128, B * NE), ones[0:B, :], dgw[:, 0:B * NE]).then_inc(S["wB_mm"], 1)
            mm(bank(7, P, B * D), ones[0:B, 0:P], dgw[:, B * NE:]).then_inc(S["bB_mm"], 1)
            pe.wait_ge(S["wbc"], 2)
            with pe.Fori(0, PAIRS) as g:
                for e in range(NE):
                    if e >= 4:
                        pe.wait_ge(S["gelu"], g * NE + (e - 3))
                    mm(ps[:, e % 4, 0:CW], w("e1", e * FE, (e + 1) * FE), TA[:, bass.ds(g * CW, CW)]).then_inc(S["e1_mm"], 1)
                pe.wait_ge(S["w2s"], g * 2 + 2)
                pe.wait_ge(S["oT"], 1 + g)
                for e in range(NE):
                    pe.wait_ge(S["gelu"], g * NE + (e + 1))
                    for i in range(2):
                        last = mm(ps[64 * i:64 * i + 64, 4, 0:N], W2S[:, i, e, :], G1[:, e, i * N:(i + 1) * N],
                                  start=(e == 0), stop=(e == NE - 1), skip_group_check=True)
                last.then_inc(S["e2_mm"], 1)
                pe.wait_ge(S["oT"], 1 + g + 1)
                pe.wait_ge(S["fo"], 1 + g)
                for t in range(2):
                    last = nc.tensor.transpose(bank(6, P, 2, 2 * D)[:, t, :], oT[:, t * P:(t + 1) * P], ident)
                last.then_inc(S["o_mm"], 1)


_ARGS = ("patches", "wpatch", "txt", "w64", "e1row", "tok66", "tok3", "c128", "b2", "idb", "sel", "rep", "hot")


def _layout(x, txt, L0_tok_Wp, L0_tok_bp, L0_tok_W1, L0_tok_b1, L0_tok_W2, L0_tok_b2, L0_attn_W_alpha,
            L0_attn_W_beta, L0_attn_W_unary, L0_attn_b_unary, L0_attn_W_r, L0_ffn_ln1_w, L0_ffn_ln2_w, L0_ffn_wq,
            L0_ffn_wk, L0_ffn_wv, L0_ffn_wo, L0_ffn_router_w, L0_ffn_w1, L0_ffn_w2, L0_ffn_w3, L1_attn_Wt,
            L1_attn_Wx, L1_attn_bh, L1_attn_Wa, L1_attn_ba, L1_ffn_Wr, L1_ffn_br, L1_ffn_W1, L1_ffn_b1,
            L1_ffn_W2, L1_ffn_b2, L1_ffn_gamma, L1_ffn_beta):
    f = np.float32
    a = np.asarray

    def zeros(*s):
        return np.zeros(s, f)

    xp = a(x).reshape(B, CH, NPS, PS, NPS, PS).transpose(1, 3, 5, 0, 2, 4).reshape(KC, 128, B * NPATCH)
    d = {"patches": xp.transpose(1, 0, 2), "wpatch": a(L0_tok_Wp).reshape(KC, 128, D).transpose(1, 0, 2),
         "txt": a(txt)}
    wq, wk = a(L0_ffn_wq), a(L0_ffn_wk)

    def heads(wt, per, swap):
        o = zeros(D, 128)
        for h in range(NH):
            rows = wt[(h // per) * HD:(h // per + 1) * HD]
            if swap:
                rows = np.concatenate([rows[HD // 2:], rows[:HD // 2]])
            o[:, 32 * h:32 * h + HD] = rows.T
        return o

    cols = {"Wa": a(L0_attn_W_alpha), "Wb": a(L0_attn_W_beta),
            "Wu": np.concatenate([a(L0_attn_W_unary), a(L0_attn_b_unary)[:, None]], 1), "WrT": a(L0_attn_W_r).T,
            "ln1": a(L0_ffn_ln1_w)[:, None], "ln2": a(L0_ffn_ln2_w)[:, None],
            "q": heads(wq, 1, False), "qs": heads(wq, 1, True), "k": heads(wk, NH // NKV, False),
            "ks": heads(wk, NH // NKV, True), "v": a(L0_ffn_wv).T, "rw": a(L0_ffn_router_w).T,
            "w1": a(L0_ffn_w1).reshape(HALL, D).T, "w3": a(L0_ffn_w3).reshape(HALL, D).T,
            "wt": a(L1_attn_Wt), "wx": np.concatenate([a(L1_attn_Wx).T] * 3, 1),
            "e1": a(L1_ffn_W1).transpose(1, 0, 2).reshape(D, NE * FE), "wr": a(L1_ffn_Wr)}
    d["w64"] = np.concatenate([cols[n] for n in W64], 1)
    d["e1row"] = np.concatenate([a(L1_ffn_b1).reshape(1, NE * FE), a(L1_ffn_br).reshape(1, NE)], 1)
    d["tok66"] = np.concatenate([a(L0_tok_W2), a(L0_tok_b2)[None], a(L0_tok_bp)[None]])
    gx, gy = np.meshgrid(np.arange(NPS), np.arange(NPS), indexing="ij")
    xy = np.stack([gx.ravel(), gy.ravel(), np.full(NPATCH, NPS - 1)]).astype(f) / f(NPS - 1)
    d["tok3"] = np.concatenate([np.concatenate([a(L0_tok_W1), a(L0_tok_b1)[None]]), xy], 1)
    inv = 1.0 / 10000.0 ** (np.arange(0, HD, 2, dtype=f) / HD)
    ang = np.outer(np.concatenate([inv, inv]).astype(f), np.arange(N, dtype=f)).astype(f)
    cos, sin = zeros(128, N), zeros(128, N)
    for h in range(NH):
        cos[32 * h:32 * h + HD] = np.cos(ang)
        sin[32 * h:32 * h + HD] = np.sin(ang) * np.where(np.arange(HD) < HD // 2, -1, 1)[:, None]
    mask = zeros(128, 3 * P)
    i = np.arange(P)
    mask[:P, 0:P] = np.where(i[None] > i[:, None], NEG, 0)
    mask[:P, 2 * P:] = mask[:P, 0:P]
    wo = zeros(128, D)
    for h in range(NH):
        wo[32 * h:32 * h + HD] = a(L0_ffn_wo).T[HD * h:HD * (h + 1)]
    w2 = zeros(MPAD, D)
    w2[:HALL] = a(L0_ffn_w2).transpose(0, 2, 1).reshape(HALL, D)
    was = zeros(IB, U, RND, IB * RND)
    for r in range(RND):
        for q in range(IB):
            was[q, :, r, IB * r + q] = a(L1_attn_Wa)[:, 0]
    cc = {"ident": np.eye(128, dtype=f), "cos": cos, "sin": sin, "mask": mask,
          "rank": np.broadcast_to(np.arange(NE, 0, -1).astype(f), (128, NE)), "wo": wo,
          "w2": w2.reshape(MT, 128, D).transpose(1, 0, 2).reshape(128, MT * D), "was": was.reshape(128, RND * U),
          "ba": np.broadcast_to(a(L1_attn_ba), (128, 1)), "bh": np.concatenate([a(L1_attn_bh)] * 4)[:, None],
          "gamma": np.broadcast_to(a(L1_ffn_gamma), (128, D)), "beta": np.broadcast_to(a(L1_ffn_beta), (128, D)),
          "e2": a(L1_ffn_W2).transpose(1, 0, 2).reshape(FE, NE * D)}
    d["c128"] = np.concatenate([cc[n] for n in C128], 1)
    d["b2"] = a(L1_ffn_b2)
    d["idb"] = np.eye(128).astype(f)
    owner = np.full(MPAD, -1)
    owner[:HALL] = np.arange(HALL) // HID
    d["sel"] = np.concatenate([owner[None] == np.arange(NE)[:, None]] * 3).astype(f)
    d["rep"] = np.concatenate([np.concatenate([np.eye(U)] * IB, 1)] * 3).astype(f)
    hot = np.zeros((2, 3, B, 2, N), f)
    hot[0, :, :, 0], hot[1, :, :, 1] = 1, 1
    d["hot"] = hot.reshape(6, B, 2, N)
    return {k: np.ascontiguousarray(v) for k, v in d.items()}


def kernel(**inputs):
    import concourse.bacc as _bacc
    from concourse.bass_utils import run_bass_kernel_spmd as _run

    nc = _bacc.Bacc("TRN2", target_bir_lowering=False, num_devices=1)
    d = _layout(**inputs)
    arrays, args = {}, []
    for name in _ARGS:
        arrays[f"in_{name}_dram"] = d[name]
        args.append(nc.dram_tensor(f"in_{name}_dram", d[name].shape, mybir.dt.from_np(d[name].dtype),
                                   kind="ExternalInput").ap())
    args.append(nc.dram_tensor("out_dram", (B, N, D), F32, kind="ExternalOutput").ap())
    early_fusion(nc, *args)
    r = _run(nc, [arrays], core_ids=[0])
    return r.results[0]["out_dram"]
```

```python
from contextlib import ExitStack

import numpy as np

import concourse.bass as bass
from concourse import mybir

ALU = mybir.AluOpType
ACT = mybir.ActivationFunctionType
F32 = mybir.dt.float32
BF16 = mybir.dt.bfloat16
X = mybir.AxisListType.X

B = 8
CH, HW, PS = 3, 128, 16
NPS = HW // PS
NPATCH = NPS * NPS
TXT = 128
N = NPATCH + TXT
D = 64
P = N // 2
NT = 2 * B
TOK = B * N
KC = CH * PS * PS // 128
PAIRS = B // 2
CW = 2 * N
NH, NKV, HD = 4, 2, 16
NE, HID = 8, 170
HALL = NE * HID
MT = -(-HALL // 128)
MPAD = MT * 128
U = 32
IB = 128 // U
NCH = P // IB
RND = 8
FE = 128
CAP = float(-(-TOK * 5 // (4 * 8)))
NEG = -1e30
FILLS = 13

W64 = {}
_at = 0
for _name, _n in (("Wa", D), ("Wb", D), ("Wu", D + 1), ("WrT", D), ("ln1", 1), ("ln2", 1),
                  ("q", 128), ("qs", 128), ("k", 128), ("ks", 128), ("v", NKV * HD),
                  ("rw", NE), ("w1", HALL), ("w3", HALL),
                  ("wt", U), ("wx", 3 * U), ("e1", NE * FE), ("wr", NE)):
    W64[_name] = (_at, _n)
    _at += _n
NW64 = _at
C128 = {}
_at = 0
for _name, _n in (("ident", 128), ("cos", N), ("sin", N), ("mask", 3 * P), ("rank", NE), ("wo", D),
                  ("w2", MT * D), ("was", RND * U), ("ba", 1), ("bh", 1), ("gamma", D), ("beta", D),
                  ("e2", NE * D)):
    C128[_name] = (_at, _n)
    _at += _n
NC128 = _at


def early_fusion(nc, patches, wpatch, txt, w64_d, e1row, tok66, tok3, c128_d, b2_d, idb_d, sel_d, rep_d, hot_d, out):
    qrows = nc.dram_tensor("qrows", (2, B, 3, P, U), BF16, kind="Internal").ap()
    with ExitStack() as ctx:
        def sb(name, shape, dt=F32):
            return ctx.enter_context(nc.sbuf_tensor(name, shape, dt))

        S = {n: ctx.enter_context(nc.semaphore(n)) for n in (
            "ld_x", "ld_txt", "ld_w64", "ld_row", "ld_c", "ld_tok", "ld_b", "ld_b2", "ld_hot", "st_q", "ld_q", "st_out",
            "filled", "gc_ready", "gt_ready", "lnw_ready", "rep_ready",
            "dve", "var", "veps", "rstd", "fo",
            "hid_mm", "hid", "emb_mm", "emb", "embT", "h0",
            "gmm",
            "z1", "zT_mm", "zT", "gv_mm", "v_sb", "zv_mm", "zv", "p_mm", "p_sb", "lo_mm", "hz1", "h1",
            "xn", "z2", "xT_mm", "xT", "v_mm", "vall", "qk_mm", "rope_cs", "rope", "vb", "s_mm", "s_sb", "nmax", "p_exp",
            "pt_mm", "pt_sb", "y_mm", "y_sb", "pr_mm", "x2", "h12",
            "xr", "rT_mm", "rT", "lg_mm", "lg_max", "lg_exp", "wp3", "wT_mm", "wT", "up_mm", "silu", "bw", "hh",
            "dn_mm", "ym", "ymT_mm", "h2",
            "z3", "aT_mm", "aT", "q_mm", "k_mm", "qp", "kp", "bld_mm", "tanh", "al_mm", "al_sb", "amax", "aexp", "pn",
            "pt2_mm", "pt2", "c_mm", "h3",
            "z4", "fT_mm", "fT", "msum", "rl_mm", "rl_max", "rl_exp", "ld_mm", "r2max", "r2exp", "e2exp",
            "wd", "zb", "wdT_mm", "wdT", "b2w_mm", "dg", "wB_mm", "bB_mm", "wbc", "w2s", "e1_mm", "gelu", "e2_mm", "oT",
            "o_mm", "y_out")}

        w64 = sb("w64", [128, NW64])
        c128 = sb("c128", [128, NC128])
        xP = sb("xP", [128, KC, B * NPATCH])
        wpT = sb("wpT", [128, KC, D])
        t66 = sb("t66", [D + 2, D])
        t3 = sb("t3", [3, D + NPATCH])
        hid = sb("hid", [D + 2, NPATCH])
        b2s = sb("b2s", [NE, D])
        idb = sb("idb", [128, 128], BF16)
        sel = sb("sel", [3 * NE, MPAD], BF16)
        rep = sb("rep", [3 * U, 128], BF16)
        GT = sb("GT", [D, D])
        GC = sb("GC", [128, 2 * D])

        def w(name, lo=0, hi=None):
            at, n = W64[name]
            return w64[:, at + lo:at + (n if hi is None else hi)]

        def c(name):
            at, n = C128[name]
            return c128[:, at:at + n]

        ident = c("ident")
        H = sb("H", [P, NT, D])
        Z = sb("Z", [P, NT, D])
        Y = sb("Y", [P, NT, D])
        XN = sb("XN", [P, NT, D])
        HZ = sb("HZ", [P, NT, D])
        V = XN
        stat = sb("stat", [P, NT, 6])
        mv = sb("mv", [P, NT, 2])
        rstd = sb("rstd", [P, NT])
        mhalf = sb("mhalf", [P, NT])
        r2 = sb("r2", [P, NT])
        dg = sb("dg", [P, NT])
        TA = sb("TA", [128, TOK])
        TB = sb("TB", [128, TOK])
        embS = sb("embS", [D, B * NPATCH])
        ZV = sb("ZV", [D, B * D])
        PB = sb("PB", [128, B, D])
        Vall = sb("Vall", [P, NT, NKV, 2 * HD])
        Vb = sb("Vb", [P, 4, NKV, 2 * HD])
        rope = sb("rope", [128, 4, CW])
        QT = sb("QT", [128, CW])
        KT = sb("KT", [128, CW])
        SP_ = sb("SP_", [128, 3, 2, NH, 3 * P])
        Ssb = SP_[0:P, 0]
        nmx = sb("nmx", [P, 2, 2, NH])
        Pex = SP_[0:P, 1]
        PT = SP_[0:P, 2]
        yT = sb("yT", [128, CW])
        ones = sb("ones", [128, 128])
        lg = sb("lg", [P, NT, NE])
        pr = sb("pr", [P, NT, NE])
        oh = sb("oh", [P, 3, NT, NE])
        sm = sb("sm", [P, 4, NT])
        wp3 = sb("wp3", [P, NT, 3, NE], BF16)
        wT = sb("wT", [3 * NE, TOK], BF16)
        up_sb = sb("up_sb", [128, 3, 2, CW])
        silu, bw, hh = up_sb[:, 0], up_sb[:, 1], up_sb[:, 2]
        ym = sb("ym", [128, N])
        qp = sb("qp", [P, 2, B, 3, U], BF16)
        qr = sb("qr", [P, NT, U])
        kb = xP[0:3 * U, 0:3, :].rearrange("p k n -> p (k n)")
        khi = xP[0:3 * U, 3:5, :].rearrange("p k n -> p (k n)").bitcast(BF16)[:, 0:TOK]
        RH = sb("RH", [3 * U + 6, B, 2, N], BF16)
        LQ_ = sb("LQ_", [128, B, NCH, 128], BF16)
        LQ = LQ_[0:3 * U + 6]
        TH = SP_[:, :, :, :, :].rearrange("p a b c d -> p (a b c d)")[:, 0:12 * CW].rearrange("p (s j n) -> p s j n", s=4, j=3)
        AL = rope[:, 0, :].rearrange("p (a n) -> p a n", a=2)
        ast = sb("ast", [128, 2, 4])
        PT2 = rope[0:P, 1, :].rearrange("p (a n) -> p a n", a=2)
        ms = sb("ms", [128, B])
        rt = sb("rt", [B, 16, NE])
        rs = sb("rs", [B, 24])
        wdT = sb("wdT", [NE, B])
        b2w = sb("b2w", [B, D])
        dgw = Vall[0:B].rearrange("p t k e -> p (t k e)")[:, 0:B * (NE + D)]
        wBC = sb("wBC", [128, B, NE])
        bBC = HZ[:, 8:16, :]
        W2S = SP_[:, :, :, :, :].rearrange("p a b c d -> p (a b c d)")[:, 0:B * NE * D].rearrange(
            "p (b e d) -> p b e d", b=B, e=NE)
        G1 = LQ_[:, :, :, :].rearrange("p b c q -> p (b c q)").bitcast(F32).rearrange(
            "p (g e n) -> p g e n", g=PAIRS, e=NE)
        oT = rope[:, 2, :].rearrange("p (s n) -> p s n", s=2)

        ps = ctx.enter_context(nc.psum_tensor("ps", [128, 8, 512], F32))

        def bank(i, rows, *dims):
            n = 1
            for x in dims:
                n *= x
            v = ps[0:rows, i, 0:n]
            if len(dims) == 2:
                v = v.rearrange("p (a b) -> p a b", a=dims[0])
            if len(dims) == 3:
                v = v.rearrange("p (a b c) -> p a b c", a=dims[0], b=dims[1])
            return v

        def mm(out_, lhsT, rhs, start=True, stop=True, **k):
            return nc.tensor.matmul(out_, lhsT, rhs, start=start, stop=stop, **k)

        def bc(ap, n):
            return ap.unsqueeze(2).to_broadcast([ap.shape[0], ap.shape[1], n])

        def after(eng, name, n):
            if not isinstance(n, int) or n > 0:
                eng.wait_ge(S[name], n)

        block = ctx.enter_context(nc.Block())

        @block.sync
        def _(sp):
            for k in range(KC):
                sp.dma_start(xP[:, k, :], patches[:, k, :]).then_inc(S["ld_x"], 16)
            sp.dma_start(c128[:, :], c128_d).then_inc(S["ld_c"], 16)
            sp.wait_ge(S["qp"], 1)
            for half in range(2):
                sp.dma_start(qrows[half].rearrange("b a p u -> p (b a) u"),
                             qp[:, half, :, :, :].rearrange("p b a u -> p (b a) u")).then_inc(S["st_q"], 16)
            sp.wait_ge(S["st_q"], 32)
            for b in range(B):
                for half in range(2):
                    row = 3 * U + 3 * half
                    sp.dma_start(LQ[row:row + 3, b, :, :].rearrange("o c q -> o (c q)"),
                                 qrows[half, b].rearrange("a p u -> a (p u)")).then_inc(S["ld_q"], 16)
            sp.wait_ge(S["y_out"], 1)
            for i in range(2):
                sp.dma_start(out[:, i * P:(i + 1) * P, :].rearrange("b p d -> p b d"),
                             Y[:, i:NT:2, :]).then_inc(S["st_out"], 16)
            sp.wait_ge(S["st_out"], 32)

        @block.gpsimd
        def _(pool):
            pool.dma_start(idb[:, :], idb_d).then_inc(S["ld_b"], 16)
            pool.dma_start(rep[:, :], rep_d).then_inc(S["ld_b"], 16)
            pool.dma_start(sel[:, :], sel_d).then_inc(S["ld_b"], 16)
            pool.dma_start(RH[3 * U:3 * U + 6, :, :, :], hot_d).then_inc(S["ld_hot"], 16)
            fills = [(w64[D:128, :], 0.0), (GC[D:128, :], 0.0), (PB[D:128, :, :], 0.0), (TB[D:128, :], 0.0),
                     (ms[D:128, :], 0.0), (TA[D:128, :], 0.0),
                     (TA[D:D + 1, :], 1.0), (TB[D:D + 1, :], 1.0), (ms[D:D + 1, :], 1.0), (hid[D:D + 2, :], 1.0),
                     (ones[:, :], 1.0), (mhalf[:, :], -0.5), (Vall[:, :, :, :], 0.0)]
            for n, (ap, value) in enumerate(fills):
                if n:
                    pool.wait_ge(S["filled"], n)
                nc.gpsimd.memset(ap, value).then_inc(S["filled"], 1)
            pool.wait_ge(S["filled"], FILLS)
            pool.dma_start(w64[D:D + 1, W64["e1"][0]:NW64], e1row).then_inc(S["ld_row"], 16)
            def rsqrt(n, out_, in_, eps):
                pool.wait_ge(S["var"], n)
                nc.gpsimd.tensor_scalar(out_, in_, eps, None, ALU.add).then_inc(S["veps"], 1)
                pool.wait_ge(S["veps"], n)
                half = mhalf[:, 0:out_.shape[1]]
                nc.gpsimd.tensor_tensor(out_, out_, half, ALU.pow).then_inc(S["rstd"], 1)

            rsqrt(1, rstd[:, :], mv[:, :, 1], 1e-5)
            pool.wait_ge(S["z1"], 1)
            nc.gpsimd.tensor_tensor(HZ[:, :, :], H[:, :, :], Z[:, :, :], ALU.add).then_inc(S["hz1"], 1)
            rsqrt(2, rstd[:, :], mv[:, :, 1], 1e-5)
            rsqrt(3, r2[:, :], r2[:, :], 1e-6)
            with pool.Fori(0, PAIRS) as g:
                pool.wait_ge(S["rope_cs"], g + 1)
                nc.gpsimd.tensor_tensor(QT[:, :], rope[:, 0, :], rope[:, 1, :], ALU.add)
                nc.gpsimd.tensor_tensor(KT[:, :], rope[:, 2, :], rope[:, 3, :], ALU.add).then_inc(S["rope"], 1)
            rsqrt(4, r2[:, :], r2[:, :], 1e-6)
            rsqrt(5, rstd[:, :], mv[:, :, 1], 1e-5)
            rsqrt(6, rstd[:, :], mv[:, :, 1], 1e-5)
            rsqrt(7, rstd[:, :], mv[:, :, 1], 1e-5)

        @block.scalar
        def _(act):
            act.dma_start(wpT[:, :, :], wpatch).then_inc(S["ld_tok"], 16)
            act.dma_start(t66[:, :], tok66).then_inc(S["ld_tok"], 16)
            act.dma_start(t3[:, :], tok3).then_inc(S["ld_tok"], 16)
            act.dma_start(w64[0:D, :], w64_d).then_inc(S["ld_w64"], 16)
            act.dma_start(H[NPATCH:P, 0:NT:2, :], txt[:, 0:P - NPATCH, :].rearrange("b p d -> p b d")
                          ).then_inc(S["ld_txt"], 16)
            act.dma_start(H[:, 1:NT:2, :], txt[:, P - NPATCH:TXT, :].rearrange("b p d -> p b d")
                          ).then_inc(S["ld_txt"], 16)
            act.dma_start(b2s[:, :], b2_d).then_inc(S["ld_b2"], 16)
            act.wait_ge(S["hid_mm"], 1)
            nc.scalar.activation(hid[0:D, :], bank(0, D, NPATCH), ACT.Relu).then_inc(S["hid"], 1)
            act.wait_ge(S["gmm"], 1)
            act.wait_ge(S["filled"], FILLS)
            nc.scalar.copy(GC[0:D, 0:D], bank(1, D, D))
            nc.scalar.copy(GC[0:D + 1, D:2 * D], bank(2, D + 1, D))
            nc.scalar.copy(GT[:, :], bank(3, D, D)).then_inc(S["gc_ready"], 1)
            act.wait_ge(S["emb_mm"], 1)
            nc.scalar.copy(embS[:, :], bank(4, D, B * NPATCH)).then_inc(S["emb"], 1)

            def feature_major(dst, done, ready):
                for g in range(PAIRS):
                    act.wait_ge(done, g + 1)
                    nc.scalar.copy(dst[0:D, g * CW:(g + 1) * CW], bank(g, D, CW)).then_inc(ready, 1)

            feature_major(TA, S["zT_mm"], S["zT"])
            for q in range(PAIRS):
                act.wait_ge(S["gv_mm"], q + 1)
                nc.scalar.copy(V[:, 4 * q:4 * q + 4, :], bank(4 + q, P, 4, 2 * D)[:, :, D:2 * D]).then_inc(S["v_sb"], 1)
            act.wait_ge(S["zv_mm"], 1)
            nc.scalar.copy(ZV[:, :], bank(0, D, B * D)).then_inc(S["zv"], 1)
            act.wait_ge(S["p_mm"], 1)
            nc.scalar.copy(PB[0:D, :, :], bank(1, D, B, D)).then_inc(S["p_sb"], 1)
            feature_major(TB, S["xT_mm"], S["xT"])
            act.wait_ge(S["v_mm"], 1)
            nc.scalar.copy(Vall[:, :, :, 0:HD].rearrange("p t k e -> p (t k) e"), bank(4, P, NT * NKV, HD)).then_inc(S["vall"], 1)
            act.wait_ge(S["vall"], 1)

            def exps(g):
                for i in range(2):
                    act.wait_ge(S["nmax"], g * 2 + (i + 1))
                    after(act, "pt_mm", g * 2 + (i - 1))
                    for h in range(NH):
                        nc.scalar.activation(Pex[:, i, h, 0:P], Ssb[:, i, h, 0:P], ACT.Exp,
                                             bias=nmx[:, i, 0, h:h + 1], scale=HD ** -0.5)
                        last = nc.scalar.activation(Pex[:, i, h, P:3 * P], Ssb[:, i, h, P:3 * P], ACT.Exp,
                                                    bias=nmx[:, i, 1, h:h + 1], scale=HD ** -0.5)
                    last.then_inc(S["p_exp"], 1)
                after(act, "y_mm", g * 2)
                nc.scalar.copy(Vb[:, :, :, :].rearrange("p t k e -> p (t k e)"),
                               Vall[:, bass.ds(g * 4, 4), :, :].rearrange("p t k e -> p (t k e)")).then_inc(S["vb"], 1)
                for i in range(2):
                    act.wait_ge(S["pt_mm"], g * 2 + (i + 1))
                    nc.scalar.copy(PT[:, i, :, :], ps[0:P, 4 * i:4 * i + 4, 0:3 * P]).then_inc(S["pt_sb"], 1)

            exps(0)
            with act.Fori(1, PAIRS) as g:
                exps(g)
            feature_major(TA, S["rT_mm"], S["rT"])
            act.wait_ge(S["lg_max"], 1)
            nc.scalar.activation(pr[:, :, :], lg[:, :, :], ACT.Exp).then_inc(S["lg_exp"], 1)
            act.wait_ge(S["wT_mm"], 1)
            nc.scalar.copy(wT[:, :].rearrange("p (a b) -> p a b", a=2),
                           ps[0:3 * NE, 5:7, :].bitcast(BF16)[:, :, 0:TOK // 2]).then_inc(S["wT"], 1)

            def silus(g):
                for m in range(MT):
                    rows = min(128, HALL - 128 * m)
                    act.wait_ge(S["up_mm"], g * MT + (m + 1))
                    after(act, "bw", g * MT + max(m - 1, 0))
                    nc.scalar.activation(silu[0:rows, m % 2, :], ps[0:rows, 3 * (m % 2), 0:CW],
                                         ACT.Silu).then_inc(S["silu"], 1)
                    if m == 1 and not isinstance(g, int):
                        out_ready(g - 1)

            def out_ready(g):
                act.wait_ge(S["dn_mm"], g * MT + MT)
                nc.scalar.copy(ym[:, :], bank(6, 128, N)).then_inc(S["ym"], 1)

            silus(0)
            with act.Fori(1, PAIRS) as g:
                silus(g)
            out_ready(PAIRS - 1)
            feature_major(TB, S["aT_mm"], S["aT"])

            def softmax_exp(b):
                act.wait_ge(S["amax"], b + 1)
                nc.scalar.activation(AL[:, 0, :], AL[:, 0, :], ACT.Exp, bias=ast[:, 0, 1:2], accum_out=ast[:, 0, 2:3])
                nc.scalar.activation(AL[0:64, 1, :], AL[0:64, 1, :], ACT.Exp, bias=ast[0:64, 1, 1:2],
                                     accum_out=ast[0:64, 1, 2:3]).then_inc(S["aexp"], 1)

            def tanhs(b):
                for r in range(RND):
                    act.wait_ge(S["bld_mm"], b * RND + (r + 1))
                    after(act, "al_mm", b * RND + (r - 3))
                    nc.scalar.activation(TH[:, r % 4, :, :], ps[:, 3 * (r % 2):3 * (r % 2) + 3, 0:CW],
                                         ACT.Tanh).then_inc(S["tanh"], 1)
                    if r == 3 and b > 0:
                        softmax_exp(b - 1)

            tanhs(0)
            for b in range(1, B):
                tanhs(b)
            softmax_exp(B - 1)
            feature_major(TA, S["fT_mm"], S["fT"])

            def gelus(g):
                for e in range(NE):
                    act.wait_ge(S["e1_mm"], g * NE + (e + 1))
                    nc.scalar.activation(G1[:, g, e, :], ps[:, e % 4, 0:CW], ACT.Gelu).then_inc(S["gelu"], 1)

            act.wait_ge(S["rl_max"], 1)
            nc.scalar.activation(rt[:, 1, :], rt[:, 0, :], ACT.Exp, accum_out=rs[:, 1:2]).then_inc(S["rl_exp"], 1)
            gelus(0)
            act.wait_ge(S["r2max"], 1)
            nc.scalar.activation(rt[:, 4, :], rt[:, 3, :], ACT.Exp, accum_out=rs[:, 3:4]).then_inc(S["r2exp"], 1)
            gelus(1)
            act.wait_ge(S["e2exp"], 1)
            nc.scalar.activation(rs[:, 11:12], rs[:, 10:11], ACT.Exp).then_inc(S["e2exp"], 1)
            gelus(2)
            act.wait_ge(S["wdT_mm"], 1)
            nc.scalar.copy(wdT[:, :], bank(5, NE, B)).then_inc(S["wdT"], 1)
            act.wait_ge(S["b2w_mm"], 1)
            nc.scalar.copy(b2w[:, :], bank(6, B, D)).then_inc(S["wdT"], 1)
            gelus(3)
            act.wait_ge(S["bB_mm"], 1)
            nc.scalar.copy(bBC[:, :, :], bank(7, P, B, D)).then_inc(S["wbc"], 1)

            for g in range(PAIRS):
                act.wait_ge(S["e2_mm"], g + 1)
                after(act, "o_mm", g - 1)
                nc.scalar.copy(oT[:, g % 2, :], bank(4 + g % 2, 128, N)).then_inc(S["oT"], 1)

        @block.vector
        def _(dve):
            count = [0]

            def link(ins, base=0):
                count[0] += 1
                ins.then_inc(S["dve"], 1)
                dve.wait_ge(S["dve"], base + count[0])

            V_ = nc.vector

            def norm(src, dst, tiles, n, base=0):
                for t in range(tiles):
                    last = V_.bn_stats(stat[:, t, :], src[:, t, :])
                link(last, base)
                for t in range(tiles):
                    last = V_.bn_aggr(mv[:, t, :], stat[:, t, :])
                last.then_inc(S["var"], 1)
                dve.wait_ge(S["var"], n)
                link(V_.tensor_tensor(dst, src, bc(mv[:, 0:tiles, 0], D), ALU.subtract), base)
                dve.wait_ge(S["rstd"], n)

            dve.wait_ge(S["ld_w64"], 16)
            q0, v1 = W64["q"][0], W64["v"][0] + W64["v"][1]
            r0, w31 = W64["rw"][0], W64["w3"][0] + W64["w3"][1]
            V_.tensor_scalar(w64[0:D, q0:v1], w64[0:D, q0:v1], w("ln1")[0:D], None, ALU.mult)
            V_.tensor_scalar(w64[0:D, r0:w31], w64[0:D, r0:w31], w("ln2")[0:D], None, ALU.mult).then_inc(S["lnw_ready"], 1)
            dve.wait_ge(S["ld_b"], 48)
            V_.tensor_copy(LQ[0:3 * U, :, :, :].rearrange("p b c q -> p (b c) q"),
                           rep[:, :].unsqueeze(1).to_broadcast([3 * U, B * NCH, 128])).then_inc(S["rep_ready"], 1)
            dve.wait_ge(S["embT"], 1)
            V_.tensor_copy(H[0:NPATCH, 0:NT:2, :], bank(5, NPATCH, B, D)).then_inc(S["h0"], 1)
            dve.wait_ge(S["h0"], 1)
            dve.wait_ge(S["ld_txt"], 32)
            norm(H[:, :, :], Z[:, :, :], NT, 1)
            V_.tensor_tensor(Z[:, :, :], Z[:, :, :], bc(rstd[:, :], D), ALU.mult).then_inc(S["z1"], 1)
            dve.wait_ge(S["z1"], 1)
            for q in range(PAIRS):
                dve.wait_ge(S["v_sb"], q + 1)
                last = V_.tensor_tensor(Y[:, 4 * q:4 * q + 4, :], bank(4 + q, P, 4, 2 * D)[:, :, 0:D],
                                        Z[:, 4 * q:4 * q + 4, :], ALU.mult)
            link(last)
            link(V_.tensor_reduce(dg[:, :], Y[:, :, :], axis=X, op=ALU.add))
            link(V_.tensor_tensor(Y[:, :, :], V[:, :, :], bc(dg[:, :], D), ALU.mult))
            for q in range(2):
                dve.wait_ge(S["lo_mm"], q + 1)
                last = V_.tensor_tensor(Y[:, 8 * q:8 * q + 8, :], bank(2 + q, P, 8, D), Y[:, 8 * q:8 * q + 8, :],
                                        ALU.subtract)
            link(last)
            dve.wait_ge(S["hz1"], 1)
            V_.scalar_tensor_tensor(H[:, :, :], Y[:, :, :], 1.0 / N, HZ[:, :, :], ALU.mult, ALU.add).then_inc(S["h1"], 1)
            dve.wait_ge(S["h1"], 1)
            norm(H[:, :, :], Z[:, :, :], NT, 2)
            link(V_.tensor_tensor(Z[:, :, :], Z[:, :, :], bc(rstd[:, :], D), ALU.mult))
            link(V_.tensor_tensor(r2[:, :], rstd[:, :], rstd[:, :], ALU.mult))
            V_.tensor_tensor(r2[:, :], r2[:, :], mv[:, :, 1], ALU.mult).then_inc(S["var"], 1)
            dve.wait_ge(S["rstd"], 3)
            V_.tensor_tensor(XN[:, :, :], Z[:, :, :], bc(r2[:, :], D), ALU.mult).then_inc(S["xn"], 1)
            def rotate(g):
                dve.wait_ge(S["qk_mm"], g * 4 + 4)
                after(dve, "rope", g)
                for j in range(4):
                    tab = c("cos") if j % 2 == 0 else c("sin")
                    last = V_.tensor_tensor(rope[:, j, :].rearrange("p (i n) -> p i n", i=2),
                                            ps[:, j, 0:CW].rearrange("p (i n) -> p i n", i=2),
                                            tab.unsqueeze(1).to_broadcast([128, 2, N]), ALU.mult)
                last.then_inc(S["rope_cs"], 1)

            b0 = count[0]
            CHB = 6

            def attend(g, more):
                count[0] = b0
                base = g * CHB
                for i in range(2):
                    dve.wait_ge(S["s_mm"], g * 2 + (i + 1))
                    link(V_.tensor_tensor(Ssb[:, i, :, :], ps[0:P, 4 * i:4 * i + 4, 0:3 * P],
                                          c("mask")[0:P].unsqueeze(1).to_broadcast([P, NH, 3 * P]), ALU.add), base)
                    V_.tensor_reduce(nmx[:, i, 0, :], Ssb[:, i, :, 0:P], axis=X, op=ALU.max).then_inc(S["s_sb"], 1)
                    link(V_.tensor_reduce(nmx[:, i, 1, :], Ssb[:, i, :, P:3 * P], axis=X, op=ALU.max), base)
                    V_.tensor_scalar(nmx[:, i, :, :], nmx[:, i, :, :], -(HD ** -0.5), None, ALU.mult).then_inc(S["nmax"], 1)
                if more:
                    rotate(g + 1)
                for i in range(2):
                    dve.wait_ge(S["y_mm"], g * 2 + (i + 1))
                    link(V_.reciprocal(yT[:, i * N:(i + 1) * N], ps[:, 4 * i + 1, 0:N]), base)
                    V_.tensor_tensor(yT[:, i * N:(i + 1) * N], ps[:, 4 * i, 0:N], yT[:, i * N:(i + 1) * N],
                                     ALU.mult).then_inc(S["y_sb"], 1)
                dve.wait_ge(S["pr_mm"], g + 1)
                V_.tensor_tensor(Y[:, bass.ds(g * 4, 4), :], bank(2, P, 4, D), Z[:, bass.ds(g * 4, 4), :],
                                 ALU.add).then_inc(S["x2"], 1)
                assert count[0] - b0 == CHB

            rotate(0)
            attend(0, True)
            with dve.Fori(1, PAIRS - 1) as g:
                attend(g, True)
            attend(PAIRS - 1, False)
            count[0] = b0 + PAIRS * CHB
            dve.wait_ge(S["x2"], PAIRS)
            link(V_.tensor_tensor(XN[:, :, :], Y[:, :, :], Y[:, :, :], ALU.mult))
            link(V_.tensor_reduce(r2[:, :], XN[:, :, :], axis=X, op=ALU.add))
            V_.tensor_scalar(r2[:, :], r2[:, :], 1.0 / D, None, ALU.mult).then_inc(S["var"], 1)
            dve.wait_ge(S["rstd"], 4)
            V_.tensor_tensor(XN[:, :, :], Y[:, :, :], bc(r2[:, :], D), ALU.mult).then_inc(S["xr"], 1)
            link(V_.tensor_tensor(H[:, :, :], H[:, :, :], Y[:, :, :], ALU.add))
            dve.wait_ge(S["lg_mm"], 1)
            link(V_.tensor_reduce(sm[:, 0, :], bank(4, P, NT, NE), axis=X, op=ALU.max))
            V_.tensor_tensor(lg[:, :, :], bank(4, P, NT, NE), bc(sm[:, 0, :], NE), ALU.subtract).then_inc(S["lg_max"], 1)
            dve.wait_ge(S["lg_exp"], 1)
            link(V_.tensor_reduce(sm[:, 1, :], pr[:, :, :], axis=X, op=ALU.add))
            link(V_.reciprocal(sm[:, 1, :], sm[:, 1, :]))
            link(V_.tensor_tensor(pr[:, :, :], pr[:, :, :], bc(sm[:, 1, :], NE), ALU.mult))
            rank = c("rank")[0:P].unsqueeze(1).to_broadcast([P, NT, NE])

            def first_max(src, dst, s):
                link(V_.tensor_reduce(s, src, axis=X, op=ALU.max))
                link(V_.tensor_tensor(dst, src, bc(s, NE), ALU.is_equal))
                link(V_.tensor_tensor(dst, dst, rank, ALU.mult))
                link(V_.tensor_reduce(s, dst, axis=X, op=ALU.max))
                link(V_.tensor_tensor(dst, dst, bc(s, NE), ALU.is_equal))

            first_max(pr[:, :, :], oh[:, 0, :, :], sm[:, 2, :])
            link(V_.scalar_tensor_tensor(oh[:, 1, :, :], oh[:, 0, :, :], -2.0, pr[:, :, :], ALU.mult, ALU.add))
            first_max(oh[:, 1, :, :], oh[:, 2, :, :], sm[:, 3, :])
            link(V_.tensor_tensor(oh[:, 0, :, :], oh[:, 0, :, :], oh[:, 2, :, :], ALU.add))
            link(V_.tensor_tensor(pr[:, :, :], pr[:, :, :], oh[:, 0, :, :], ALU.mult))
            link(V_.tensor_reduce(sm[:, 0, :], pr[:, :, :], axis=X, op=ALU.add))
            link(V_.tensor_scalar(sm[:, 0, :], sm[:, 0, :], 1e-9, None, ALU.add))
            link(V_.reciprocal(sm[:, 0, :], sm[:, 0, :]))
            link(V_.tensor_tensor(pr[:, :, :], pr[:, :, :], bc(sm[:, 0, :], NE), ALU.mult))

            def split3(src, hi, mid, lo, rest):
                link(V_.tensor_copy(hi, src))
                link(V_.tensor_tensor(rest, src, hi, ALU.subtract))
                link(V_.tensor_copy(mid, rest))
                return V_.tensor_tensor(lo, rest, mid, ALU.subtract)

            split3(pr[:, :, :], wp3[:, :, 0, :], wp3[:, :, 1, :], wp3[:, :, 2, :], lg[:, :, :]).then_inc(S["wp3"], 1)
            def add_mixture(g):
                dve.wait_ge(S["ymT_mm"], g + 1)
                V_.tensor_tensor(H[:, bass.ds(g * 4, 4), :].rearrange("p (i h) d -> p i h d", i=2),
                                 H[:, bass.ds(g * 4, 4), :].rearrange("p (i h) d -> p i h d", i=2),
                                 bank(7, P, 2, 2, D).rearrange("p h i d -> p i h d"), ALU.add).then_inc(S["h2"], 1)

            def gated(g):
                for m in range(MT):
                    rows = min(128, HALL - 128 * m)
                    bk = 3 * (m % 2)
                    dve.wait_ge(S["silu"], g * MT + (m + 1))
                    V_.tensor_tensor(bw[0:rows, m % 2, :], silu[0:rows, m % 2, :], ps[0:rows, bk + 1, 0:CW],
                                     ALU.mult).then_inc(S["bw"], 1)
                    dve.wait_ge(S["bw"], g * MT + (m + 1))
                    after(dve, "dn_mm", g * MT + max(m - 1, 0))
                    V_.tensor_tensor(hh[0:rows, m % 2, :], bw[0:rows, m % 2, :], ps[0:rows, bk + 2, 0:CW],
                                     ALU.mult).then_inc(S["hh"], 1)
                    if m == 5 and not isinstance(g, int):
                        add_mixture(g - 1)

            gated(0)
            with dve.Fori(1, PAIRS) as g:
                gated(g)
            add_mixture(PAIRS - 1)
            dve.wait_ge(S["h2"], PAIRS)
            norm(H[:, :, :], Z[:, :, :], NT, 5)
            V_.tensor_tensor(Z[:, :, :], Z[:, :, :], bc(rstd[:, :], D), ALU.mult).then_inc(S["z3"], 1)
            dve.wait_ge(S["q_mm"], 1)
            qv = qp[:, :, :, :, :].rearrange("p h b a u -> p b h a u")
            split3(bank(4, P, B, 2, U), qv[:, :, :, 0, :], qv[:, :, :, 1, :], qv[:, :, :, 2, :],
                   qr[:, :, :].rearrange("p (b h) u -> p b h u", h=2)).then_inc(S["qp"], 1)
            for g in range(PAIRS):
                dve.wait_ge(S["k_mm"], g + 1)
                last = V_.tensor_scalar(kb[:, g * CW:(g + 1) * CW], bank(g, 3 * U, CW), c("bh")[0:3 * U], None, ALU.add)
            link(last)
            link(V_.tensor_copy(khi[:, :], kb[:, :]))
            RHv = RH[:, :, :, :]

            def twice(ap, p):
                return ap.rearrange("p (b n) -> p b n", b=B).unsqueeze(2).to_broadcast([p, B, 2, N])

            def rows2(dst, src, sub=None):
                for s in range(2):
                    o = dst[:, :, s, :]
                    if sub is None:
                        last = V_.tensor_copy(o, src.rearrange("p (b n) -> p b n", b=B))
                    else:
                        last = V_.tensor_tensor(o, src.rearrange("p (b n) -> p b n", b=B),
                                                sub.rearrange("p (b n) -> p b n", b=B), ALU.subtract)
                return last

            rows2(RHv[0:U], khi[0:U, :])
            for p0, p1 in ((U, 2 * U), (2 * U, 3 * U)):
                last = V_.tensor_tensor(kb[p0:p1, :], kb[p0:p1, :], khi[p0:p1, :], ALU.subtract)
            link(last)
            for p0, p1 in ((U, 2 * U), (2 * U, 3 * U)):
                last = V_.tensor_copy(khi[p0:p1, :], kb[p0:p1, :])
            link(last)
            rows2(RHv[U:2 * U], khi[U:2 * U, :])
            rows2(RHv[2 * U:3 * U], kb[2 * U:3 * U, :], khi[2 * U:3 * U, :]).then_inc(S["kp"], 1)
            b1 = count[0]
            CHD = 2

            def softmax(b):
                count[0] = b1
                base = b * CHD
                dve.wait_ge(S["al_mm"], b * RND + RND)
                V_.tensor_scalar(AL[:, 0, :], ps[:, 6, 0:N], c("ba"), None, ALU.add)
                V_.tensor_scalar(AL[0:64, 1, :], ps[0:64, 6, N:2 * N], c("ba")[0:64], None, ALU.add).then_inc(S["al_sb"], 1)
                dve.wait_ge(S["al_sb"], b + 1)
                V_.tensor_reduce(ast[:, 0, 0:1], AL[:, 0, :], axis=X, op=ALU.max)
                link(V_.tensor_reduce(ast[0:64, 1, 0:1], AL[0:64, 1, :], axis=X, op=ALU.max), base)
                V_.tensor_scalar(ast[:, 0, 1:2], ast[:, 0, 0:1], -1.0, None, ALU.mult)
                V_.tensor_scalar(ast[0:64, 1, 1:2], ast[0:64, 1, 0:1], -1.0, None, ALU.mult).then_inc(S["amax"], 1)
                dve.wait_ge(S["aexp"], b + 1)
                V_.reciprocal(ast[:, 0, 3:4], ast[:, 0, 2:3])
                link(V_.reciprocal(ast[0:64, 1, 3:4], ast[0:64, 1, 2:3]), base)
                V_.tensor_scalar(AL[:, 0, :], AL[:, 0, :], ast[:, 0, 3:4], None, ALU.mult)
                V_.tensor_scalar(AL[0:64, 1, :], AL[0:64, 1, :], ast[0:64, 1, 3:4], None, ALU.mult).then_inc(S["pn"], 1)
                dve.wait_ge(S["pt2_mm"], b + 1)
                V_.tensor_copy(PT2[:, :, :], bank(7, P, 2, N)).then_inc(S["pt2"], 1)
                dve.wait_ge(S["c_mm"], b + 1)
                V_.tensor_tensor(H[:, bass.ds(b * 2, 2), :], bank(7, P, 2, D), H[:, bass.ds(b * 2, 2), :],
                                 ALU.add).then_inc(S["h3"], 1)
                assert count[0] - b1 == CHD

            softmax(0)
            for b in range(1, B):
                softmax(b)
            count[0] = b1 + B * CHD
            dve.wait_ge(S["h3"], B)
            norm(H[:, :, :], Z[:, :, :], NT, 6)
            V_.tensor_tensor(Z[:, :, :], Z[:, :, :], bc(rstd[:, :], D), ALU.mult).then_inc(S["z4"], 1)
            dve.wait_ge(S["fT"], PAIRS)
            link(V_.tensor_reduce(ms[0:D, :], TA[0:D, :].rearrange("p (b n) -> p b n", b=B), axis=X, op=ALU.add))
            V_.tensor_scalar(ms[0:D, :], ms[0:D, :], 1.0 / N, None, ALU.mult).then_inc(S["msum"], 1)
            dve.wait_ge(S["rl_mm"], 1)
            link(V_.tensor_reduce(rs[:, 0:1], bank(4, B, NE), axis=X, op=ALU.max))
            V_.tensor_scalar(rt[:, 0, :], bank(4, B, NE), rs[:, 0:1], None, ALU.subtract).then_inc(S["rl_max"], 1)
            dve.wait_ge(S["rl_exp"], 1)
            link(V_.reciprocal(rs[:, 1:2], rs[:, 1:2]))
            V_.tensor_scalar(rt[:, 2, :], rt[:, 1, :], rs[:, 1:2], None, ALU.mult).then_inc(S["wd"], 1)
            dve.wait_ge(S["ld_mm"], 1)
            link(V_.tensor_scalar(rt[:, 5, :], bank(5, B, NE), float(N), None, ALU.mult))
            link(V_.reciprocal(rt[:, 5, :], rt[:, 5, :]))
            link(V_.tensor_scalar(rt[:, 5, :], rt[:, 5, :], CAP, 1.0, ALU.mult, ALU.min))
            link(V_.tensor_tensor(rt[:, 2, :], rt[:, 2, :], rt[:, 5, :], ALU.mult))
            link(V_.tensor_reduce(rs[:, 2:3], rt[:, 2, :], axis=X, op=ALU.max))
            V_.tensor_scalar(rt[:, 3, :], rt[:, 2, :], rs[:, 2:3], None, ALU.subtract).then_inc(S["r2max"], 1)
            dve.wait_ge(S["r2exp"], 1)
            link(V_.reciprocal(rs[:, 3:4], rs[:, 3:4]))
            link(V_.tensor_scalar(rt[:, 7, :], rt[:, 4, :], rs[:, 3:4], None, ALU.mult))

            def first_max8(src, dst, s):
                link(V_.tensor_reduce(s, src, axis=X, op=ALU.max))
                link(V_.tensor_scalar(dst, src, s, None, ALU.is_equal))
                link(V_.tensor_tensor(dst, dst, c("rank")[0:B], ALU.mult))
                link(V_.tensor_reduce(rs[:, 4:5], dst, axis=X, op=ALU.max))
                link(V_.tensor_scalar(dst, dst, rs[:, 4:5], None, ALU.is_equal))

            first_max8(rt[:, 7, :], rt[:, 8, :], rs[:, 5:6])
            link(V_.scalar_tensor_tensor(rt[:, 9, :], rt[:, 8, :], -2.0, rt[:, 7, :], ALU.mult, ALU.add))
            first_max8(rt[:, 9, :], rt[:, 10, :], rs[:, 6:7])
            V_.tensor_tensor(rs[:, 10:11], rs[:, 6:7], rs[:, 5:6], ALU.subtract).then_inc(S["e2exp"], 1)
            dve.wait_ge(S["e2exp"], 2)
            link(V_.tensor_scalar(rs[:, 12:13], rs[:, 11:12], 1.0, None, ALU.add))
            link(V_.scalar_tensor_tensor(rt[:, 11, :], rt[:, 10, :], rs[:, 11:12], rt[:, 8, :], ALU.mult, ALU.add))
            link(V_.reciprocal(rs[:, 12:13], rs[:, 12:13]))
            V_.tensor_scalar(rt[:, 12, :], rt[:, 11, :], rs[:, 12:13], None, ALU.mult).then_inc(S["wd"], 1)
            dve.wait_ge(S["wd"], 2)
            eye = ident[0:B, 0:B]
            V_.tensor_tensor(dgw[:, 0:B * NE].rearrange("p (b e) -> p b e", b=B),
                             rt[:, 12, :].unsqueeze(1).to_broadcast([B, B, NE]), bc(eye, NE), ALU.mult)
            dve.wait_ge(S["wdT"], 2)
            V_.tensor_tensor(dgw[:, B * NE:].rearrange("p (b e) -> p b e", b=B),
                             b2w[:, :].unsqueeze(1).to_broadcast([B, B, D]), bc(eye, D), ALU.mult).then_inc(S["dg"], 1)
            dve.wait_ge(S["wB_mm"], 1)
            V_.tensor_copy(wBC[:, :, :], bank(6, 128, B, NE)).then_inc(S["wbc"], 1)
            dve.wait_ge(S["wbc"], 2)
            for i in range(B):
                V_.tensor_tensor(W2S[:, i, :, :], c("e2").rearrange("p (e d) -> p e d", e=NE),
                                 bc(wBC[:, i, :], D), ALU.mult).then_inc(S["w2s"], 1)
                if i == 1:
                    V_.tensor_tensor(Z[:, :, :].rearrange("p (b h) d -> p b h d", h=2),
                                     Z[:, :, :].rearrange("p (b h) d -> p b h d", h=2),
                                     bBC.unsqueeze(2).to_broadcast([P, B, 2, D]), ALU.add).then_inc(S["zb"], 1)
            dve.wait_ge(S["zb"], 1)
            for g in range(PAIRS):
                dve.wait_ge(S["o_mm"], g + 1)
                V_.tensor_tensor(Y[:, 4 * g:4 * g + 4, :].rearrange("p (i h) d -> p i h d", i=2),
                                 Z[:, 4 * g:4 * g + 4, :].rearrange("p (i h) d -> p i h d", i=2),
                                 bank(6 + g % 2, P, 2, 2, D).rearrange("p h i d -> p i h d"), ALU.add).then_inc(S["fo"], 1)
            dve.wait_ge(S["fo"], PAIRS)
            norm(Y[:, :, :], Y[:, :, :], NT, 7)
            link(V_.tensor_tensor(Y[:, :, :], Y[:, :, :], bc(rstd[:, :], D), ALU.mult))
            link(V_.tensor_tensor(Y[:, :, :], Y[:, :, :], c("gamma")[0:P].unsqueeze(1).to_broadcast([P, NT, D]),
                                  ALU.mult))
            link(V_.tensor_tensor(Y[:, :, :], Y[:, :, :], c("beta")[0:P].unsqueeze(1).to_broadcast([P, NT, D]),
                                  ALU.add))
            V_.tensor_tensor(Y[:, :, :], Y[:, :, :], H[:, :, :], ALU.add).then_inc(S["y_out"], 1)

        @block.tensor
        def _(pe):
            pe.wait_ge(S["ld_tok"], 48)
            mm(bank(0, D, NPATCH), t3[:, 0:D], t3[:, D:]).then_inc(S["hid_mm"], 1)
            pe.wait_ge(S["ld_w64"], 16)
            mm(bank(1, D, D), w("Wa")[0:D], w("Wb")[0:D])
            mm(bank(2, D + 1, D), w("Wu")[0:D], w("WrT")[0:D])
            mm(bank(3, D, D), w("Wb")[0:D], w("Wa")[0:D]).then_inc(S["gmm"], 1)
            for k in range(KC):
                pe.wait_ge(S["ld_x"], 16 * KC) if k == 0 else None
                mm(bank(4, D, B * NPATCH), wpT[:, k, :], xP[:, k, :], start=(k == 0), stop=False)
            pe.wait_ge(S["hid"], 1)
            pe.wait_ge(S["filled"], FILLS)
            mm(bank(4, D, B, NPATCH), t66[:, :], hid[:, :].unsqueeze(1).to_broadcast([D + 2, B, NPATCH]),
               start=False, stop=True).then_inc(S["emb_mm"], 1)
            pe.wait_ge(S["emb"], 1)
            pe.wait_ge(S["ld_c"], 16)
            for b in range(B):
                last = nc.tensor.transpose(bank(5, NPATCH, B, D)[:, b, :], embS[:, b * NPATCH:(b + 1) * NPATCH],
                                           ident[0:D, 0:D])
            last.then_inc(S["embT"], 1)

            def transposes(src, done):
                for g in range(PAIRS):
                    for t in range(4):
                        last = nc.tensor.transpose(bank(g, D, 4, P)[:, t, :], src[:, 4 * g + t, :], ident[0:P, 0:P])
                    last.then_inc(done, 1)

            pe.wait_ge(S["z1"], 1)
            pe.wait_ge(S["gc_ready"], 1)
            transposes(Z, S["zT_mm"])
            for q in range(PAIRS):
                pe.wait_ge(S["zT"], q + 1)
                if q == 1:
                    pe.wait_ge(S["h0"], 1)
                for t in range(4):
                    a = (4 * q + t) * P
                    last = mm(bank(4 + q, P, 4, 2 * D)[:, t, :], TA[:, a:a + P], GC[:, :])
                last.then_inc(S["gv_mm"], 1)
            pe.wait_ge(S["v_sb"], PAIRS)
            for b in range(B):
                for t in (2 * b, 2 * b + 1):
                    last = mm(bank(0, D, B, D)[:, b, :], Z[:, t, :], V[:, t, :], start=(t % 2 == 0), stop=(t % 2 == 1))
            last.then_inc(S["zv_mm"], 1)
            pe.wait_ge(S["zv"], 1)
            mm(bank(1, D, B * D), GT[:, :], ZV[:, :]).then_inc(S["p_mm"], 1)
            pe.wait_ge(S["p_sb"], 1)
            for q in range(2):
                for t in range(8):
                    a = (8 * q + t) * P
                    last = mm(bank(2 + q, P, 8, D)[:, t, :], TA[:, a:a + P], PB[:, (8 * q + t) // 2, :])
                last.then_inc(S["lo_mm"], 1)
            pe.wait_ge(S["xn"], 1)
            pe.wait_ge(S["lnw_ready"], 1)
            transposes(XN, S["xT_mm"])
            pe.wait_ge(S["xT"], PAIRS)
            for t in range(NT):
                last = mm(bank(4, P, NT, NKV * HD)[:, t, :], TB[:, t * P:(t + 1) * P], w("v"))
            last.then_inc(S["v_mm"], 1)
            pe.wait_ge(S["vall"], 1)

            def project_qk(g):
                for j, name in enumerate(("q", "qs", "k", "ks")):
                    mm(ps[:, j, 0:CW], w(name), TB[:, bass.ds(g * CW, CW)]).then_inc(S["qk_mm"], 1)

            def attend(g, more):
                pe.wait_ge(S["rope"], g + 1)
                after(pe, "x2", g)
                for i in range(2):
                    for h in range(NH):
                        r = slice(32 * h, 32 * h + 32)
                        for t in range(2):
                            a = i * N + t * P
                            last = mm(ps[0:P, 4 * i + h, t * P:t * P + (t + 1) * P], QT[r, a:a + P],
                                      KT[r, i * N:i * N + (t + 1) * P])
                    last.then_inc(S["s_mm"], 1)
                if more:
                    pe.wait_ge(S["s_sb"], g * 2 + 1)
                    project_qk(g + 1)
                    pe.wait_ge(S["rope_cs"], g + 2)
                for i in range(2):
                    pe.wait_ge(S["p_exp"], g * 2 + (i + 1))
                    for h in range(NH):
                        for at in (0, P, 2 * P):
                            last = nc.tensor.transpose(ps[0:P, 4 * i + h, at:at + P],
                                                       Pex[:, i, h, at:at + P], ident[0:P, 0:P])
                    last.then_inc(S["pt_mm"], 1)
                pe.wait_ge(S["vb"], g + 1)
                for i in range(2):
                    pe.wait_ge(S["pt_sb"], g * 2 + (i + 1))
                    for k in range(2):
                        for t in range(2):
                            for h in range(NH):
                                lhs = ones[0:P, 0:32] if k else Vb[:, 2 * i + t, h // 2, :]
                                last = mm(ps[32 * h:32 * h + 32, 4 * i + k, t * P:N], lhs,
                                          PT[:, i, h, 2 * P * t:2 * P + P * t], start=(t == 0), stop=(t == 1),
                                          skip_group_check=True)
                    last.then_inc(S["y_mm"], 1)
                for i in range(2):
                    pe.wait_ge(S["y_sb"], g * 2 + (i + 1))
                    for t in range(2):
                        a = i * N + t * P
                        last = mm(bank(2, P, 4, D)[:, 2 * i + t, :], yT[:, a:a + P], c("wo"))
                last.then_inc(S["pr_mm"], 1)

            project_qk(0)
            attend(0, True)
            with pe.Fori(1, PAIRS - 1) as g:
                attend(g, True)
            attend(PAIRS - 1, False)
            pe.wait_ge(S["xr"], 1)
            transposes(XN, S["rT_mm"])
            pe.wait_ge(S["rT"], PAIRS)
            for t in range(NT):
                last = mm(bank(4, P, NT, NE)[:, t, :], TA[:, t * P:(t + 1) * P], w("rw"))
            last.then_inc(S["lg_mm"], 1)
            pe.wait_ge(S["wp3"], 1)
            pe.wait_ge(S["ld_b"], 48)
            for t in range(NT):
                dst = ps[0:3 * NE, 5 + t // 8, :].bitcast(BF16)[:, (t % 8) * P:(t % 8 + 1) * P]
                last = nc.tensor.transpose(dst, wp3[:, t, :, :].rearrange("p a e -> p (a e)"), idb[0:P, 0:P])
            last.then_inc(S["wT_mm"], 1)
            pe.wait_ge(S["wT"], 1)
            def up(g, m):
                rows = min(128, HALL - 128 * m)
                bk = 3 * (m % 2)
                before = g * MT + max(m - 1, 0)
                rhs = TA[:, bass.ds(g * CW, CW)]
                after(pe, "silu", before)
                mm(ps[0:rows, bk, 0:CW], w("w1", 128 * m, 128 * m + rows), rhs)
                after(pe, "bw", before)
                mm(ps[0:rows, bk + 1, 0:CW], w("w3", 128 * m, 128 * m + rows), rhs)

            def spread_weights(g, m):
                rows = min(128, HALL - 128 * m)
                mm(ps[0:rows, 3 * (m % 2) + 2, 0:CW], sel[:, 128 * m:128 * m + rows],
                   wT[:, bass.ds(g * CW, CW)]).then_inc(S["up_mm"], 1)

            def down(g, m):
                rows = min(128, HALL - 128 * m)
                pe.wait_ge(S["hh"], g * MT + (m + 1))
                if m == 0:
                    after(pe, "ym", g)
                w2 = c("w2").rearrange("p (m d) -> p m d", m=MT)[0:rows, m, :]
                for i in range(2):
                    last = mm(ps[64 * i:64 * i + 64, 6, 0:N], w2, hh[0:rows, m % 2, i * N:(i + 1) * N],
                              start=(m == 0), stop=(m == MT - 1), skip_group_check=True)
                last.then_inc(S["dn_mm"], 1)

            def to_tokens(g):
                pe.wait_ge(S["ym"], g + 1)
                for t in range(2):
                    last = nc.tensor.transpose(bank(7, P, 2, 2 * D)[:, t, :], ym[:, t * P:(t + 1) * P], ident)
                last.then_inc(S["ymT_mm"], 1)

            def mixture(g):
                later = not isinstance(g, int)
                if later:
                    down(g - 1, MT - 2)
                for m in range(MT):
                    up(g, m)
                    if m >= 2:
                        down(g, m - 2)
                    elif m == 0 and later:
                        down(g - 1, MT - 1)
                    spread_weights(g, m)
                    if m == 4 and not isinstance(g, int):
                        to_tokens(g - 1)

            mixture(0)
            with pe.Fori(1, PAIRS) as g:
                mixture(g)
            down(PAIRS - 1, MT - 2)
            down(PAIRS - 1, MT - 1)
            to_tokens(PAIRS - 1)
            pe.wait_ge(S["z3"], 1)
            transposes(Z, S["aT_mm"])
            pe.wait_ge(S["aT"], PAIRS)
            for t in range(NT):
                last = mm(bank(4, P, NT, U)[:, t, :], TB[:, t * P:(t + 1) * P], w("wt"))
            last.then_inc(S["q_mm"], 1)
            for g in range(PAIRS):
                mm(bank(g, 3 * U, CW), w("wx"), TB[:, g * CW:(g + 1) * CW]).then_inc(S["k_mm"], 1)
            pe.wait_ge(S["kp"], 1)
            pe.wait_ge(S["ld_hot"], 16)
            pe.wait_ge(S["rep_ready"], 1)
            pe.wait_ge(S["ld_q"], 16 * 2 * B)
            was = c("was").rearrange("p (r u) -> p r u", r=RND)

            def build(b, r):
                after(pe, "tanh", b * RND + (r - 1))
                for j in range(3):
                    last = mm(ps[:, 3 * (r % 2) + j, 0:CW],
                              LQ[:, bass.ds(b, 1), RND * j + r, :].rearrange("p o q -> p (o q)"),
                              RH[:, bass.ds(b, 1), :, :].rearrange("p o s n -> p (o s n)"))
                last.then_inc(S["bld_mm"], 1)

            def contract(b, r):
                pe.wait_ge(S["tanh"], b * RND + (r + 1))
                if r == 0:
                    after(pe, "al_sb", b)
                for j in range(3):
                    for s in range(2):
                        n = j + 3 * s
                        last = mm(ps[32 * (n % 4):32 * (n % 4) + 32, 6, N * (n // 4):N * (n // 4) + N], was[:, r, :],
                                  TH[:, r % 4, j, s * N:(s + 1) * N], start=(r == 0 and n < 4), stop=(r == RND - 1),
                                  skip_group_check=True)
                last.then_inc(S["al_mm"], 1)

            def keys_first(b):
                pe.wait_ge(S["pn"], b + 1)
                for t in range(2):
                    nc.tensor.transpose(bank(7, P, 2, N)[:, t, 0:128], AL[:, 0, t * P:(t + 1) * P], ident)
                    last = nc.tensor.transpose(bank(7, P, 2, N)[:, t, 128:N], AL[0:64, 1, t * P:(t + 1) * P],
                                               ident[0:64, 0:64])
                last.then_inc(S["pt2_mm"], 1)

            def values(b):
                pe.wait_ge(S["pt2"], b + 1)
                for q in range(2):
                    for t in range(2):
                        last = mm(bank(7, P, 2, D)[:, q, :], PT2[:, t, q * P:(q + 1) * P],
                                  Z[:, bass.ds(b * 2 + t, 1), :].rearrange("p o d -> p (o d)"),
                                  start=(t == 0), stop=(t == 1))
                last.then_inc(S["c_mm"], 1)

            def image(b):
                later = b > 0
                for r in range(RND):
                    build(b, r)
                    if r >= 2:
                        contract(b, r - 2)
                    elif later:
                        contract(b - 1, RND - 2 + r)
                    if later and r == 6:
                        keys_first(b - 1)
                    if later and r == 7:
                        values(b - 1)

            image(0)
            for b in range(1, B):
                image(b)
            contract(B - 1, RND - 2)
            contract(B - 1, RND - 1)
            keys_first(B - 1)
            values(B - 1)
            pe.wait_ge(S["z4"], 1)
            transposes(Z, S["fT_mm"])

            def hidden(g):
                for e in range(NE):
                    after(pe, "gelu", g * NE + (e - 3))
                    mm(ps[:, e % 4, 0:CW], w("e1", e * FE, (e + 1) * FE), TA[:, g * CW:(g + 1) * CW]
                       ).then_inc(S["e1_mm"], 1)

            pe.wait_ge(S["ld_row"], 16)
            pe.wait_ge(S["msum"], 1)
            mm(bank(4, B, NE), ms[:, :], w("wr")).then_inc(S["rl_mm"], 1)
            hidden(0)
            pe.wait_ge(S["wd"], 1)
            mm(bank(5, B, NE), ones[0:B, 0:B], rt[:, 2, :]).then_inc(S["ld_mm"], 1)
            hidden(1)
            hidden(2)
            pe.wait_ge(S["wd"], 2)
            nc.tensor.transpose(bank(5, NE, B), rt[:, 12, :], ident[0:B, 0:B]).then_inc(S["wdT_mm"], 1)
            pe.wait_ge(S["wdT"], 1)
            pe.wait_ge(S["ld_b2"], 16)
            mm(bank(6, B, D), wdT[:, :], b2s[:, :]).then_inc(S["b2w_mm"], 1)
            hidden(3)
            pe.wait_ge(S["dg"], 1)
            mm(bank(6, 128, B * NE), ones[0:B, :], dgw[:, 0:B * NE]).then_inc(S["wB_mm"], 1)
            mm(bank(7, P, B * D), ones[0:B, 0:P], dgw[:, B * NE:]).then_inc(S["bB_mm"], 1)
            pe.wait_ge(S["wbc"], 2)

            def mix(g):
                after(pe, "oT", g - 1)
                for i in range(2):
                    pe.wait_ge(S["w2s"], g * 2 + i + 1)
                    for e in range(NE):
                        last = mm(ps[64 * i:64 * i + 64, 4 + g % 2, 0:N], W2S[:, 2 * g + i, e, :],
                                  G1[:, g, e, i * N:(i + 1) * N],
                                  start=(e == 0), stop=(e == NE - 1), skip_group_check=True)
                last.then_inc(S["e2_mm"], 1)

            def mixed_to_tokens(g):
                pe.wait_ge(S["oT"], g + 1)
                after(pe, "fo", g - 1)
                for t in range(2):
                    last = nc.tensor.transpose(bank(6 + g % 2, P, 2, 2 * D)[:, t, :], oT[:, g % 2, t * P:(t + 1) * P],
                                               ident)
                last.then_inc(S["o_mm"], 1)

            pe.wait_ge(S["gelu"], PAIRS * NE)
            for g in range(PAIRS):
                mix(g)
                if g:
                    mixed_to_tokens(g - 1)
            mixed_to_tokens(PAIRS - 1)



_ARGS = ("patches", "wpatch", "txt", "w64", "e1row", "tok66", "tok3", "c128", "b2", "idb", "sel", "rep", "hot")


def _layout(x, txt, L0_tok_Wp, L0_tok_bp, L0_tok_W1, L0_tok_b1, L0_tok_W2, L0_tok_b2, L0_attn_W_alpha,
            L0_attn_W_beta, L0_attn_W_unary, L0_attn_b_unary, L0_attn_W_r, L0_ffn_ln1_w, L0_ffn_ln2_w, L0_ffn_wq,
            L0_ffn_wk, L0_ffn_wv, L0_ffn_wo, L0_ffn_router_w, L0_ffn_w1, L0_ffn_w2, L0_ffn_w3, L1_attn_Wt,
            L1_attn_Wx, L1_attn_bh, L1_attn_Wa, L1_attn_ba, L1_ffn_Wr, L1_ffn_br, L1_ffn_W1, L1_ffn_b1,
            L1_ffn_W2, L1_ffn_b2, L1_ffn_gamma, L1_ffn_beta):
    f = np.float32
    a = np.asarray

    def zeros(*s):
        return np.zeros(s, f)

    xp = a(x).reshape(B, CH, NPS, PS, NPS, PS).transpose(1, 3, 5, 0, 2, 4).reshape(KC, 128, B * NPATCH)
    d = {"patches": xp.transpose(1, 0, 2), "wpatch": a(L0_tok_Wp).reshape(KC, 128, D).transpose(1, 0, 2),
         "txt": a(txt)}
    wq, wk = a(L0_ffn_wq), a(L0_ffn_wk)

    def heads(wt, per, swap):
        o = zeros(D, 128)
        for h in range(NH):
            rows = wt[(h // per) * HD:(h // per + 1) * HD]
            if swap:
                rows = np.concatenate([rows[HD // 2:], rows[:HD // 2]])
            o[:, 32 * h:32 * h + HD] = rows.T
        return o

    cols = {"Wa": a(L0_attn_W_alpha), "Wb": a(L0_attn_W_beta),
            "Wu": np.concatenate([a(L0_attn_W_unary), a(L0_attn_b_unary)[:, None]], 1), "WrT": a(L0_attn_W_r).T,
            "ln1": a(L0_ffn_ln1_w)[:, None], "ln2": a(L0_ffn_ln2_w)[:, None],
            "q": heads(wq, 1, False), "qs": heads(wq, 1, True), "k": heads(wk, NH // NKV, False),
            "ks": heads(wk, NH // NKV, True), "v": a(L0_ffn_wv).T, "rw": a(L0_ffn_router_w).T,
            "w1": a(L0_ffn_w1).reshape(HALL, D).T, "w3": a(L0_ffn_w3).reshape(HALL, D).T,
            "wt": a(L1_attn_Wt), "wx": np.concatenate([a(L1_attn_Wx).T] * 3, 1),
            "e1": a(L1_ffn_W1).transpose(1, 0, 2).reshape(D, NE * FE), "wr": a(L1_ffn_Wr)}
    d["w64"] = np.concatenate([cols[n] for n in W64], 1)
    d["e1row"] = np.concatenate([a(L1_ffn_b1).reshape(1, NE * FE), a(L1_ffn_br).reshape(1, NE)], 1)
    d["tok66"] = np.concatenate([a(L0_tok_W2), a(L0_tok_b2)[None], a(L0_tok_bp)[None]])
    gx, gy = np.meshgrid(np.arange(NPS), np.arange(NPS), indexing="ij")
    xy = np.stack([gx.ravel(), gy.ravel(), np.full(NPATCH, NPS - 1)]).astype(f) / f(NPS - 1)
    d["tok3"] = np.concatenate([np.concatenate([a(L0_tok_W1), a(L0_tok_b1)[None]]), xy], 1)
    inv = 1.0 / 10000.0 ** (np.arange(0, HD, 2, dtype=f) / HD)
    ang = np.outer(np.concatenate([inv, inv]).astype(f), np.arange(N, dtype=f)).astype(f)
    cos, sin = zeros(128, N), zeros(128, N)
    for h in range(NH):
        cos[32 * h:32 * h + HD] = np.cos(ang)
        sin[32 * h:32 * h + HD] = np.sin(ang) * np.where(np.arange(HD) < HD // 2, -1, 1)[:, None]
    mask = zeros(128, 3 * P)
    i = np.arange(P)
    mask[:P, 0:P] = np.where(i[None] > i[:, None], NEG, 0)
    mask[:P, 2 * P:] = mask[:P, 0:P]
    wo = zeros(128, D)
    for h in range(NH):
        wo[32 * h:32 * h + HD] = a(L0_ffn_wo).T[HD * h:HD * (h + 1)]
    w2 = zeros(MPAD, D)
    w2[:HALL] = a(L0_ffn_w2).transpose(0, 2, 1).reshape(HALL, D)
    was = zeros(IB, U, RND, IB * RND)
    for r in range(RND):
        for q in range(IB):
            was[q, :, r, IB * r + q] = a(L1_attn_Wa)[:, 0]
    cc = {"ident": np.eye(128, dtype=f), "cos": cos, "sin": sin, "mask": mask,
          "rank": np.broadcast_to(np.arange(NE, 0, -1).astype(f), (128, NE)), "wo": wo,
          "w2": w2.reshape(MT, 128, D).transpose(1, 0, 2).reshape(128, MT * D), "was": was.reshape(128, RND * U),
          "ba": np.broadcast_to(a(L1_attn_ba), (128, 1)), "bh": np.concatenate([a(L1_attn_bh)] * 4)[:, None],
          "gamma": np.broadcast_to(a(L1_ffn_gamma), (128, D)), "beta": np.broadcast_to(a(L1_ffn_beta), (128, D)),
          "e2": a(L1_ffn_W2).transpose(1, 0, 2).reshape(FE, NE * D)}
    d["c128"] = np.concatenate([cc[n] for n in C128], 1)
    d["b2"] = a(L1_ffn_b2)
    d["idb"] = np.eye(128).astype(f)
    owner = np.full(MPAD, -1)
    owner[:HALL] = np.arange(HALL) // HID
    d["sel"] = np.concatenate([owner[None] == np.arange(NE)[:, None]] * 3).astype(f)
    d["rep"] = np.concatenate([np.concatenate([np.eye(U)] * IB, 1)] * 3).astype(f)
    hot = np.zeros((2, 3, B, 2, N), f)
    hot[0, :, :, 0], hot[1, :, :, 1] = 1, 1
    d["hot"] = hot.reshape(6, B, 2, N)
    return {k: np.ascontiguousarray(v) for k, v in d.items()}


def kernel(**inputs):
    import concourse.bacc as _bacc
    from concourse.bass_utils import run_bass_kernel_spmd as _run

    nc = _bacc.Bacc("TRN2", target_bir_lowering=False, num_devices=1)
    d = _layout(**inputs)
    arrays, args = {}, []
    for name in _ARGS:
        arrays[f"in_{name}_dram"] = d[name]
        args.append(nc.dram_tensor(f"in_{name}_dram", d[name].shape, mybir.dt.from_np(d[name].dtype),
                                   kind="ExternalInput").ap())
    args.append(nc.dram_tensor("out_dram", (B, N, D), F32, kind="ExternalOutput").ap())
    early_fusion(nc, *args)
    r = _run(nc, [arrays], core_ids=[0])
    return r.results[0]["out_dram"]
```

```python
from contextlib import ExitStack

import numpy as np

import concourse.bass as bass
from concourse import mybir

ALU = mybir.AluOpType
ACT = mybir.ActivationFunctionType
F32 = mybir.dt.float32
BF16 = mybir.dt.bfloat16
X = mybir.AxisListType.X

B = 8
CH, HW, PS = 3, 128, 16
NPS = HW // PS
NPATCH = NPS * NPS
TXT = 128
N = NPATCH + TXT
D = 64
P = N // 2
NT = 2 * B
TOK = B * N
KC = CH * PS * PS // 128
PAIRS = B // 2
CW = 2 * N
NH, NKV, HD = 4, 2, 16
NE, HID = 8, 170
HALL = NE * HID
MT = -(-HALL // 128)
MPAD = MT * 128
U = 32
IB = 128 // U
NCH = P // IB
RND = 8
FE = 128
CAP = float(-(-TOK * 5 // (4 * 8)))
NEG = -1e30
EARLY = 6
FT = (0, 1, 2, 6)
QK = (5, 0)
FILLS = 13

RSQ = {}
_at = 0
for _name, _n in (("z1", PAIRS), ("z2", PAIRS), ("xn", PAIRS), ("xr", PAIRS), ("z3", PAIRS), ("z4", PAIRS), ("y", PAIRS)):
    RSQ[_name] = _at
    _at += _n

W64 = {}
_at = 0
for _name, _n in (("Wa", D), ("Wb", D), ("Wu", D + 1), ("WrT", D), ("ln1", 1),
                  ("q", 128), ("k", 128), ("ks", 128), ("v", NKV * HD),
                  ("rw", NE), ("w1", HALL), ("w3", HALL), ("e1", NE * FE), ("ln2", 1),
                  ("wt", U), ("wx", 3 * U), ("wr", NE)):
    W64[_name] = (_at, _n)
    _at += _n
NW64 = _at
C128 = {}
_at = 0
for _name, _n in (("ident", 128), ("qtab", N), ("cos", N), ("sin", N), ("head", NH), ("rank", NE), ("wo", D),
                  ("w2", MT * D), ("was", RND * U), ("ba", 1), ("bh", 1), ("b1", NE), ("gamma", D), ("beta", D),
                  ("e2", NE * D)):
    C128[_name] = (_at, _n)
    _at += _n
NC128 = _at




def early_fusion(nc, patches, wpatch, txt, w64_d, wrrow, tok66, tok3, c128_d, b2_d, idb_d, sel_d, rep_d, mask_d, hot_d, out):
    qrows = nc.dram_tensor("qrows", (2, B, 3, P, U), BF16, kind="Internal").ap()
    with ExitStack() as ctx:
        def sb(name, shape, dt=F32):
            return ctx.enter_context(nc.sbuf_tensor(name, shape, dt))

        S = {n: ctx.enter_context(nc.semaphore(n)) for n in (
            "ld_x0", "ld_x1", "ld_txt", "ld_w64", "ld_dup", "ld_row", "ld_c", "ld_tok", "ld_b", "ld_b2", "ld_hot", "st_q", "ld_q0", "ld_q", "st_out",
            "filled", "gc_ready", "lnw_ready", "rep_ready", "dup_scaled", "w_lead", "w_rest", "w_mid", "w_parts",
            "dve", "ctr", "var", "veps", "rstd", "fo",
            "hid_mm", "hid", "emb_mm", "emb", "embT", "h0",
            "gmm",
            "z1", "zT_mm", "zT", "gv_mm", "v_sb", "zv_mm", "zv", "p_mm", "p_sb", "lo_mm", "hz1", "h1",
            "xn", "rr", "z2", "xT_mm", "xT", "v_mm", "vall", "qk_mm", "rope_cs", "keys", "headq", "vb", "s_mm", "nmax", "p_exp", "pnorm",
            "pt_mm", "pt_sb0", "pt_sb1", "y_mm", "y_sb0", "y_sb1", "pr_mm", "x2",
            "xr", "rT_mm", "rT", "x_parts", "lg_mm", "lg_max", "lg_exp", "wp3", "wT_mm", "wT", "up0_mm", "up_mm", "silu", "bw", "hh",
            "dn_mm", "ym", "ymT_mm", "h2",
            "z3", "aT_mm", "aT", "q_mm", "k_mm", "qp", "kb", "kp", "bld_mm", "tanh", "al_mm", "al_sb", "amax", "aexp", "pn",
            "pt2_mm", "pt2", "c_mm", "h3",
            "z4", "fT_mm", "fT", "z_parts", "msum", "rl_mm", "rl_max", "rl_exp", "ld_mm", "r2max", "r2exp", "p_less", "e2exp",
            "wd", "zb", "hb", "wdT_mm", "wdT", "b2w_mm", "dg", "wB_mm", "bB_mm", "wbc", "w2s", "e1_mm", "gelu", "e2_mm", "oT",
            "o_mm", "y_out")}

        w64 = sb("w64", [128, NW64])
        c128 = sb("c128", [128, NC128])
        xP = sb("xP", [128, KC, B * NPATCH])
        wpT = sb("wpT", [128, KC, D])
        t66 = sb("t66", [D + 2, D])
        t3 = sb("t3", [3, D + NPATCH])
        hid = sb("hid", [D + 2, NPATCH])
        b2s = sb("b2s", [NE, D])
        idb = sb("idb", [128, 128], BF16)
        sel = sb("sel", [3 * NE, MPAD], BF16)
        rep = sb("rep", [3 * U, 128], BF16)
        GT = sb("GT", [D, D])
        GC = sb("GC", [128, 2 * D])

        def w(name, lo=0, hi=None):
            at, n = W64[name]
            return w64[:, at + lo:at + (n if hi is None else hi)]

        def c(name):
            at, n = C128[name]
            return c128[:, at:at + n]

        ident = c("ident")
        H = sb("H", [P, NT, D])
        Z = sb("Z", [P, NT, D])
        Y = sb("Y", [P, NT, D])
        XH = sb("XH", [P, 2, NT, D])
        XN, HZ = XH[:, 0], XH[:, 1]
        XR = XH[:, :, :, :].rearrange("p a t d -> p (a t d)").rearrange("p (t a d) -> p t a d", a=2, d=D)
        V = XN
        stat = sb("stat", [P, NT, 6])
        mv = sb("mv", [P, NT, 2])
        rstd = sb("rstd", [P, NT])
        mhalf = sb("mhalf", [P, NT])
        r2 = sb("r2", [P, NT])
        dg = sb("dg", [P, NT])
        TA = sb("TA", [128, TOK])
        TB = sb("TB", [128, TOK])
        embS = sb("embS", [D, B * NPATCH])
        ZV = sb("ZV", [D, B * D])
        PB = sb("PB", [128, B, D])
        Vall = sb("Vall", [P, NT, NKV, 2 * HD])
        Vb = sb("Vb", [P, 4, NKV, 2 * HD])
        headq = sb("headq", [128, NH, CW])
        SP_ = sb("SP_", [128, 2, 2, NH, 3 * P])
        mask = sb("mask", [P, P], BF16)
        asum = sb("asum", [P, 2, 2, NH])
        nmx = sb("nmx", [P, 2, 2, NH])
        Pex = SP_[0:P, 0]
        PT = SP_[0:P, 1]
        yT = sb("yT", [128, CW])
        ones = sb("ones", [128, 128])
        lg = sb("lg", [P, NT, NE])
        pr = sb("pr", [P, NT, NE])
        oh = sb("oh", [P, 3, NT, NE])
        sm = sb("sm", [P, 4, NT])
        wp3 = sb("wp3", [P, NT, 3, NE], BF16)
        wT = sb("wT", [3 * NE, TOK], BF16)
        up_sb = sb("up_sb", [128, 3, 2, CW])
        silu, bw, hh = up_sb[:, 0], up_sb[:, 1], up_sb[:, 2]
        BW0 = SP_[:, :, :, :, :].rearrange("p a b c d -> p (a b c d)")[:, 0:MT * CW].rearrange("p (m n) -> p m n", m=MT)
        ym = sb("ym", [128, N])
        QA = up_sb[:, :, :, :].rearrange("p a b n -> p (a b n)")[:, 0:TOK]
        kcs = up_sb[:, 2, :, :]
        NUP = 2 * HALL + NE * FE
        WUP = w64[:, W64["w1"][0]:W64["w1"][0] + NUP]
        W12 = sb("W12", [128, NUP], BF16)
        W13 = sb("W13", [128, NUP], BF16)
        x3 = xP[:, :, :].rearrange("p k n -> p (k n)").bitcast(BF16)[:, 0:3 * TOK].rearrange("p (a n) -> p a n", a=3)
        X11, X22, X31 = x3[:, 0, :], x3[:, 1, :], x3[:, 2, :]
        qp = sb("qp", [P, 2, B, 3, U], BF16)
        qr = sb("qr", [P, NT, U])
        kb = xP[0:3 * U, 0:3, :].rearrange("p k n -> p (k n)")
        khi = xP[0:3 * U, 3:5, :].rearrange("p k n -> p (k n)").bitcast(BF16)[:, 0:TOK]
        RH = sb("RH", [3 * U + 6, B, 2, N], BF16)
        LQ_ = sb("LQ_", [128, B, NCH, 128], BF16)
        LQ = LQ_[0:3 * U + 6]
        TH = SP_[:, :, :, :, :].rearrange("p a b c d -> p (a b c d)")[:, 0:12 * CW].rearrange("p (s j n) -> p s j n", s=4, j=3)
        AL = headq[:, 0, :].rearrange("p (a n) -> p a n", a=2)
        ast = sb("ast", [128, 2, 4])
        PT2 = headq[0:P, 1, :].rearrange("p (a n) -> p a n", a=2)
        ms = sb("ms", [128, B])
        rt = sb("rt", [B, 16, NE])
        rs = sb("rs", [B, 24])
        wdT = sb("wdT", [NE, B])
        b2w = sb("b2w", [B, D])
        dgw = Vall[0:B].rearrange("p t k e -> p (t k e)")[:, 0:B * (NE + D)]
        wBC = sb("wBC", [128, B, NE])
        bBC = HZ[:, 8:16, :]
        W2S = SP_[:, :, :, :, :].rearrange("p a b c d -> p (a b c d)")[:, 0:B * NE * D].rearrange(
            "p (b e d) -> p b e d", b=B, e=NE)
        G1 = LQ_[:, :, :, :].rearrange("p b c q -> p (b c q)").bitcast(F32).rearrange(
            "p (g e n) -> p g e n", g=PAIRS, e=NE)
        oT = headq[:, 2, :].rearrange("p (s n) -> p s n", s=2)

        ps = ctx.enter_context(nc.psum_tensor("ps", [128, 8, 512], F32))

        def bank(i, rows, *dims):
            n = 1
            for x in dims:
                n *= x
            v = ps[0:rows, i, 0:n]
            if len(dims) == 2:
                v = v.rearrange("p (a b) -> p a b", a=dims[0])
            if len(dims) == 3:
                v = v.rearrange("p (a b c) -> p a b c", a=dims[0], b=dims[1])
            return v

        def mm(out_, lhsT, rhs, start=True, stop=True, **k):
            return nc.tensor.matmul(out_, lhsT, rhs, start=start, stop=stop, **k)

        def bc(ap, n):
            return ap.unsqueeze(2).to_broadcast([ap.shape[0], ap.shape[1], n])

        def after(eng, name, n):
            if not isinstance(n, int) or n > 0:
                eng.wait_ge(S[name], n)

        block = ctx.enter_context(nc.Block())

        @block.sync
        def _(sp):
            for k in range(KC):
                sp.dma_start(xP[:, k, :], patches[:, k, :]).then_inc(S["ld_x0" if k < KC // 2 else "ld_x1"], 16)
            sp.dma_start(c128[:, :], c128_d).then_inc(S["ld_c"], 16)
            sp.wait_ge(S["filled"], FILLS)
            at, n = W64["w1"][0], NUP + 1
            sp.dma_start(w64[D:128, at:at + n], w64_d[:, at:at + n]).then_inc(S["ld_dup"], 16)
            sp.wait_ge(S["qp"], 1)
            for half in range(2):
                sp.dma_start(qrows[half].rearrange("b a p u -> p (b a) u"),
                             qp[:, half, :, :, :].rearrange("p b a u -> p (b a) u")).then_inc(S["st_q"], 16)
            sp.wait_ge(S["st_q"], 32)
            for b in range(B):
                for half in range(2):
                    row = 3 * U + 3 * half
                    sp.dma_start(LQ[row:row + 3, b, :, :].rearrange("o c q -> o (c q)"),
                                 qrows[half, b].rearrange("a p u -> a (p u)")).then_inc(S["ld_q" if b else "ld_q0"], 16)
            for g in range(PAIRS):
                sp.wait_ge(S["y_out"], g + 1)
                for i in range(2):
                    sp.dma_start(out[2 * g:2 * g + 2, i * P:(i + 1) * P, :].rearrange("b p d -> p b d"),
                                 Y[:, 4 * g + i:4 * g + 4:2, :]).then_inc(S["st_out"], 16)
            sp.wait_ge(S["st_out"], 32 * PAIRS)

        @block.gpsimd
        def _(pool):
            pool.dma_start(idb[:, :], idb_d).then_inc(S["ld_b"], 16)
            pool.dma_start(rep[:, :], rep_d).then_inc(S["ld_b"], 16)
            pool.dma_start(sel[:, :], sel_d).then_inc(S["ld_b"], 16)
            pool.dma_start(mask[:, :], mask_d).then_inc(S["ld_b"], 16)
            pool.dma_start(RH[3 * U:3 * U + 6, :, :, :], hot_d).then_inc(S["ld_hot"], 16)
            fills = [(w64[D:128, :], 0.0), (GC[D:128, :], 0.0), (PB[D:128, :, :], 0.0), (TB[D:128, :], 0.0),
                     (ms[D:128, :], 0.0), (TA[D:128, :], 0.0),
                     (TA[D:D + 1, :], 1.0), (TB[D:D + 1, :], 1.0), (ms[D:D + 1, :], 1.0), (hid[D:D + 2, :], 1.0),
                     (ones[:, :], 1.0), (mhalf[:, :], -0.5), (Vall[:, :, :, :], 0.0)]
            for n, (ap, value) in enumerate(fills):
                if n:
                    pool.wait_ge(S["filled"], n)
                nc.gpsimd.memset(ap, value).then_inc(S["filled"], 1)
            pool.wait_ge(S["filled"], FILLS)
            pool.dma_start(w64[D:D + 1, W64["wr"][0]:NW64], wrrow).then_inc(S["ld_row"], 16)

            def rsqrt(n, out_, in_, eps):
                pool.wait_ge(S["var"], n)
                nc.gpsimd.tensor_scalar(out_, in_, eps, None, ALU.add).then_inc(S["veps"], 1)
                pool.wait_ge(S["veps"], n)
                half = mhalf[:, 0:out_.shape[1]]
                nc.gpsimd.tensor_tensor(out_, out_, half, ALU.pow).then_inc(S["rstd"], 1)

            def layer_rstd(name, c):
                rsqrt(RSQ[name] + c + 1, rstd[:, 4 * c:4 * c + 4], mv[:, 4 * c:4 * c + 4, 1], 1e-5)

            for g in range(PAIRS):
                layer_rstd("z1", g)
            pool.wait_ge(S["z1"], PAIRS)
            nc.gpsimd.tensor_tensor(HZ[:, :, :], H[:, :, :], Z[:, :, :], ALU.add).then_inc(S["hz1"], 1)
            for g in range(PAIRS):
                layer_rstd("z2", g)
            for g in range(PAIRS):
                rsqrt(RSQ["xn"] + g + 1, r2[:, 4 * g:4 * g + 4], r2[:, 4 * g:4 * g + 4], 1e-6)
            pool.wait_ge(S["rstd"], RSQ["xn"] + PAIRS)
            pool.wait_ge(S["w_lead"], 2)
            nc.gpsimd.tensor_tensor(WUP[D:128], WUP[D:128], W12[D:128, :], ALU.subtract).then_inc(S["w_rest"], 1)
            pool.wait_ge(S["w_rest"], 1)
            for g in range(PAIRS):
                pool.wait_ge(S["rope_cs"], g + 1)
                nc.gpsimd.tensor_tensor(TB[:, g * CW:(g + 1) * CW], kcs[:, 0, :], kcs[:, 1, :], ALU.add
                                        ).then_inc(S["keys"], 1)

            def head_queries(g):
                after(pool, "s_mm", g * 2)
                nc.gpsimd.tensor_tensor(headq[:, :, :], QA[:, bass.ds(g * CW, CW)].unsqueeze(1).to_broadcast([128, NH, CW]),
                                        bc(c("head"), CW), ALU.mult).then_inc(S["headq"], 1)

            def values(g):
                after(pool, "y_mm", g * 2)
                nc.gpsimd.tensor_copy(Vb[:, :, :, :].rearrange("p t k e -> p (t k e)"),
                                      Vall[:, bass.ds(g * 4, 4), :, :].rearrange("p t k e -> p (t k e)")
                                      ).then_inc(S["vb"], 1)

            pool.wait_ge(S["keys"], PAIRS)
            head_queries(0)
            pool.wait_ge(S["vall"], 1)
            values(0)
            pool.wait_ge(S["vb"], 1)
            pool.wait_ge(S["w_mid"], 1)
            nc.gpsimd.tensor_tensor(W13[D:128, :], WUP[D:128], W12[D:128, :], ALU.subtract).then_inc(S["w_parts"], 1)
            pool.wait_ge(S["w_parts"], 1)
            with pool.Fori(1, PAIRS) as g:
                head_queries(g)
                values(g)
            for g in range(PAIRS):
                rsqrt(RSQ["xr"] + g + 1, r2[:, 4 * g:4 * g + 4], r2[:, 4 * g:4 * g + 4], 1e-6)
            for name in ("z3", "z4", "y"):
                for g in range(PAIRS):
                    layer_rstd(name, g)

        @block.scalar
        def _(act):
            act.dma_start(wpT[:, :, :], wpatch).then_inc(S["ld_tok"], 16)
            act.dma_start(t66[:, :], tok66).then_inc(S["ld_tok"], 16)
            act.dma_start(t3[:, :], tok3).then_inc(S["ld_tok"], 16)
            act.dma_start(w64[0:D, :], w64_d).then_inc(S["ld_w64"], 16)
            act.dma_start(H[NPATCH:P, 0:NT:2, :], txt[:, 0:P - NPATCH, :].rearrange("b p d -> p b d")
                          ).then_inc(S["ld_txt"], 16)
            act.dma_start(H[:, 1:NT:2, :], txt[:, P - NPATCH:TXT, :].rearrange("b p d -> p b d")
                          ).then_inc(S["ld_txt"], 16)
            act.dma_start(b2s[:, :], b2_d).then_inc(S["ld_b2"], 16)
            act.wait_ge(S["hid_mm"], 1)
            nc.scalar.activation(hid[0:D, :], bank(0, D, NPATCH), ACT.Relu).then_inc(S["hid"], 1)
            act.wait_ge(S["gmm"], 1)
            act.wait_ge(S["filled"], FILLS)
            nc.scalar.copy(GC[0:D, 0:D], bank(1, D, D))
            nc.scalar.copy(GC[0:D + 1, D:2 * D], bank(2, D + 1, D))
            nc.scalar.copy(GT[:, :], bank(3, D, D)).then_inc(S["gc_ready"], 1)
            act.wait_ge(S["emb_mm"], 1)
            nc.scalar.copy(embS[:, :], bank(4, D, B * NPATCH)).then_inc(S["emb"], 1)

            def feature_major(dst, done, ready):
                for g in range(PAIRS):
                    act.wait_ge(done, g + 1)
                    nc.scalar.copy(dst[0:D, g * CW:(g + 1) * CW], bank(g, D, CW)).then_inc(ready, 1)

            feature_major(TA, S["zT_mm"], S["zT"])
            for q in range(PAIRS):
                act.wait_ge(S["gv_mm"], q + 1)
                nc.scalar.copy(V[:, 4 * q:4 * q + 4, :], bank(4 + q, P, 4, 2 * D)[:, :, D:2 * D]).then_inc(S["v_sb"], 1)
            act.wait_ge(S["zv_mm"], 1)
            nc.scalar.copy(ZV[:, :], bank(0, D, B * D)).then_inc(S["zv"], 1)
            act.wait_ge(S["p_mm"], 1)
            nc.scalar.copy(PB[0:D, :, :], bank(1, D, B, D)).then_inc(S["p_sb"], 1)
            act.wait_ge(S["lnw_ready"], 1)
            act.wait_ge(S["dup_scaled"], 1)
            nc.scalar.copy(W12[:, :], WUP).then_inc(S["w_lead"], 1)
            nc.scalar.copy(W13[0:D, :], WUP[0:D]).then_inc(S["w_lead"], 1)
            feature_major(TB, S["xT_mm"], S["xT"])
            act.wait_ge(S["w_rest"], 1)
            nc.scalar.copy(W12[D:128, :], WUP[D:128]).then_inc(S["w_mid"], 1)
            act.wait_ge(S["v_mm"], 1)
            nc.scalar.copy(Vall[:, :, :, 0:HD].rearrange("p t k e -> p (t k) e"), bank(4, P, NT * NKV, HD)).then_inc(S["vall"], 1)
            act.wait_ge(S["vall"], 1)

            def exps(g):
                for i in range(2):
                    act.wait_ge(S["nmax"], g * 2 + (i + 1))
                    for h in range(NH):
                        nc.scalar.activation(Pex[:, i, h, 0:P], ps[0:P, 4 * i + h, 0:P], ACT.Exp,
                                             bias=nmx[:, i, 0, h:h + 1], scale=HD ** -0.5, accum_out=asum[:, i, 0, h:h + 1])
                        last = nc.scalar.activation(Pex[:, i, h, P:3 * P], ps[0:P, 4 * i + h, P:3 * P], ACT.Exp,
                                                    bias=nmx[:, i, 1, h:h + 1], scale=HD ** -0.5,
                                                    accum_out=asum[:, i, 1, h:h + 1])
                    last.then_inc(S["p_exp"], 1)
                act.wait_ge(S["pt_mm"], g * 2 + 2)
                nc.scalar.copy(PT[:, 1, :, :], ps[0:P, 4:8, 0:3 * P]).then_inc(S["pt_sb1"], 1)
                act.wait_ge(S["y_mm"], g * 2 + 2)
                nc.scalar.copy(yT[:, N:2 * N], ps[:, 4, 0:N]).then_inc(S["y_sb1"], 1)

            exps(0)
            with act.Fori(1, PAIRS) as g:
                exps(g)
            for g in range(PAIRS):
                act.wait_ge(S["rT_mm"], g + 1)
                nc.scalar.copy(TA[0:D, g * CW:(g + 1) * CW], bank(g, D, CW))
                nc.scalar.copy(X11[:, g * CW:(g + 1) * CW], bank(g, 128, CW)).then_inc(S["rT"], 1)
            act.wait_ge(S["lg_max"], 1)
            nc.scalar.activation(pr[:, :, :], lg[:, :, :], ACT.Exp).then_inc(S["lg_exp"], 1)

            def silu_of(g, m):
                rows = min(128, HALL - 128 * m)
                after(act, "bw", g * MT + max(m - 1, 0))
                nc.scalar.activation(silu[0:rows, m % 2, :], ps[0:rows, 3 * (m % 2), 0:CW],
                                     ACT.Silu).then_inc(S["silu"], 1)

            for m in range(MT):
                if m == EARLY:
                    act.wait_ge(S["wT_mm"], 1)
                    nc.scalar.copy(wT[:, :].rearrange("p (a b) -> p a b", a=2),
                                   ps[0:3 * NE, 5:7, :].bitcast(BF16)[:, :, 0:TOK // 2]).then_inc(S["wT"], 1)
                act.wait_ge(S["up0_mm"], m + 1)
                silu_of(0, m)

            def silus(g):
                for m in range(MT):
                    act.wait_ge(S["up_mm"], g * MT + (m + 1))
                    silu_of(g, m)
                    if m == 1:
                        out_ready(g - 1)

            def out_ready(g):
                act.wait_ge(S["dn_mm"], g * MT + MT)
                nc.scalar.copy(ym[:, :], bank(6, 128, N)).then_inc(S["ym"], 1)

            with act.Fori(1, PAIRS) as g:
                silus(g)
            out_ready(PAIRS - 1)
            feature_major(TB, S["aT_mm"], S["aT"])

            for g in range(PAIRS):
                act.wait_ge(S["k_mm"], g + 1)
                nc.scalar.activation(kb[:, g * CW:(g + 1) * CW], bank(g, 3 * U, CW), ACT.Identity,
                                     bias=c("bh")[0:3 * U]).then_inc(S["kb"], 1)

            def softmax_exp(b):
                act.wait_ge(S["amax"], b + 1)
                for k in range(2):
                    last = nc.scalar.activation(AL[:, k, :], AL[:, k, :], ACT.Exp, bias=ast[:, k, 1:2],
                                                accum_out=ast[:, k, 2:3])
                last.then_inc(S["aexp"], 1)

            def tanhs(b):
                for r in range(RND):
                    act.wait_ge(S["bld_mm"], b * RND + (r + 1))
                    after(act, "al_mm", b * RND // 2 + r // 2 - 1)
                    nc.scalar.activation(TH[:, r % 4, :, :], ps[:, 3 * (r % 2):3 * (r % 2) + 3, 0:CW],
                                         ACT.Tanh).then_inc(S["tanh"], 1)
                    if r == 3 and b > 0:
                        softmax_exp(b - 1)

            tanhs(0)
            for b in range(1, B):
                tanhs(b)
            softmax_exp(B - 1)
            def last_features(g):
                act.wait_ge(S["fT_mm"], g + 1)
                nc.scalar.copy(X11[:, g * CW:(g + 1) * CW], bank(FT[g], 128, CW))
                nc.scalar.copy(TA[:, g * CW:(g + 1) * CW], bank(FT[g], 128, CW)).then_inc(S["fT"], 1)

            for g in range(PAIRS - 1):
                last_features(g)

            def gelus(g, experts=range(NE)):
                for e in experts:
                    act.wait_ge(S["e1_mm"], g * NE + (e + 1))
                    nc.scalar.activation(G1[:, g, e, :], ps[:, e % 4, 0:CW], ACT.Gelu, bias=c("b1")[:, e:e + 1]).then_inc(S["gelu"], 1)

            gelus(0, range(4))
            last_features(PAIRS - 1)
            act.wait_ge(S["rl_max"], 1)
            nc.scalar.activation(rt[:, 1, :], rt[:, 0, :], ACT.Exp, accum_out=rs[:, 1:2]).then_inc(S["rl_exp"], 1)
            act.wait_ge(S["r2max"], 1)
            nc.scalar.activation(rt[:, 4, :], rt[:, 3, :], ACT.Exp, accum_out=rs[:, 3:4]).then_inc(S["r2exp"], 1)
            act.wait_ge(S["p_less"], 1)
            nc.scalar.activation(rt[:, 13, :], rt[:, 13, :], ACT.Exp).then_inc(S["e2exp"], 1)
            gelus(0, range(4, NE))
            gelus(1)
            act.wait_ge(S["wdT_mm"], 1)
            nc.scalar.copy(wdT[:, :], bank(5, NE, B)).then_inc(S["wdT"], 1)
            gelus(2, range(2))
            act.wait_ge(S["b2w_mm"], 1)
            nc.scalar.copy(b2w[:, :], bank(6, B, D)).then_inc(S["wdT"], 1)
            gelus(2, range(2, 5))
            act.wait_ge(S["bB_mm"], 1)
            nc.scalar.copy(bBC[:, :, :], bank(6, P, B, D)).then_inc(S["wbc"], 1)
            gelus(2, range(5, NE))

            def token_rows(g):
                act.wait_ge(S["e2_mm"], g + 1)
                after(act, "o_mm", g - 1)
                nc.scalar.copy(oT[:, g % 2, :], bank(4 + g % 2, 128, N)).then_inc(S["oT"], 1)

            gelus(3, range(4))
            token_rows(0)
            gelus(3, range(4, NE))
            for g in range(1, PAIRS):
                token_rows(g)

        @block.vector
        def _(dve):
            count = [0]

            def link(ins, base=0, beside=None):
                count[0] += 1
                ins.then_inc(S["dve"], 1)
                if beside is not None:
                    unweighted(beside)
                dve.wait_ge(S["dve"], base + count[0])

            V_ = nc.vector

            def stats(src, name, g):
                for t in range(4 * g, 4 * g + 4):
                    last = V_.bn_stats(stat[:, t, :], src[:, t, :])
                link(last)
                for t in range(4 * g, 4 * g + 4):
                    last = V_.bn_aggr(mv[:, t, :], stat[:, t, :])
                last.then_inc(S["var"], 1)

            def centre(src, dst, name, g):
                dve.wait_ge(S["var"], RSQ[name] + g + 1)
                t = slice(4 * g, 4 * g + 4)
                V_.tensor_tensor(dst[:, t, :], src[:, t, :], bc(mv[:, t, 0], D), ALU.subtract).then_inc(S["ctr"], 1)

            def scaled(dst, name, g):
                dve.wait_ge(S["rstd"], RSQ[name] + g + 1)
                dve.wait_ge(S["ctr"], CTR[name] + g + 1)
                t = slice(4 * g, 4 * g + 4)
                return V_.tensor_tensor(dst[:, t, :], dst[:, t, :], bc(rstd[:, t], D), ALU.mult)

            CTR = {name: k * PAIRS for k, name in enumerate(("z1", "z2", "z3", "z4", "y"))}

            def norm(src, dst, name, done, chunks=range(PAIRS)):
                ready = []
                for g in chunks:
                    stats(src, name, g)
                    centre(src, dst, name, g)
                    if ready:
                        scaled(dst, name, ready[-1]).then_inc(S[done], 1)
                    ready.append(g)
                scaled(dst, name, ready[-1]).then_inc(S[done], 1)

            dve.wait_ge(S["ld_w64"], 16)
            q0, v1 = W64["q"][0], W64["v"][0] + W64["v"][1]
            r0, w31 = W64["rw"][0], W64["w3"][0] + W64["w3"][1]
            V_.tensor_scalar(w64[0:D, q0:v1], w64[0:D, q0:v1], w("ln1")[0:D], None, ALU.mult)
            V_.tensor_scalar(w64[0:D, r0:w31], w64[0:D, r0:w31], w("ln2")[0:D], None, ALU.mult).then_inc(S["lnw_ready"], 1)
            dve.wait_ge(S["ld_b"], 64)
            V_.tensor_copy(LQ[0:3 * U, :, :, :].rearrange("p b c q -> p (b c) q"),
                           rep[:, :].unsqueeze(1).to_broadcast([3 * U, B * NCH, 128])).then_inc(S["rep_ready"], 1)
            dve.wait_ge(S["embT"], 1)
            V_.tensor_copy(H[0:NPATCH, 0:NT:2, :], bank(5, NPATCH, B, D)).then_inc(S["h0"], 1)
            dve.wait_ge(S["h0"], 1)
            dve.wait_ge(S["ld_txt"], 32)
            norm(H, Z, "z1", "z1")
            dve.wait_ge(S["z1"], PAIRS)
            for q in range(PAIRS):
                dve.wait_ge(S["v_sb"], q + 1)
                last = V_.tensor_tensor(Y[:, 4 * q:4 * q + 4, :], bank(4 + q, P, 4, 2 * D)[:, :, 0:D],
                                        Z[:, 4 * q:4 * q + 4, :], ALU.mult)
            link(last)
            link(V_.tensor_reduce(dg[:, :], Y[:, :, :], axis=X, op=ALU.add))
            link(V_.tensor_tensor(Y[:, :, :], V[:, :, :], bc(dg[:, :], D), ALU.mult))
            dve.wait_ge(S["ld_dup"], 16)
            V_.tensor_scalar(WUP[D:128, 0:2 * HALL], WUP[D:128, 0:2 * HALL], w("ln2")[D:128], None, ALU.mult).then_inc(S["dup_scaled"], 1)
            for q in range(2):
                dve.wait_ge(S["lo_mm"], q + 1)
                last = V_.tensor_tensor(Y[:, 8 * q:8 * q + 8, :], bank(2 + q, P, 8, D), Y[:, 8 * q:8 * q + 8, :],
                                        ALU.subtract)
            link(last)
            dve.wait_ge(S["hz1"], 1)
            V_.scalar_tensor_tensor(H[:, :, :], Y[:, :, :], 1.0 / N, HZ[:, :, :], ALU.mult, ALU.add).then_inc(S["h1"], 1)
            dve.wait_ge(S["h1"], 1)
            norm(H, Z, "z2", "z2")
            for g in range(PAIRS):
                t = slice(4 * g, 4 * g + 4)
                dve.wait_ge(S["z2"], g + 1)
                V_.tensor_tensor(r2[:, t], rstd[:, t], rstd[:, t], ALU.mult).then_inc(S["rr"], 1)
            for g in range(PAIRS):
                t = slice(4 * g, 4 * g + 4)
                dve.wait_ge(S["rr"], g + 1)
                V_.tensor_tensor(r2[:, t], r2[:, t], mv[:, t, 1], ALU.mult).then_inc(S["var"], 1)
            for g in range(PAIRS):
                t = slice(4 * g, 4 * g + 4)
                dve.wait_ge(S["rstd"], RSQ["xn"] + g + 1)
                V_.tensor_tensor(XN[:, t, :], Z[:, t, :], bc(r2[:, t], D), ALU.mult).then_inc(S["xn"], 1)
            for g in range(PAIRS):
                dve.wait_ge(S["qk_mm"], g + 1)
                after(dve, "keys", g)
                for j, (dst, tab) in enumerate(((QA[:, g * CW:(g + 1) * CW], "qtab"), (kcs[:, 0, :], "cos"),
                                                (kcs[:, 1, :], "sin"))):
                    last = V_.tensor_tensor(dst.rearrange("p (i n) -> p i n", i=2),
                                            ps[:, QK[g % 2] + j, 0:CW].rearrange("p (i n) -> p i n", i=2),
                                            c(tab).unsqueeze(1).to_broadcast([128, 2, N]), ALU.mult)
                last.then_inc(S["rope_cs"], 1)

            def maxima(g, i, base=0):
                dve.wait_ge(S["s_mm"], g * 2 + (i + 1))
                V_.tensor_reduce(nmx[:, i, 0, :], ps[0:P, 4 * i:4 * i + 4, 0:P], axis=X, op=ALU.max)
                link(V_.tensor_reduce(nmx[:, i, 1, :], ps[0:P, 4 * i:4 * i + 4, P:3 * P], axis=X, op=ALU.max), base)
                V_.tensor_scalar(nmx[:, i, :, :], nmx[:, i, :, :], -(HD ** -0.5), None, ALU.mult).then_inc(S["nmax"], 1)

            def divide(g, i, base=0):
                dve.wait_ge(S["p_exp"], g * 2 + (i + 1))
                link(V_.reciprocal(asum[:, i, :, :], asum[:, i, :, :]), base)
                V_.tensor_tensor(Pex[:, i, :, 0:P], Pex[:, i, :, 0:P], bc(asum[:, i, 0, :], P), ALU.mult)
                V_.tensor_tensor(Pex[:, i, :, P:3 * P], Pex[:, i, :, P:3 * P], bc(asum[:, i, 1, :], N),
                                 ALU.mult).then_inc(S["pnorm"], 1)

            def residual(g, i):
                dve.wait_ge(S["pr_mm"], g * 2 + (i + 1))
                V_.tensor_tensor(Y[:, bass.ds(g * 4 + 2 * i, 2), :], bank(4 * i + 2, P, 2, D),
                                 Z[:, bass.ds(g * 4 + 2 * i, 2), :], ALU.add).then_inc(S["x2"], 1)

            def probs_0(g):
                dve.wait_ge(S["pt_mm"], g * 2 + 1)
                V_.tensor_copy(PT[:, 0, :, :], ps[0:P, 0:4, 0:3 * P]).then_inc(S["pt_sb0"], 1)

            def rows_0(g):
                dve.wait_ge(S["y_mm"], g * 2 + 1)
                V_.tensor_copy(yT[:, 0:N], ps[:, 0, 0:N]).then_inc(S["y_sb0"], 1)

            maxima(0, 0)
            b0 = count[0]
            CHB = 4

            def attend(g):
                count[0] = b0
                base = g * CHB
                divide(g, 0, base)
                maxima(g, 1, base)
                probs_0(g)
                rows_0(g)
                divide(g, 1, base)
                residual(g, 0)
                maxima(g + 1, 0, base)
                residual(g, 1)
                assert count[0] - b0 == CHB

            attend(0)
            with dve.Fori(1, PAIRS - 1) as g:
                attend(g)
            count[0] = b0 + (PAIRS - 1) * CHB

            def mean_square(g):
                t = slice(4 * g, 4 * g + 4)
                dve.wait_ge(S["x2"], 2 * g + 2)
                link(V_.tensor_tensor(Z[:, t, :], Y[:, t, :], Y[:, t, :], ALU.mult))
                link(V_.tensor_reduce(r2[:, t], Z[:, t, :], axis=X, op=ALU.add))
                V_.tensor_scalar(r2[:, t], r2[:, t], 1.0 / D, None, ALU.mult).then_inc(S["var"], 1)

            def router_input(g):
                t = slice(4 * g, 4 * g + 4)
                dve.wait_ge(S["rstd"], RSQ["xr"] + g + 1)
                for half in range(2):
                    last = V_.tensor_tensor(XR[:, t, half, :], Y[:, t, :], bc(r2[:, t], D), ALU.mult)
                last.then_inc(S["xr"], 1)

            g = PAIRS - 1
            divide(g, 0)
            mean_square(0)
            maxima(g, 1)
            probs_0(g)
            mean_square(1)
            rows_0(g)
            divide(g, 1)
            mean_square(2)
            residual(g, 0)
            router_input(0)
            router_input(1)
            residual(g, 1)
            mean_square(g)
            router_input(2)
            link(V_.tensor_tensor(H[:, :, :], H[:, :, :], Y[:, :, :], ALU.add))
            router_input(g)
            for g in range(PAIRS):
                cols = slice(g * CW, (g + 1) * CW)
                rest = hh[:, g % 2, :]
                dve.wait_ge(S["rT"], g + 1)
                link(V_.tensor_tensor(rest, bank(g, 128, CW), X11[:, cols], ALU.subtract))
                V_.tensor_copy(X31[D:128, cols], X11[D:128, cols])
                link(V_.tensor_copy(X22[:, cols], rest))
                V_.tensor_tensor(X31[0:D, cols], rest[0:D], X22[0:D, cols], ALU.subtract).then_inc(S["x_parts"], 1)
            dve.wait_ge(S["lg_mm"], 1)
            link(V_.tensor_reduce(sm[:, 0, :], bank(4, P, NT, NE), axis=X, op=ALU.max))
            V_.tensor_tensor(lg[:, :, :], bank(4, P, NT, NE), bc(sm[:, 0, :], NE), ALU.subtract).then_inc(S["lg_max"], 1)
            dve.wait_ge(S["lg_exp"], 1)
            link(V_.tensor_reduce(sm[:, 1, :], pr[:, :, :], axis=X, op=ALU.add))
            link(V_.reciprocal(sm[:, 1, :], sm[:, 1, :]))
            link(V_.tensor_tensor(pr[:, :, :], pr[:, :, :], bc(sm[:, 1, :], NE), ALU.mult))

            def unweighted(m):
                rows = min(128, HALL - 128 * m)
                dve.wait_ge(S["silu"], m + 1)
                V_.tensor_tensor(BW0[0:rows, m, :], silu[0:rows, m % 2, :], ps[0:rows, 3 * (m % 2) + 1, 0:CW],
                                 ALU.mult).then_inc(S["bw"], 1)

            rank = c("rank")[0:P].unsqueeze(1).to_broadcast([P, NT, NE])

            def first_max(src, dst, s):
                link(V_.tensor_reduce(s, src, axis=X, op=ALU.max))
                link(V_.tensor_tensor(dst, src, bc(s, NE), ALU.is_equal))
                link(V_.tensor_tensor(dst, dst, rank, ALU.mult))
                link(V_.tensor_reduce(s, dst, axis=X, op=ALU.max))
                link(V_.tensor_tensor(dst, dst, bc(s, NE), ALU.is_equal))

            first_max(pr[:, :, :], oh[:, 0, :, :], sm[:, 2, :])
            link(V_.scalar_tensor_tensor(oh[:, 1, :, :], oh[:, 0, :, :], -2.0, pr[:, :, :], ALU.mult, ALU.add), beside=0)
            first_max(oh[:, 1, :, :], oh[:, 2, :, :], sm[:, 3, :])
            link(V_.tensor_tensor(oh[:, 0, :, :], oh[:, 0, :, :], oh[:, 2, :, :], ALU.add), beside=1)
            link(V_.tensor_tensor(pr[:, :, :], pr[:, :, :], oh[:, 0, :, :], ALU.mult))
            link(V_.tensor_reduce(sm[:, 0, :], pr[:, :, :], axis=X, op=ALU.add))
            link(V_.tensor_scalar(sm[:, 0, :], sm[:, 0, :], 1e-9, None, ALU.add), beside=2)
            link(V_.reciprocal(sm[:, 0, :], sm[:, 0, :]))
            link(V_.tensor_tensor(pr[:, :, :], pr[:, :, :], bc(sm[:, 0, :], NE), ALU.mult))

            def split3(src, hi, mid, lo, rest):
                link(V_.tensor_copy(hi, src))
                link(V_.tensor_tensor(rest, src, hi, ALU.subtract))
                link(V_.tensor_copy(mid, rest))
                return V_.tensor_tensor(lo, rest, mid, ALU.subtract)

            split3(pr[:, :, :], wp3[:, :, 0, :], wp3[:, :, 1, :], wp3[:, :, 2, :], lg[:, :, :]).then_inc(S["wp3"], 1)
            for m in range(3, MT):
                unweighted(m)
            def add_mixture(g):
                dve.wait_ge(S["ymT_mm"], g + 1)
                V_.tensor_tensor(H[:, bass.ds(g * 4, 4), :].rearrange("p (i h) d -> p i h d", i=2),
                                 H[:, bass.ds(g * 4, 4), :].rearrange("p (i h) d -> p i h d", i=2),
                                 bank(7, P, 2, 2, D).rearrange("p h i d -> p i h d"), ALU.add).then_inc(S["h2"], 1)

            def weighted_0(m):
                rows = min(128, HALL - 128 * m)
                dve.wait_ge(S["up_mm"], m + 1)
                after(dve, "dn_mm", max(m - 1, 0))
                V_.tensor_tensor(hh[0:rows, m % 2, :], BW0[0:rows, m, :], ps[0:rows, 3 * (m % 2) + 2, 0:CW],
                                 ALU.mult).then_inc(S["hh"], 1)

            def gated(g):
                for m in range(MT):
                    rows = min(128, HALL - 128 * m)
                    bk = 3 * (m % 2)
                    dve.wait_ge(S["silu"], g * MT + (m + 1))
                    V_.tensor_tensor(bw[0:rows, m % 2, :], silu[0:rows, m % 2, :], ps[0:rows, bk + 1, 0:CW],
                                     ALU.mult).then_inc(S["bw"], 1)
                    dve.wait_ge(S["bw"], g * MT + (m + 1))
                    after(dve, "dn_mm", g * MT + max(m - 1, 0))
                    V_.tensor_tensor(hh[0:rows, m % 2, :], bw[0:rows, m % 2, :], ps[0:rows, bk + 2, 0:CW],
                                     ALU.mult).then_inc(S["hh"], 1)
                    if m == 5 and not (isinstance(g, int) and g == 0):
                        add_mixture(g - 1)
                    if isinstance(g, int) and g == PAIRS - 1:
                        for c0, m0 in ((0, 0), (1, 3), (2, 6)):
                            if m == m0:
                                dve.wait_ge(S["h2"], c0 + 1)
                                stats(H, "z3", c0)
                            if m == m0 + 1:
                                centre(H, Z, "z3", c0)
                            if m == m0 + 2:
                                scaled(Z, "z3", c0).then_inc(S["z3"], 1)

            dve.wait_ge(S["bw"], MT)
            for m in range(MT):
                weighted_0(m)
            with dve.Fori(1, PAIRS - 1) as g:
                gated(g)
            gated(PAIRS - 1)
            add_mixture(PAIRS - 1)
            dve.wait_ge(S["h2"], PAIRS)
            norm(H, Z, "z3", "z3", (PAIRS - 1,))
            def keys(g):
                cols = slice(g * CW, (g + 1) * CW)
                images = slice(2 * g, 2 * g + 2)

                def seen(ap):
                    return ap[:, cols].rearrange("p (b n) -> p b n", b=2)

                dve.wait_ge(S["kb"], g + 1)
                link(V_.tensor_copy(khi[:, cols], kb[:, cols]))
                for s in range(2):
                    V_.tensor_copy(RH[0:U, images, s, :], seen(khi[0:U]))
                link(V_.tensor_tensor(kb[:, cols], kb[:, cols], khi[:, cols], ALU.subtract))
                link(V_.tensor_copy(khi[:, cols], kb[:, cols]))
                for s in range(2):
                    V_.tensor_copy(RH[U:2 * U, images, s, :], seen(khi[U:2 * U]))
                for s in range(2):
                    last = V_.tensor_tensor(RH[2 * U:3 * U, images, s, :], seen(kb[2 * U:3 * U]),
                                            seen(khi[2 * U:3 * U]), ALU.subtract)
                last.then_inc(S["kp"], 1)

            keys(0)
            dve.wait_ge(S["q_mm"], 1)
            qv = qp[:, :, :, :, :].rearrange("p h b a u -> p b h a u")
            split3(bank(4, P, B, 2, U), qv[:, :, :, 0, :], qv[:, :, :, 1, :], qv[:, :, :, 2, :],
                   qr[:, :, :].rearrange("p (b h) u -> p b h u", h=2)).then_inc(S["qp"], 1)
            for g in range(1, PAIRS):
                keys(g)

            def softmax(b):
                dve.wait_ge(S["al_mm"], (b + 1) * RND // 2)
                V_.tensor_scalar(AL, bank(6, 128, 2, N), c("ba"), None, ALU.add).then_inc(S["al_sb"], 1)
                dve.wait_ge(S["al_sb"], b + 1)
                link(V_.tensor_reduce(ast[:, :, 0], AL, axis=X, op=ALU.max))
                V_.tensor_scalar(ast[:, :, 1], ast[:, :, 0], -1.0, None, ALU.mult).then_inc(S["amax"], 1)
                dve.wait_ge(S["aexp"], b + 1)
                link(V_.reciprocal(ast[:, :, 3], ast[:, :, 2]))
                V_.tensor_tensor(AL, AL, bc(ast[:, :, 3], N), ALU.mult).then_inc(S["pn"], 1)
                if b == B - 1:
                    link(feature_sums(0))
                    parts(0)
                dve.wait_ge(S["pt2_mm"], b + 1)
                rows = bank(7, P, 2, 256)
                V_.tensor_copy(PT2[:, :, 0:128], rows[:, :, 0:128])
                for odd in range(2):
                    last = V_.tensor_copy(
                        PT2[:, :, 128:N].rearrange("p t (k o q) -> p t k o q", o=2, q=IB)[:, :, :, odd, :],
                        rows[:, :, 128 + 64 * odd:N + 64 * odd].rearrange("p t (k o q) -> p t k o q", o=2, q=IB)[:, :, :, odd, :])
                last.then_inc(S["pt2"], 1)
                dve.wait_ge(S["c_mm"], b + 1)
                V_.tensor_tensor(H[:, bass.ds(b * 2, 2), :], bank(7, P, 2, D), H[:, bass.ds(b * 2, 2), :],
                                 ALU.add).then_inc(S["h3"], 1)

            def feature_sums(g):
                dve.wait_ge(S["fT"], g + 1)
                return V_.tensor_reduce(ms[0:D, 2 * g:2 * g + 2],
                                        TA[0:D, g * CW:(g + 1) * CW].rearrange("p (b n) -> p b n", b=2), axis=X, op=ALU.add)

            def parts(g):
                cols = slice(g * CW, (g + 1) * CW)
                dve.wait_ge(S["fT"], g + 1)
                link(V_.tensor_tensor(TA[:, cols], TA[:, cols], X11[:, cols], ALU.subtract))
                V_.tensor_copy(X31[D:128, cols], X11[D:128, cols])
                link(V_.tensor_copy(X22[:, cols], TA[:, cols]))
                V_.tensor_tensor(X31[0:D, cols], TA[0:D, cols], X22[0:D, cols], ALU.subtract).then_inc(S["z_parts"], 1)

            softmax(0)
            for b in range(1, B):
                softmax(b)
                if b % 2:
                    dve.wait_ge(S["h3"], b + 1)
                    g = b // 2
                    t = slice(4 * g, 4 * g + 4)
                    stats(H, "z4", g)
                    centre(H, Z, "z4", g)
                    if g == PAIRS - 1:
                        feature_sums(1)
                    dve.wait_ge(S["rstd"], RSQ["z4"] + g + 1)
                    dve.wait_ge(S["ctr"], CTR["z4"] + g + 1)
                    for half in range(2):
                        V_.tensor_tensor(XR[:, t, half, :], Z[:, t, :], bc(rstd[:, t], D), ALU.mult)
                    scaled(Z, "z4", g).then_inc(S["z4"], 1)
            feature_sums(2)
            link(feature_sums(3))
            V_.tensor_scalar(ms[0:D, :], ms[0:D, :], 1.0 / N, None, ALU.mult).then_inc(S["msum"], 1)

            dve.wait_ge(S["rl_mm"], 1)
            link(V_.tensor_reduce(rs[:, 0:1], bank(4, B, NE), axis=X, op=ALU.max))
            V_.tensor_scalar(rt[:, 0, :], bank(4, B, NE), rs[:, 0:1], None, ALU.subtract).then_inc(S["rl_max"], 1)
            parts(1)
            dve.wait_ge(S["rl_exp"], 1)
            link(V_.reciprocal(rs[:, 1:2], rs[:, 1:2]))
            V_.tensor_scalar(rt[:, 2, :], rt[:, 1, :], rs[:, 1:2], None, ALU.mult).then_inc(S["wd"], 1)
            dve.wait_ge(S["ld_mm"], 1)
            link(V_.tensor_scalar(rt[:, 5, :], bank(5, B, NE), float(N), None, ALU.mult))
            link(V_.reciprocal(rt[:, 5, :], rt[:, 5, :]))
            link(V_.tensor_scalar(rt[:, 5, :], rt[:, 5, :], CAP, 1.0, ALU.mult, ALU.min))
            link(V_.tensor_tensor(rt[:, 2, :], rt[:, 2, :], rt[:, 5, :], ALU.mult))
            link(V_.tensor_reduce(rs[:, 2:3], rt[:, 2, :], axis=X, op=ALU.max))
            V_.tensor_scalar(rt[:, 3, :], rt[:, 2, :], rs[:, 2:3], None, ALU.subtract).then_inc(S["r2max"], 1)
            parts(2)
            dve.wait_ge(S["r2exp"], 1)
            link(V_.reciprocal(rs[:, 3:4], rs[:, 3:4]))
            link(V_.tensor_scalar(rt[:, 7, :], rt[:, 4, :], rs[:, 3:4], None, ALU.mult))

            def first_max8(src, dst, s):
                link(V_.tensor_reduce(s, src, axis=X, op=ALU.max))
                link(V_.tensor_scalar(dst, src, s, None, ALU.is_equal))
                link(V_.tensor_tensor(dst, dst, c("rank")[0:B], ALU.mult))
                link(V_.tensor_reduce(rs[:, 4:5], dst, axis=X, op=ALU.max))
                link(V_.tensor_scalar(dst, dst, rs[:, 4:5], None, ALU.is_equal))

            link(V_.tensor_reduce(rs[:, 7:8], rt[:, 7, :], axis=X, op=ALU.max))
            V_.tensor_scalar(rt[:, 13, :], rt[:, 7, :], rs[:, 7:8], None, ALU.subtract).then_inc(S["p_less"], 1)
            parts(3)
            first_max8(rt[:, 7, :], rt[:, 8, :], rs[:, 5:6])
            link(V_.scalar_tensor_tensor(rt[:, 9, :], rt[:, 8, :], -2.0, rt[:, 7, :], ALU.mult, ALU.add))
            first_max8(rt[:, 9, :], rt[:, 10, :], rs[:, 6:7])
            link(V_.tensor_tensor(rt[:, 11, :], rt[:, 8, :], rt[:, 10, :], ALU.add))
            dve.wait_ge(S["e2exp"], 1)
            link(V_.tensor_tensor(rt[:, 11, :], rt[:, 11, :], rt[:, 13, :], ALU.mult))
            link(V_.tensor_reduce(rs[:, 12:13], rt[:, 11, :], axis=X, op=ALU.add))
            link(V_.reciprocal(rs[:, 12:13], rs[:, 12:13]))
            V_.tensor_scalar(rt[:, 12, :], rt[:, 11, :], rs[:, 12:13], None, ALU.mult).then_inc(S["wd"], 1)
            dve.wait_ge(S["wd"], 2)
            eye = ident[0:B, 0:B]
            V_.tensor_tensor(dgw[:, 0:B * NE].rearrange("p (b e) -> p b e", b=B),
                             rt[:, 12, :].unsqueeze(1).to_broadcast([B, B, NE]), bc(eye, NE), ALU.mult).then_inc(S["dg"], 1)
            V_.tensor_tensor(H[:, :, :], H[:, :, :], c("beta")[0:P].unsqueeze(1).to_broadcast([P, NT, D]),
                             ALU.add).then_inc(S["hb"], 1)
            dve.wait_ge(S["wB_mm"], 1)
            link(V_.tensor_copy(wBC[:, :, :], bank(7, 128, B, NE)))

            def scale_weights(b):
                V_.tensor_tensor(W2S[:, b, :, :], c("e2").rearrange("p (e d) -> p e d", e=NE),
                                 bc(wBC[:, b, :], D), ALU.mult).then_inc(S["w2s"], 1)

            scale_weights(0)
            scale_weights(1)
            dve.wait_ge(S["wdT"], 2)
            V_.tensor_tensor(dgw[:, B * NE:].rearrange("p (b e) -> p b e", b=B),
                             b2w[:, :].unsqueeze(1).to_broadcast([B, B, D]), bc(eye, D), ALU.mult).then_inc(S["dg"], 1)
            for b in range(2, B):
                scale_weights(b)
            dve.wait_ge(S["wbc"], 1)
            V_.tensor_tensor(Z[:, :, :].rearrange("p (b h) d -> p b h d", h=2),
                             Z[:, :, :].rearrange("p (b h) d -> p b h d", h=2),
                             bBC.unsqueeze(2).to_broadcast([P, B, 2, D]), ALU.add).then_inc(S["zb"], 1)
            dve.wait_ge(S["zb"], 1)
            dve.wait_ge(S["hb"], 1)

            def with_residual(g):
                dve.wait_ge(S["o_mm"], g + 1)
                V_.tensor_tensor(Y[:, 4 * g:4 * g + 4, :].rearrange("p (i h) d -> p i h d", i=2),
                                 Z[:, 4 * g:4 * g + 4, :].rearrange("p (i h) d -> p i h d", i=2),
                                 bank(6 + g % 2, P, 2, 2, D).rearrange("p h i d -> p i h d"), ALU.add).then_inc(S["fo"], 1)

            def marked(ins):
                count[0] += 1
                ins.then_inc(S["dve"], 1)
                return count[0]

            for g in range(PAIRS + 1):
                old = slice(4 * g - 4, 4 * g)
                if g < PAIRS:
                    with_residual(g)
                if g:
                    n_scaled = marked(scaled(Y, "y", g - 1))
                if g < PAIRS:
                    dve.wait_ge(S["fo"], g + 1)
                    for t in range(4 * g, 4 * g + 4):
                        last = V_.bn_stats(stat[:, t, :], Y[:, t, :])
                    n_stats = marked(last)
                if g:
                    dve.wait_ge(S["dve"], n_scaled)
                    n_gamma = marked(V_.tensor_tensor(Y[:, old, :], Y[:, old, :],
                                                      c("gamma")[0:P].unsqueeze(1).to_broadcast([P, 4, D]), ALU.mult))
                if g < PAIRS:
                    dve.wait_ge(S["dve"], n_stats)
                    for t in range(4 * g, 4 * g + 4):
                        last = V_.bn_aggr(mv[:, t, :], stat[:, t, :])
                    last.then_inc(S["var"], 1)
                if g:
                    dve.wait_ge(S["dve"], n_gamma)
                    V_.tensor_tensor(Y[:, old, :], Y[:, old, :], H[:, old, :], ALU.add).then_inc(S["y_out"], 1)
                if g < PAIRS:
                    centre(Y, Y, "y", g)

        @block.tensor
        def _(pe):
            pe.wait_ge(S["ld_tok"], 48)
            mm(bank(0, D, NPATCH), t3[:, 0:D], t3[:, D:]).then_inc(S["hid_mm"], 1)
            pe.wait_ge(S["ld_w64"], 16)
            mm(bank(1, D, D), w("Wa")[0:D], w("Wb")[0:D])
            mm(bank(2, D + 1, D), w("Wu")[0:D], w("WrT")[0:D])
            mm(bank(3, D, D), w("Wb")[0:D], w("Wa")[0:D]).then_inc(S["gmm"], 1)
            for k in range(KC):
                if k == 0:
                    pe.wait_ge(S["ld_x0"], 16 * (KC // 2))
                if k == KC // 2:
                    pe.wait_ge(S["ld_x1"], 16 * (KC - KC // 2))
                mm(bank(4, D, B * NPATCH), wpT[:, k, :], xP[:, k, :], start=(k == 0), stop=False)
            pe.wait_ge(S["hid"], 1)
            pe.wait_ge(S["filled"], FILLS)
            mm(bank(4, D, B, NPATCH), t66[:, :], hid[:, :].unsqueeze(1).to_broadcast([D + 2, B, NPATCH]),
               start=False, stop=True).then_inc(S["emb_mm"], 1)
            pe.wait_ge(S["emb"], 1)
            pe.wait_ge(S["ld_c"], 16)
            for b in range(B):
                last = nc.tensor.transpose(bank(5, NPATCH, B, D)[:, b, :], embS[:, b * NPATCH:(b + 1) * NPATCH],
                                           ident[0:D, 0:D])
            last.then_inc(S["embT"], 1)

            def transposes(src, ready, done):
                for g in range(PAIRS):
                    pe.wait_ge(ready, g + 1)
                    for t in range(4):
                        last = nc.tensor.transpose(bank(g, D, 4, P)[:, t, :], src[:, 4 * g + t, :], ident[0:P, 0:P])
                    last.then_inc(done, 1)

            pe.wait_ge(S["gc_ready"], 1)
            transposes(Z, S["z1"], S["zT_mm"])
            for q in range(PAIRS):
                pe.wait_ge(S["zT"], q + 1)
                if q == 1:
                    pe.wait_ge(S["h0"], 1)
                for t in range(4):
                    a = (4 * q + t) * P
                    last = mm(bank(4 + q, P, 4, 2 * D)[:, t, :], TA[:, a:a + P], GC[:, :])
                last.then_inc(S["gv_mm"], 1)
            pe.wait_ge(S["v_sb"], PAIRS)
            for b in range(B):
                for t in (2 * b, 2 * b + 1):
                    last = mm(bank(0, D, B, D)[:, b, :], Z[:, t, :], V[:, t, :], start=(t % 2 == 0), stop=(t % 2 == 1))
            last.then_inc(S["zv_mm"], 1)
            pe.wait_ge(S["zv"], 1)
            mm(bank(1, D, B * D), GT[:, :], ZV[:, :]).then_inc(S["p_mm"], 1)
            pe.wait_ge(S["p_sb"], 1)
            for q in range(2):
                for t in range(8):
                    a = (8 * q + t) * P
                    last = mm(bank(2 + q, P, 8, D)[:, t, :], TA[:, a:a + P], PB[:, (8 * q + t) // 2, :])
                last.then_inc(S["lo_mm"], 1)
            pe.wait_ge(S["lnw_ready"], 1)
            transposes(XN, S["xn"], S["xT_mm"])
            pe.wait_ge(S["xT"], PAIRS)
            pe.wait_ge(S["ld_b"], 64)
            for g in range(PAIRS):
                for t in range(4 * g, 4 * g + 4):
                    last = mm(bank(4, P, NT, NKV * HD)[:, t, :], TB[:, t * P:(t + 1) * P], w("v"))
                if g == PAIRS - 1:
                    last.then_inc(S["v_mm"], 1)
                after(pe, "rope_cs", g - 1)
                for j, name in enumerate(("q", "k", "ks")):
                    last = mm(ps[:, QK[g % 2] + j, 0:CW], w(name), TB[:, g * CW:(g + 1) * CW])
                last.then_inc(S["qk_mm"], 1)

            def scores(g, i):
                if i == 0:
                    pe.wait_ge(S["headq"], g + 1)
                after(pe, "x2", g * 2 + (i - 1))
                for h in range(NH):
                    for t in range(2):
                        a = i * N + t * P
                        mm(ps[0:P, 4 * i + h, t * P:t * P + (t + 1) * P], headq[:, h, a:a + P],
                           TB[:, bass.ds(g * CW + i * N, (t + 1) * P)], stop=False, skip_group_check=True)
                        last = mm(ps[0:P, 4 * i + h, 2 * t * P:(2 * t + 1) * P], idb[0:P, 0:P], mask[:, :],
                                  start=False, skip_group_check=True)
                last.then_inc(S["s_mm"], 1)

            def probs_to_keys(g, i):
                pe.wait_ge(S["pnorm"], g * 2 + (i + 1))
                for h in range(NH):
                    for at in (0, P, 2 * P):
                        last = nc.tensor.transpose(ps[0:P, 4 * i + h, at:at + P], Pex[:, i, h, at:at + P],
                                                   ident[0:P, 0:P])
                last.then_inc(S["pt_mm"], 1)

            def weigh(g, i):
                if i == 0:
                    pe.wait_ge(S["vb"], g + 1)
                pe.wait_ge(S["pt_sb1" if i else "pt_sb0"], g + 1)
                for t in range(2):
                    for h in range(NH):
                        last = mm(ps[32 * h:32 * h + 32, 4 * i, t * P:N], Vb[:, 2 * i + t, h // 2, :],
                                  PT[:, i, h, 2 * P * t:2 * P + P * t], start=(t == 0), stop=(t == 1),
                                  skip_group_check=True)
                last.then_inc(S["y_mm"], 1)
                pe.wait_ge(S["y_sb1" if i else "y_sb0"], g + 1)
                for t in range(2):
                    a = i * N + t * P
                    last = mm(bank(4 * i + 2, P, 2, D)[:, t, :], yT[:, a:a + P], c("wo"))
                last.then_inc(S["pr_mm"], 1)

            pe.wait_ge(S["keys"], PAIRS)
            pe.wait_ge(S["vall"], 1)
            scores(0, 0)
            scores(0, 1)

            def attend(g):
                probs_to_keys(g, 0)
                weigh(g, 0)
                probs_to_keys(g, 1)
                scores(g + 1, 0)
                weigh(g, 1)
                scores(g + 1, 1)

            attend(0)
            with pe.Fori(1, PAIRS - 1) as g:
                attend(g)
            for i in range(2):
                probs_to_keys(PAIRS - 1, i)
                weigh(PAIRS - 1, i)
            for g in range(PAIRS):
                pe.wait_ge(S["xr"], g + 1)
                for t in range(4):
                    last = nc.tensor.transpose(bank(g, 128, 4, P)[:, t, :],
                                               XR[:, 4 * g + t, :, :].rearrange("p a d -> p (a d)"), ident[0:P, 0:P])
                last.then_inc(S["rT_mm"], 1)
            pe.wait_ge(S["rT"], PAIRS)
            for t in range(NT):
                last = mm(bank(4, P, NT, NE)[:, t, :], TA[:, t * P:(t + 1) * P], w("rw"))
            last.then_inc(S["lg_mm"], 1)
            def up(g, m):
                rows = min(128, HALL - 128 * m)
                bk = 3 * (m % 2)
                before = g * MT + max(m - 1, 0)
                for k, freed in ((0, "silu"), (1, "bw")):
                    after(pe, freed, before)
                    cols = slice(k * HALL + 128 * m, k * HALL + 128 * m + rows)
                    for n, (wp, xp) in enumerate(((W12, X11), (W12, X22), (W13, X31))):
                        last = mm(ps[0:rows, bk + k, 0:CW], wp[:, cols], xp[:, bass.ds(g * CW, CW)],
                                  start=(n == 0), stop=(n == 2))
                return last

            def spread_weights(g, m):
                rows = min(128, HALL - 128 * m)
                mm(ps[0:rows, 3 * (m % 2) + 2, 0:CW], sel[:, 128 * m:128 * m + rows],
                   wT[:, bass.ds(g * CW, CW)]).then_inc(S["up_mm"], 1)

            def down(g, m):
                rows = min(128, HALL - 128 * m)
                pe.wait_ge(S["hh"], g * MT + (m + 1))
                if m == 0:
                    after(pe, "ym", g)
                w2 = c("w2").rearrange("p (m d) -> p m d", m=MT)[0:rows, m, :]
                for i in range(2):
                    last = mm(ps[64 * i:64 * i + 64, 6, 0:N], w2, hh[0:rows, m % 2, i * N:(i + 1) * N],
                              start=(m == 0), stop=(m == MT - 1), skip_group_check=True)
                last.then_inc(S["dn_mm"], 1)

            def to_tokens(g):
                pe.wait_ge(S["ym"], g + 1)
                for t in range(2):
                    last = nc.tensor.transpose(bank(7, P, 2, 2 * D)[:, t, :], ym[:, t * P:(t + 1) * P], ident)
                last.then_inc(S["ymT_mm"], 1)

            pe.wait_ge(S["lg_max"], 1)
            pe.wait_ge(S["x_parts"], PAIRS)
            pe.wait_ge(S["w_parts"], 1)
            for m in range(MT):
                if m == EARLY:
                    pe.wait_ge(S["wp3"], 1)
                    pe.wait_ge(S["ld_b"], 64)
                    for t in range(NT):
                        dst = ps[0:3 * NE, 5 + t // 8, :].bitcast(BF16)[:, (t % 8) * P:(t % 8 + 1) * P]
                        last = nc.tensor.transpose(dst, wp3[:, t, :, :].rearrange("p a e -> p (a e)"), idb[0:P, 0:P])
                    last.then_inc(S["wT_mm"], 1)
                up(0, m).then_inc(S["up0_mm"], 1)
            pe.wait_ge(S["wT"], 1)
            for m in range(MT):
                if m >= 2:
                    down(0, m - 2)
                spread_weights(0, m)

            def mixture(g):
                down(g - 1, MT - 2)
                for m in range(MT):
                    up(g, m)
                    if m == 0:
                        down(g - 1, MT - 1)
                    if m >= 2:
                        down(g, m - 2)
                    spread_weights(g, m)
                    if m == 4:
                        to_tokens(g - 1)

            with pe.Fori(1, PAIRS) as g:
                mixture(g)
            down(PAIRS - 1, MT - 2)
            down(PAIRS - 1, MT - 1)
            to_tokens(PAIRS - 1)
            transposes(Z, S["z3"], S["aT_mm"])
            pe.wait_ge(S["aT"], 1)
            mm(bank(0, 3 * U, CW), w("wx"), TB[:, 0:CW]).then_inc(S["k_mm"], 1)
            pe.wait_ge(S["aT"], PAIRS)
            for t in range(NT):
                last = mm(bank(4, P, NT, U)[:, t, :], TB[:, t * P:(t + 1) * P], w("wt"))
            last.then_inc(S["q_mm"], 1)
            for g in range(1, PAIRS):
                mm(bank(g, 3 * U, CW), w("wx"), TB[:, g * CW:(g + 1) * CW]).then_inc(S["k_mm"], 1)
            pe.wait_ge(S["ld_hot"], 16)
            pe.wait_ge(S["rep_ready"], 1)
            pe.wait_ge(S["kb"], PAIRS)
            was = c("was").rearrange("p (r u) -> p r u", r=RND)

            def build(b, r):
                after(pe, "tanh", b * RND + (r - 1))
                for j in range(3):
                    last = mm(ps[:, 3 * (r % 2) + j, 0:CW],
                              LQ[:, bass.ds(b, 1), RND * j + r, :].rearrange("p o q -> p (o q)"),
                              RH[:, bass.ds(b, 1), :, :].rearrange("p o s n -> p (o s n)"))
                last.then_inc(S["bld_mm"], 1)

            def contract(b, r):
                pe.wait_ge(S["tanh"], b * RND + (r + 2))
                if r == 0:
                    after(pe, "al_sb", b)
                for k, n in ((0, 0), (0, 1), (0, 2), (0, 3), (0, 4), (0, 5), (1, 2), (1, 3), (1, 0), (1, 1), (1, 4), (1, 5)):
                    quadrant = (n + 2 * k) % 4 if n > 3 else n
                    j, half = n % 3, n // 3
                    last = mm(ps[32 * quadrant:32 * quadrant + 32, 6, N * (n // 4):N * (n // 4) + N], was[:, r + k, :],
                              TH[:, (r + k) % 4, j, half * N:(half + 1) * N], start=(r + k == 0 and n < 4),
                              stop=(r + k >= RND - 2), skip_group_check=True)
                last.then_inc(S["al_mm"], 1)

            def keys_first(b):
                pe.wait_ge(S["pn"], b + 1)
                for t in range(2):
                    for k in range(2):
                        last = nc.tensor.transpose(bank(7, P, 2, 256)[:, t, 128 * k:128 * k + 128],
                                                   AL[:, k, t * P:(t + 1) * P], ident)
                last.then_inc(S["pt2_mm"], 1)

            def values(b):
                pe.wait_ge(S["pt2"], b + 1)
                for q in range(2):
                    for t in range(2):
                        last = mm(bank(7, P, 2, D)[:, q, :], PT2[:, t, q * P:(q + 1) * P],
                                  Z[:, bass.ds(b * 2 + t, 1), :].rearrange("p o d -> p (o d)"),
                                  start=(t == 0), stop=(t == 1))
                last.then_inc(S["c_mm"], 1)

            def image(b):
                later = b > 0
                if b % 2 == 0:
                    pe.wait_ge(S["kp"], b // 2 + 1)
                if b == 0:
                    pe.wait_ge(S["ld_q0"], 32)
                if b == 1:
                    pe.wait_ge(S["ld_q"], 32 * (B - 1))
                for r in range(0, RND, 2):
                    build(b, r)
                    build(b, r + 1)
                    if later and r == RND - 2:
                        keys_first(b - 1)
                    if r:
                        contract(b, r - 2)
                    elif later:
                        contract(b - 1, RND - 2)
                    if later and r == RND - 2:
                        values(b - 1)

            for b in range(B):
                image(b)
            contract(B - 1, RND - 2)
            def last_transposes(g):
                pe.wait_ge(S["z4"], g + 1)
                for t in range(4):
                    last = nc.tensor.transpose(bank(FT[g], 128, 4, P)[:, t, :],
                                               XR[:, 4 * g + t, :, :].rearrange("p a d -> p (a d)"), ident[0:P, 0:P])
                last.then_inc(S["fT_mm"], 1)

            for g in range(PAIRS - 1):
                last_transposes(g)
            keys_first(B - 1)
            values(B - 1)
            def hidden(g, experts=range(NE)):
                pe.wait_ge(S["z_parts"], g + 1)
                for e in experts:
                    after(pe, "gelu", g * NE + (e - 3))
                    cols = slice(2 * HALL + e * FE, 2 * HALL + (e + 1) * FE)
                    for n, (wp, xp) in enumerate(((W12, X11), (W12, X22), (W13, X31))):
                        last = mm(ps[:, e % 4, 0:CW], wp[:, cols], xp[:, g * CW:(g + 1) * CW], start=(n == 0), stop=(n == 2))
                    last.then_inc(S["e1_mm"], 1)

            pe.wait_ge(S["fT"], PAIRS - 1)
            hidden(0, range(4))
            last_transposes(PAIRS - 1)
            pe.wait_ge(S["ld_row"], 16)
            pe.wait_ge(S["msum"], 1)
            mm(bank(4, B, NE), ms[:, :], w("wr")).then_inc(S["rl_mm"], 1)
            hidden(0, range(4, 6))
            pe.wait_ge(S["wd"], 1)
            mm(bank(5, B, NE), ones[0:B, 0:B], rt[:, 2, :]).then_inc(S["ld_mm"], 1)
            hidden(0, range(6, NE))
            hidden(1)
            pe.wait_ge(S["wd"], 2)
            nc.tensor.transpose(bank(5, NE, B), rt[:, 12, :], ident[0:B, 0:B]).then_inc(S["wdT_mm"], 1)
            hidden(2, range(2))
            pe.wait_ge(S["dg"], 1)
            mm(bank(7, 128, B * NE), ones[0:B, :], dgw[:, 0:B * NE]).then_inc(S["wB_mm"], 1)
            pe.wait_ge(S["wdT"], 1)
            pe.wait_ge(S["ld_b2"], 16)
            mm(bank(6, B, D), wdT[:, :], b2s[:, :]).then_inc(S["b2w_mm"], 1)
            hidden(2, range(2, 5))
            pe.wait_ge(S["dg"], 2)
            mm(bank(6, P, B * D), ones[0:B, 0:P], dgw[:, B * NE:]).then_inc(S["bB_mm"], 1)
            hidden(2, range(5, NE))

            def mix(g, experts):
                if experts[0] == 0:
                    after(pe, "oT", g - 1)
                    pe.wait_ge(S["gelu"], (g + 1) * NE)
                    pe.wait_ge(S["w2s"], g * 2 + 2)
                for e in experts:
                    for i in range(2):
                        last = mm(ps[64 * i:64 * i + 64, 4 + g % 2, 0:N], W2S[:, 2 * g + i, e, :],
                                  G1[:, g, e, i * N:(i + 1) * N],
                                  start=(e == 0), stop=(e == NE - 1), skip_group_check=True)
                if experts[-1] == NE - 1:
                    last.then_inc(S["e2_mm"], 1)

            def mixed_to_tokens(g):
                pe.wait_ge(S["oT"], g + 1)
                after(pe, "fo", g - 1)
                for t in range(2):
                    last = nc.tensor.transpose(bank(6 + g % 2, P, 2, 2 * D)[:, t, :], oT[:, g % 2, t * P:(t + 1) * P],
                                               ident)
                last.then_inc(S["o_mm"], 1)

            mix(0, range(NE))
            hidden(3, range(4))
            mix(1, range(NE // 2))
            pe.wait_ge(S["wbc"], 1)
            mixed_to_tokens(0)
            mix(1, range(NE // 2, NE))
            hidden(3, range(4, NE))
            mix(2, range(NE // 2))
            mixed_to_tokens(1)
            mix(2, range(NE // 2, NE))
            mix(3, range(NE // 2))
            mixed_to_tokens(2)
            mix(3, range(NE // 2, NE))
            mixed_to_tokens(3)


_ARGS = ("patches", "wpatch", "txt", "w64", "wrrow", "tok66", "tok3", "c128", "b2", "idb", "sel", "rep", "mask", "hot")


def _layout(x, txt, L0_tok_Wp, L0_tok_bp, L0_tok_W1, L0_tok_b1, L0_tok_W2, L0_tok_b2, L0_attn_W_alpha,
            L0_attn_W_beta, L0_attn_W_unary, L0_attn_b_unary, L0_attn_W_r, L0_ffn_ln1_w, L0_ffn_ln2_w, L0_ffn_wq,
            L0_ffn_wk, L0_ffn_wv, L0_ffn_wo, L0_ffn_router_w, L0_ffn_w1, L0_ffn_w2, L0_ffn_w3, L1_attn_Wt,
            L1_attn_Wx, L1_attn_bh, L1_attn_Wa, L1_attn_ba, L1_ffn_Wr, L1_ffn_br, L1_ffn_W1, L1_ffn_b1,
            L1_ffn_W2, L1_ffn_b2, L1_ffn_gamma, L1_ffn_beta):
    f = np.float32
    a = np.asarray

    def zeros(*s):
        return np.zeros(s, f)

    xp = a(x).reshape(B, CH, NPS, PS, NPS, PS).transpose(1, 3, 5, 0, 2, 4).reshape(KC, 128, B * NPATCH)
    d = {"patches": xp.transpose(1, 0, 2), "wpatch": a(L0_tok_Wp).reshape(KC, 128, D).transpose(1, 0, 2),
         "txt": a(txt)}
    wq, wk = a(L0_ffn_wq), a(L0_ffn_wk)

    def heads(wt, per, halves):
        o = zeros(D, 128)
        for h in range(NH):
            rows = wt[(h // per) * HD:(h // per + 1) * HD]
            for n, swap in enumerate(halves):
                at = 32 * h + n * HD
                o[:, at:at + HD] = (np.concatenate([rows[HD // 2:], rows[:HD // 2]]) if swap else rows).T
        return o

    cols = {"Wa": a(L0_attn_W_alpha), "Wb": a(L0_attn_W_beta),
            "Wu": np.concatenate([a(L0_attn_W_unary), a(L0_attn_b_unary)[:, None]], 1), "WrT": a(L0_attn_W_r).T,
            "ln1": a(L0_ffn_ln1_w)[:, None], "ln2": a(L0_ffn_ln2_w)[:, None],
            "q": heads(wq, 1, (0, 1)), "k": heads(wk, NH // NKV, (0, 0)), "ks": heads(wk, NH // NKV, (1, 1)), "v": a(L0_ffn_wv).T, "rw": a(L0_ffn_router_w).T,
            "w1": a(L0_ffn_w1).reshape(HALL, D).T, "w3": a(L0_ffn_w3).reshape(HALL, D).T,
            "wt": a(L1_attn_Wt), "wx": np.concatenate([a(L1_attn_Wx).T] * 3, 1),
            "e1": a(L1_ffn_W1).transpose(1, 0, 2).reshape(D, NE * FE), "wr": a(L1_ffn_Wr)}
    d["w64"] = np.concatenate([cols[n] for n in W64], 1)
    d["wrrow"] = a(L1_ffn_br).reshape(1, NE)
    d["tok66"] = np.concatenate([a(L0_tok_W2), a(L0_tok_b2)[None], a(L0_tok_bp)[None]])
    gx, gy = np.meshgrid(np.arange(NPS), np.arange(NPS), indexing="ij")
    xy = np.stack([gx.ravel(), gy.ravel(), np.full(NPATCH, NPS - 1)]).astype(f) / f(NPS - 1)
    d["tok3"] = np.concatenate([np.concatenate([a(L0_tok_W1), a(L0_tok_b1)[None]]), xy], 1)
    inv = 1.0 / 10000.0 ** (np.arange(0, HD, 2, dtype=f) / HD)
    ang = np.outer(np.concatenate([inv, inv]).astype(f), np.arange(N, dtype=f)).astype(f)
    half = 2 * NH
    cos = np.tile(np.cos(ang), (half, 1))
    sin = np.tile(np.sin(ang) * np.where(np.arange(HD) < HD // 2, -1, 1)[:, None], (half, 1))
    first = (np.arange(128) % 32 < HD)[:, None]
    i = np.arange(P)
    d["mask"] = np.where(i[None] > i[:, None], NEG, 0).astype(f)
    wo = zeros(128, D)
    for h in range(NH):
        wo[32 * h:32 * h + HD] = a(L0_ffn_wo).T[HD * h:HD * (h + 1)]
    w2 = zeros(MPAD, D)
    w2[:HALL] = a(L0_ffn_w2).transpose(0, 2, 1).reshape(HALL, D)
    was = zeros(IB, U, RND, IB * RND)
    for r in range(RND):
        for q in range(IB):
            was[q, :, r, IB * r + q] = a(L1_attn_Wa)[:, 0]
    cc = {"ident": np.eye(128, dtype=f), "qtab": np.where(first, cos, sin), "cos": cos, "sin": sin,
          "head": np.arange(128)[:, None] // 32 == np.arange(NH)[None],
          "rank": np.broadcast_to(np.arange(NE, 0, -1).astype(f), (128, NE)), "wo": wo,
          "w2": w2.reshape(MT, 128, D).transpose(1, 0, 2).reshape(128, MT * D), "was": was.reshape(128, RND * U),
          "ba": np.broadcast_to(a(L1_attn_ba), (128, 1)), "bh": np.concatenate([a(L1_attn_bh)] * 4)[:, None],
          "b1": a(L1_ffn_b1).T, "gamma": np.broadcast_to(a(L1_ffn_gamma), (128, D)), "beta": np.broadcast_to(a(L1_ffn_beta), (128, D)),
          "e2": a(L1_ffn_W2).transpose(1, 0, 2).reshape(FE, NE * D)}
    d["c128"] = np.concatenate([cc[n] for n in C128], 1).astype(f)
    d["b2"] = a(L1_ffn_b2)
    d["idb"] = np.eye(128).astype(f)
    owner = np.full(MPAD, -1)
    owner[:HALL] = np.arange(HALL) // HID
    d["sel"] = np.concatenate([owner[None] == np.arange(NE)[:, None]] * 3).astype(f)
    d["rep"] = np.concatenate([np.concatenate([np.eye(U)] * IB, 1)] * 3).astype(f)
    hot = np.zeros((2, 3, B, 2, N), f)
    hot[0, :, :, 0], hot[1, :, :, 1] = 1, 1
    d["hot"] = hot.reshape(6, B, 2, N)
    return {k: np.ascontiguousarray(v) for k, v in d.items()}


def kernel(**inputs):
    import concourse.bacc as _bacc
    from concourse.bass_utils import run_bass_kernel_spmd as _run

    nc = _bacc.Bacc("TRN2", target_bir_lowering=False, num_devices=1)
    d = _layout(**inputs)
    arrays, args = {}, []
    for name in _ARGS:
        arrays[f"in_{name}_dram"] = d[name]
        args.append(nc.dram_tensor(f"in_{name}_dram", d[name].shape, mybir.dt.from_np(d[name].dtype),
                                   kind="ExternalInput").ap())
    args.append(nc.dram_tensor("out_dram", (B, N, D), F32, kind="ExternalOutput").ap())
    early_fusion(nc, *args)
    r = _run(nc, [arrays], core_ids=[0])
    return r.results[0]["out_dram"]
```
